# Optimizing a Trainium2 kernel written in Bass

```python
import numpy as np
import jax
import jax.numpy as jnp

def _softmax(x, axis=-1):
    return jax.nn.softmax(x, axis=axis)

def _gelu(x):
    return jax.nn.gelu(x, approximate=True)

def _silu(x):
    return jax.nn.silu(x)

def _sigmoid(x):
    return jax.nn.sigmoid(x)

def _layernorm(x, axis=-1, eps=1e-05):
    m = jnp.mean(x, axis=axis, keepdims=True)
    v = jnp.var(x, axis=axis, keepdims=True)
    return (x - m) / jnp.sqrt(v + eps)

def _scatter_add(tgt, idx, src, axis=0):
    return tgt.at[idx].add(src)

def _segment_sum(src, seg, n):
    return jax.ops.segment_sum(src, seg, n)
kernel_name = 'mk_adaln_ffn_d4_seqx_r4_1634b2'

def setup_inputs(seed: int=0):
    np.random.seed(seed)
    _w = jnp.asarray

    def _rec_inputs():
        import jax
        import jax.numpy as jnp
        _rk = jax.random.key(seed)
        x = -0.000125 + 0.9999 * jax.random.normal(jax.random.fold_in(_rk, 1), (2, 1024, 256), jnp.float32)
        _lenS = 1024 - jax.random.randint(jax.random.fold_in(_rk, 7), (2,), 0, max(1, 1024 // 4) + 1, jnp.int32)
        _lenS2 = 1024 - jax.random.randint(jax.random.fold_in(_rk, 8), (2,), 0, max(1, 1024 // 4) + 1, jnp.int32)
        cond_8 = jax.random.uniform(jax.random.fold_in(_rk, 11), (2, 8), jnp.float32, 0.0, 0.983423)
        return (x, cond_8)
    x, cond_8 = _rec_inputs()

    def _L0_cond_setup():
        import jax, jax.numpy as jnp
        import numpy as np
        B, S, D = (16, 512, 256)
        E, H = (8, 512)
        key = jax.random.key(seed)
        ks = jax.random.split(key, 8)
        scale = 0.02
        x = jax.random.normal(ks[0], (B, S, D), dtype=jnp.float32)
        opcode_onehot = jax.random.uniform(ks[1], (B, E), dtype=jnp.float32)
        W_up = jax.random.normal(ks[2], (E, H, D), dtype=jnp.float32) * scale
        b_up = jnp.zeros((E, H), dtype=jnp.float32)
        W_gate = jax.random.normal(ks[3], (E, H, D), dtype=jnp.float32) * scale
        b_gate = jnp.zeros((E, H), dtype=jnp.float32)
        W_down = jax.random.normal(ks[4], (E, D, H), dtype=jnp.float32) * scale
        b_down = jnp.zeros((E, D), dtype=jnp.float32)
        return {'x': x, 'opcode_onehot': opcode_onehot, 'W_up': W_up, 'b_up': b_up, 'W_gate': W_gate, 'b_gate': b_gate, 'W_down': W_down, 'b_down': b_down}
    _L0_cond_all = _L0_cond_setup()
    _L0_cond_in = {k: v for k, v in _L0_cond_all.items() if k in ('W_up', 'b_up', 'W_gate', 'b_gate', 'W_down', 'b_down')}
    del _L0_cond_all

    def _L0_ffn_setup():
        import jax, jax.numpy as jnp
        import numpy as np
        B, T, D = (2, 256, 256)
        H, DK, K = (8, 128, 8)
        NKEYS = 64
        NEXP = NKEYS * NKEYS

        def _rmsnorm(x, w, eps=1e-06):
            inv = jax.lax.rsqrt(jnp.mean(x * x, axis=-1, keepdims=True) + eps)
            return x * inv * w
        key = jax.random.key(seed)
        ks = jax.random.split(key, 5)
        return {'x': jax.random.normal(ks[0], (B, T, D), jnp.float32), 'w_q': jax.random.normal(ks[1], (H * 2 * DK, D), jnp.float32) * 0.02, 'keys': jax.random.normal(ks[2], (H, NKEYS, 2, DK), jnp.float32) * 0.02, 'expert_down': jax.random.normal(ks[3], (NEXP, D), jnp.float32) * 0.02, 'expert_up': jax.random.normal(ks[4], (NEXP, D), jnp.float32) * 0.02, 'norm_w': jnp.ones((D,), jnp.float32)}
    _L0_ffn_all = _L0_ffn_setup()
    _L0_ffn_in = {k: v for k, v in _L0_ffn_all.items() if k in ('w_q', 'keys', 'expert_down', 'expert_up', 'norm_w')}
    del _L0_ffn_all

    def _L1_cond_setup():
        import jax, jax.numpy as jnp
        import numpy as np
        R = 16
        ALPHA = 32.0
        SCALING = ALPHA / R
        key = jax.random.key(seed)
        ks = jax.random.split(key, 6)
        B, T, C, O, E = (16, 375, 256, 256, 8)
        x = jax.random.normal(ks[0], (B, T, C), dtype=jnp.float32)
        w = jax.random.uniform(ks[1], (B, E), dtype=jnp.float32)
        W_base = jax.random.normal(ks[2], (O, C), dtype=jnp.float32) * 0.02
        b_base = jax.random.normal(ks[3], (O,), dtype=jnp.float32) * 0.02
        As = jax.random.normal(ks[4], (E, R, C), dtype=jnp.float32) * 0.02
        Bs = jax.random.normal(ks[5], (E, O, R), dtype=jnp.float32) * 0.02
        return {'x': x, 'w': w, 'W_base': W_base, 'b_base': b_base, 'As': As, 'Bs': Bs}
    _L1_cond_all = _L1_cond_setup()
    _L1_cond_in = {k: v for k, v in _L1_cond_all.items() if k in ('W_base', 'b_base', 'As', 'Bs')}
    del _L1_cond_all

    def _L1_ffn_setup():
        import jax, jax.numpy as jnp
        import numpy as np
        B, S, D = (8, 1024, 256)
        E, R, K = (6, 16, 2)
        key = jax.random.key(seed)
        ks = jax.random.split(key, 9)
        sc = 0.02
        return {'x': jax.random.normal(ks[0], (B, S, D), jnp.float32), 'base_W': jax.random.normal(ks[1], (D, D), jnp.float32) * sc, 'base_b': jax.random.normal(ks[2], (D,), jnp.float32) * sc, 'shared_A': jax.random.normal(ks[3], (R, D), jnp.float32) * sc, 'shared_B': jax.random.normal(ks[4], (D, R), jnp.float32) * sc, 'routed_A': jax.random.normal(ks[5], (E, R, D), jnp.float32) * sc, 'routed_B': jax.random.normal(ks[6], (E, D, R), jnp.float32) * sc, 'router_W': jax.random.normal(ks[7], (E, D), jnp.float32) * sc, 'router_b': jax.random.normal(ks[8], (E,), jnp.float32) * sc}
    _L1_ffn_all = _L1_ffn_setup()
    _L1_ffn_in = {k: v for k, v in _L1_ffn_all.items() if k in ('base_W', 'base_b', 'shared_A', 'shared_B', 'routed_A', 'routed_B', 'router_W', 'router_b')}
    del _L1_ffn_all

    def _L2_cond_setup():
        import jax, jax.numpy as jnp
        import numpy as np
        TOP_K = 2
        NUM_MOE_LAYERS = 12

        def _gemma_mlp(x, gate_w, up_w, down_w):
            g = jnp.einsum('bsh,hi->bsi', x, gate_w)
            u = jnp.einsum('bsh,hi->bsi', x, up_w)
            return jnp.einsum('bsi,ih->bsh', jax.nn.gelu(g, approximate=True) * u, down_w)
        key = jax.random.key(seed)
        ks = jax.random.split(key, 8)
        B, S, H, I, E = (32, 64, 256, 1024, 8)
        std = 0.02
        return {'x': jax.random.normal(ks[0], (B, S, H), jnp.float32), 'router_logits': jax.random.normal(ks[1], (B, E), jnp.float32), 'skill_gate': jax.random.normal(ks[2], (E, H, I), jnp.float32) * std, 'skill_up': jax.random.normal(ks[3], (E, H, I), jnp.float32) * std, 'skill_down': jax.random.normal(ks[4], (E, I, H), jnp.float32) * std, 'shared_gate': jax.random.normal(ks[5], (H, I), jnp.float32) * std, 'shared_up': jax.random.normal(ks[6], (H, I), jnp.float32) * std, 'shared_down': jax.random.normal(ks[7], (I, H), jnp.float32) * std}
    _L2_cond_all = _L2_cond_setup()
    _L2_cond_in = {k: v for k, v in _L2_cond_all.items() if k in ('skill_gate', 'skill_up', 'skill_down', 'shared_gate', 'shared_up', 'shared_down')}
    del _L2_cond_all

    def _L2_ffn_setup():
        import jax, jax.numpy as jnp
        import numpy as np
        BLOCK = 32
        W_BITS = 4
        ACT_BITS = 16

        def act_qdq(x):
            qmax = 2.0 ** (ACT_BITS - 1) - 1.0
            scale = jnp.maximum(jnp.max(jnp.abs(x)) / qmax, 1e-12)
            return jnp.clip(jnp.round(x / scale), -qmax - 1.0, qmax) * scale

        def fixed_qdq_u16(x):
            scale = 1.0 / 65536.0
            return jnp.clip(jnp.round(x / scale), 0.0, 65535.0) * scale

        def lpbq_dequant(w):
            O, I = w.shape
            qmax = 2.0 ** (W_BITS - 1) - 1.0
            wb = w.reshape(O, I // BLOCK, BLOCK)
            s = jnp.maximum(jnp.max(jnp.abs(wb), axis=-1, keepdims=True) / qmax, 1e-12)
            wq = jnp.clip(jnp.round(wb / s), -qmax - 1.0, qmax) * s
            return wq.reshape(O, I)
        key = jax.random.key(seed)
        k1, k2, k3, k4 = jax.random.split(key, 4)
        B, S, H, I = (2, 1024, 256, 768)
        x = jax.random.normal(k1, (B, S, H), jnp.float32)
        w_gate = jax.random.normal(k2, (I, H), jnp.float32) * 0.02
        w_up = jax.random.normal(k3, (I, H), jnp.float32) * 0.02
        w_down = jax.random.normal(k4, (H, I), jnp.float32) * 0.02
        return {'x': x, 'w_gate': w_gate, 'w_up': w_up, 'w_down': w_down}
    _L2_ffn_all = _L2_ffn_setup()
    _L2_ffn_in = {k: v for k, v in _L2_ffn_all.items() if k in ('w_gate', 'w_up', 'w_down')}
    del _L2_ffn_all

    def _L3_cond_setup():
        import jax, jax.numpy as jnp
        import numpy as np
        key = jax.random.key(seed)
        k1, k2, k3, k4, k5 = jax.random.split(key, 5)
        B, N, T, O, G = (32, 64, 256, 256, 8)
        x = jax.random.normal(k1, (B, N, T), dtype=jnp.float32)
        y = jax.random.uniform(k2, (B, G), dtype=jnp.float32)
        weight = jax.random.normal(k3, (G, O, T), dtype=jnp.float32) * (1.0 / np.sqrt(T))
        mask = jax.random.uniform(k4, (O, T), dtype=jnp.float32)
        bias = jax.random.normal(k5, (O,), dtype=jnp.float32)
        return {'x': x, 'y': y, 'weight': weight, 'mask': mask, 'bias': bias}
    _L3_cond_all = _L3_cond_setup()
    _L3_cond_in = {k: v for k, v in _L3_cond_all.items() if k in ('weight', 'mask', 'bias')}
    del _L3_cond_all

    def _L3_ffn_setup():
        import jax, jax.numpy as jnp
        import numpy as np
        D = 256
        H = 4
        HD = D // H
        E = 8
        FF = 1024
        CAP_FACTOR = 1.0

        def _ln(x, g, b, eps=1e-05):
            mu = jnp.mean(x, -1, keepdims=True)
            v = jnp.mean((x - mu) ** 2, -1, keepdims=True)
            return (x - mu) * jax.lax.rsqrt(v + eps) * g + b

        def _mha(x, w, b, ow, ob):
            L, N, _ = x.shape
            qkv = x @ w.T + b
            q, k, v = jnp.split(qkv, 3, axis=-1)
            rh = lambda t: t.reshape(L, N, H, HD).transpose(1, 2, 0, 3)
            q, k, v = (rh(q), rh(k), rh(v))
            scores = jnp.einsum('nhld,nhmd->nhlm', q, k) / np.float32(np.sqrt(HD))
            attn = jax.nn.softmax(scores, axis=-1)
            o = jnp.einsum('nhlm,nhmd->nhld', attn, v).transpose(2, 0, 1, 3).reshape(L, N, D)
            return o @ ow.T + ob

        def _moe(x, wg, w1, b1, w2, b2):
            L, N, _ = x.shape
            S = L * N
            cap = int(CAP_FACTOR * S) // E
            xf = x.reshape(S, D)
            gates = jax.nn.softmax(xf @ wg, axis=-1)
            idx = jnp.argmax(gates, axis=-1)
            mask1 = jax.nn.one_hot(idx, E, dtype=x.dtype)
            loc = jnp.sum((jnp.cumsum(mask1, 0) - 1.0) * mask1, -1).astype(jnp.int32)
            keep = loc < cap
            gate_val = jnp.take_along_axis(gates, idx[:, None], -1)[:, 0]
            slot = jnp.where(keep, idx.astype(jnp.int32) * cap + loc, E * cap)
            disp = jnp.zeros((E * cap, D), x.dtype).at[slot].set(xf, mode='drop')
            disp = disp.reshape(E, cap, D)
            h = jnp.einsum('ecd,edf->ecf', disp, w1) + b1[:, None, :]
            y = (jnp.einsum('ecf,efd->ecd', h, w2) + b2[:, None, :]).reshape(E * cap, D)
            out = jnp.where(keep[:, None], gate_val[:, None] * y[jnp.minimum(slot, E * cap - 1)], 0.0)
            return out.reshape(L, N, D)
        key = jax.random.key(seed)
        ks = jax.random.split(key, 8)
        L, N = (256, 16)
        s = 0.02
        return {'x': jax.random.normal(ks[0], (L, N, D), jnp.float32), 'in_proj_w': jax.random.normal(ks[1], (3 * D, D), jnp.float32) * s, 'in_proj_b': jnp.zeros((3 * D,), jnp.float32), 'out_proj_w': jax.random.normal(ks[2], (D, D), jnp.float32) * s, 'out_proj_b': jnp.zeros((D,), jnp.float32), 'ln1_g': jnp.ones((D,), jnp.float32), 'ln1_b': jnp.zeros((D,), jnp.float32), 'ln2_g': jnp.ones((D,), jnp.float32), 'ln2_b': jnp.zeros((D,), jnp.float32), 'wg': jax.random.normal(ks[3], (D, E), jnp.float32) * s, 'w1': jax.random.normal(ks[4], (E, D, FF), jnp.float32) * s, 'b1': jnp.zeros((E, FF), jnp.float32), 'w2': jax.random.normal(ks[5], (E, FF, D), jnp.float32) * s, 'b2': jnp.zeros((E, D), jnp.float32)}
    _L3_ffn_all = _L3_ffn_setup()
    _L3_ffn_in = {k: v for k, v in _L3_ffn_all.items() if k in ('in_proj_w', 'in_proj_b', 'out_proj_w', 'out_proj_b', 'ln1_g', 'ln1_b', 'ln2_g', 'ln2_b', 'wg', 'w1', 'b1', 'w2', 'b2')}
    del _L3_ffn_all
    return {'x': x, 'cond_8': cond_8, 'L0_cond_W_up': _L0_cond_in['W_up'], 'L0_cond_b_up': _L0_cond_in['b_up'], 'L0_cond_W_gate': _L0_cond_in['W_gate'], 'L0_cond_b_gate': _L0_cond_in['b_gate'], 'L0_cond_W_down': _L0_cond_in['W_down'], 'L0_cond_b_down': _L0_cond_in['b_down'], 'L0_ffn_w_q': _L0_ffn_in['w_q'], 'L0_ffn_keys': _L0_ffn_in['keys'], 'L0_ffn_expert_down': _L0_ffn_in['expert_down'], 'L0_ffn_expert_up': _L0_ffn_in['expert_up'], 'L0_ffn_norm_w': _L0_ffn_in['norm_w'], 'L1_cond_W_base': _L1_cond_in['W_base'], 'L1_cond_b_base': _L1_cond_in['b_base'], 'L1_cond_As': _L1_cond_in['As'], 'L1_cond_Bs': _L1_cond_in['Bs'], 'L1_ffn_base_W': _L1_ffn_in['base_W'], 'L1_ffn_base_b': _L1_ffn_in['base_b'], 'L1_ffn_shared_A': _L1_ffn_in['shared_A'], 'L1_ffn_shared_B': _L1_ffn_in['shared_B'], 'L1_ffn_routed_A': _L1_ffn_in['routed_A'], 'L1_ffn_routed_B': _L1_ffn_in['routed_B'], 'L1_ffn_router_W': _L1_ffn_in['router_W'], 'L1_ffn_router_b': _L1_ffn_in['router_b'], 'L2_cond_skill_gate': _L2_cond_in['skill_gate'], 'L2_cond_skill_up': _L2_cond_in['skill_up'], 'L2_cond_skill_down': _L2_cond_in['skill_down'], 'L2_cond_shared_gate': _L2_cond_in['shared_gate'], 'L2_cond_shared_up': _L2_cond_in['shared_up'], 'L2_cond_shared_down': _L2_cond_in['shared_down'], 'L2_ffn_w_gate': _L2_ffn_in['w_gate'], 'L2_ffn_w_up': _L2_ffn_in['w_up'], 'L2_ffn_w_down': _L2_ffn_in['w_down'], 'L3_cond_weight': _L3_cond_in['weight'], 'L3_cond_mask': _L3_cond_in['mask'], 'L3_cond_bias': _L3_cond_in['bias'], 'L3_ffn_in_proj_w': _L3_ffn_in['in_proj_w'], 'L3_ffn_in_proj_b': _L3_ffn_in['in_proj_b'], 'L3_ffn_out_proj_w': _L3_ffn_in['out_proj_w'], 'L3_ffn_out_proj_b': _L3_ffn_in['out_proj_b'], 'L3_ffn_ln1_g': _L3_ffn_in['ln1_g'], 'L3_ffn_ln1_b': _L3_ffn_in['ln1_b'], 'L3_ffn_ln2_g': _L3_ffn_in['ln2_g'], 'L3_ffn_ln2_b': _L3_ffn_in['ln2_b'], 'L3_ffn_wg': _L3_ffn_in['wg'], 'L3_ffn_w1': _L3_ffn_in['w1'], 'L3_ffn_b1': _L3_ffn_in['b1'], 'L3_ffn_w2': _L3_ffn_in['w2'], 'L3_ffn_b2': _L3_ffn_in['b2']}

def reference(x, cond_8, L0_cond_W_up, L0_cond_b_up, L0_cond_W_gate, L0_cond_b_gate, L0_cond_W_down, L0_cond_b_down, L0_ffn_w_q, L0_ffn_keys, L0_ffn_expert_down, L0_ffn_expert_up, L0_ffn_norm_w, L1_cond_W_base, L1_cond_b_base, L1_cond_As, L1_cond_Bs, L1_ffn_base_W, L1_ffn_base_b, L1_ffn_shared_A, L1_ffn_shared_B, L1_ffn_routed_A, L1_ffn_routed_B, L1_ffn_router_W, L1_ffn_router_b, L2_cond_skill_gate, L2_cond_skill_up, L2_cond_skill_down, L2_cond_shared_gate, L2_cond_shared_up, L2_cond_shared_down, L2_ffn_w_gate, L2_ffn_w_up, L2_ffn_w_down, L3_cond_weight, L3_cond_mask, L3_cond_bias, L3_ffn_in_proj_w, L3_ffn_in_proj_b, L3_ffn_out_proj_w, L3_ffn_out_proj_b, L3_ffn_ln1_g, L3_ffn_ln1_b, L3_ffn_ln2_g, L3_ffn_ln2_b, L3_ffn_wg, L3_ffn_w1, L3_ffn_b1, L3_ffn_w2, L3_ffn_b2):
    import jax
    import jax.numpy as jnp

    def _L0_cond_ref(x, opcode_onehot, W_up, b_up, W_gate, b_gate, W_down, b_down):
        import jax, jax.numpy as jnp
        import numpy as np
        B, S, D = (16, 512, 256)
        E, H = (8, 512)
        expert = jnp.argmax(opcode_onehot, axis=-1)
        wu, bu = (W_up[expert], b_up[expert])
        wg, bg = (W_gate[expert], b_gate[expert])
        wd, bd = (W_down[expert], b_down[expert])
        up = jnp.einsum('bsd,bhd->bsh', x, wu) + bu[:, None, :]
        gate = jnp.einsum('bsd,bhd->bsh', x, wg) + bg[:, None, :]
        hidden = jax.nn.silu(up) * gate
        out = jnp.einsum('bsh,bdh->bsd', hidden, wd) + bd[:, None, :]
        return out

    def _L0_ffn_ref(x, w_q, keys, expert_down, expert_up, norm_w):
        import jax, jax.numpy as jnp
        import numpy as np
        B, T, D = (2, 256, 256)
        H, DK, K = (8, 128, 8)
        NKEYS = 64
        NEXP = NKEYS * NKEYS

        def _rmsnorm(x, w, eps=1e-06):
            inv = jax.lax.rsqrt(jnp.mean(x * x, axis=-1, keepdims=True) + eps)
            return x * inv * w
        b, t, d = x.shape
        xn = _rmsnorm(x, norm_w)
        q = (xn @ w_q.T).reshape(b, t, H, 2, DK)
        sim1 = jnp.einsum('bthd,hkd->bthk', q[..., 0, :], keys[:, :, 0, :])
        sim2 = jnp.einsum('bthd,hkd->bthk', q[..., 1, :], keys[:, :, 1, :])
        s1, i1 = jax.lax.top_k(sim1, K)
        s2, i2 = jax.lax.top_k(sim2, K)
        all_idx = (i1[..., :, None] * NKEYS + i2[..., None, :]).reshape(b, t, H, K * K)
        all_sc = (s1[..., :, None] + s2[..., None, :]).reshape(b, t, H, K * K)
        fs, pk = jax.lax.top_k(all_sc, K)
        fi = jnp.take_along_axis(all_idx, pk, axis=-1)
        wd = expert_down[fi]
        wu = expert_up[fi]
        hidden = jax.nn.gelu(jnp.einsum('btd,bthkd->bthk', xn, wd), approximate=False)
        hidden = hidden * jax.nn.relu(fs)
        return jnp.einsum('bthk,bthkd->btd', hidden, wu)

    def _L1_cond_ref(x, w, W_base, b_base, As, Bs):
        import jax, jax.numpy as jnp
        import numpy as np
        R = 16
        ALPHA = 32.0
        SCALING = ALPHA / R
        out = jnp.einsum('btc,oc->bto', x, W_base) + b_base
        h = jnp.einsum('btc,erc->bter', x, As)
        lora = jnp.einsum('bter,eor,be->bto', h, Bs, w)
        return out + lora * SCALING

    def _L1_ffn_ref(x, base_W, base_b, shared_A, shared_B, routed_A, routed_B, router_W, router_b):
        import jax, jax.numpy as jnp
        import numpy as np
        B, S, D = (8, 1024, 256)
        E, R, K = (6, 16, 2)
        base_out = jax.lax.stop_gradient(jnp.einsum('bsi,oi->bso', x, base_W) + base_b)
        shared_out = jnp.einsum('bsr,or->bso', jnp.einsum('bsi,ri->bsr', x, shared_A), shared_B)
        logits = jnp.einsum('bsi,ei->bse', x, router_W) + router_b
        gate = jax.nn.softmax(logits, axis=-1)
        topk_w, topk_i = jax.lax.top_k(gate, K)
        sparse_w = jnp.sum(jax.nn.one_hot(topk_i, E, dtype=gate.dtype) * topk_w[..., None], axis=-2)
        sparse_w = sparse_w / (jnp.sum(sparse_w, axis=-1, keepdims=True) + 1e-06)
        h = jnp.einsum('bsi,eri->bser', x, routed_A)
        routed_outs = jnp.einsum('bser,eor->bseo', h, routed_B)
        routed_out = jnp.einsum('bseo,bse->bso', routed_outs, sparse_w)
        return base_out + shared_out + routed_out

    def _L2_cond_ref(x, router_logits, skill_gate, skill_up, skill_down, shared_gate, shared_up, shared_down):
        import jax, jax.numpy as jnp
        import numpy as np
        TOP_K = 2
        NUM_MOE_LAYERS = 12

        def _gemma_mlp(x, gate_w, up_w, down_w):
            g = jnp.einsum('bsh,hi->bsi', x, gate_w)
            u = jnp.einsum('bsh,hi->bsi', x, up_w)
            return jnp.einsum('bsi,ih->bsh', jax.nn.gelu(g, approximate=True) * u, down_w)
        B = x.shape[0]
        E = skill_gate.shape[0]
        rw = jax.nn.softmax(router_logits.astype(jnp.float32), axis=-1)
        w, sel = jax.lax.top_k(rw, TOP_K)
        w = w / w.sum(axis=-1, keepdims=True)
        w = w.astype(x.dtype)
        scale = 1.0 / NUM_MOE_LAYERS
        w = scale * w + (1.0 - scale) * jax.lax.stop_gradient(w)
        dense_w = jnp.zeros((B, E), x.dtype).at[jnp.arange(B)[:, None], sel].add(w)

        def step(acc, params):
            g, u, d, we = params
            return (acc + we[:, None, None] * _gemma_mlp(x, g, u, d), None)
        out, _ = jax.lax.scan(step, jnp.zeros_like(x), (skill_gate, skill_up, skill_down, dense_w.T))
        out = out + _gemma_mlp(x, shared_gate, shared_up, shared_down)
        return out

    def _L2_ffn_ref(x, w_gate, w_up, w_down):
        import jax, jax.numpy as jnp
        import numpy as np
        BLOCK = 32
        W_BITS = 4
        ACT_BITS = 16

        def act_qdq(x):
            qmax = 2.0 ** (ACT_BITS - 1) - 1.0
            scale = jnp.maximum(jnp.max(jnp.abs(x)) / qmax, 1e-12)
            return jnp.clip(jnp.round(x / scale), -qmax - 1.0, qmax) * scale

        def fixed_qdq_u16(x):
            scale = 1.0 / 65536.0
            return jnp.clip(jnp.round(x / scale), 0.0, 65535.0) * scale

        def lpbq_dequant(w):
            O, I = w.shape
            qmax = 2.0 ** (W_BITS - 1) - 1.0
            wb = w.reshape(O, I // BLOCK, BLOCK)
            s = jnp.maximum(jnp.max(jnp.abs(wb), axis=-1, keepdims=True) / qmax, 1e-12)
            wq = jnp.clip(jnp.round(wb / s), -qmax - 1.0, qmax) * s
            return wq.reshape(O, I)
        x = act_qdq(x)
        up = act_qdq(x @ lpbq_dequant(w_up).T)
        gate = act_qdq(x @ lpbq_dequant(w_gate).T)
        sig = fixed_qdq_u16(jax.nn.sigmoid(gate))
        gate = act_qdq(gate * sig)
        o = act_qdq(gate * up)
        return o @ lpbq_dequant(w_down).T

    def _L3_cond_ref(x, y, weight, mask, bias):
        import jax, jax.numpy as jnp
        import numpy as np
        masked_w = weight * mask[None, :, :]
        w_bot = jnp.einsum('bg,got->bot', y, masked_w)
        return jnp.einsum('bnt,bot->bno', x, w_bot) + bias

    def _L3_ffn_ref(x, in_proj_w, in_proj_b, out_proj_w, out_proj_b, ln1_g, ln1_b, ln2_g, ln2_b, wg, w1, b1, w2, b2):
        import jax, jax.numpy as jnp
        import numpy as np
        D = 256
        H = 4
        HD = D // H
        E = 8
        FF = 1024
        CAP_FACTOR = 1.0

        def _ln(x, g, b, eps=1e-05):
            mu = jnp.mean(x, -1, keepdims=True)
            v = jnp.mean((x - mu) ** 2, -1, keepdims=True)
            return (x - mu) * jax.lax.rsqrt(v + eps) * g + b

        def _mha(x, w, b, ow, ob):
            L, N, _ = x.shape
            qkv = x @ w.T + b
            q, k, v = jnp.split(qkv, 3, axis=-1)
            rh = lambda t: t.reshape(L, N, H, HD).transpose(1, 2, 0, 3)
            q, k, v = (rh(q), rh(k), rh(v))
            scores = jnp.einsum('nhld,nhmd->nhlm', q, k) / np.float32(np.sqrt(HD))
            attn = jax.nn.softmax(scores, axis=-1)
            o = jnp.einsum('nhlm,nhmd->nhld', attn, v).transpose(2, 0, 1, 3).reshape(L, N, D)
            return o @ ow.T + ob

        def _moe(x, wg, w1, b1, w2, b2):
            L, N, _ = x.shape
            S = L * N
            cap = int(CAP_FACTOR * S) // E
            xf = x.reshape(S, D)
            gates = jax.nn.softmax(xf @ wg, axis=-1)
            idx = jnp.argmax(gates, axis=-1)
            mask1 = jax.nn.one_hot(idx, E, dtype=x.dtype)
            loc = jnp.sum((jnp.cumsum(mask1, 0) - 1.0) * mask1, -1).astype(jnp.int32)
            keep = loc < cap
            gate_val = jnp.take_along_axis(gates, idx[:, None], -1)[:, 0]
            slot = jnp.where(keep, idx.astype(jnp.int32) * cap + loc, E * cap)
            disp = jnp.zeros((E * cap, D), x.dtype).at[slot].set(xf, mode='drop')
            disp = disp.reshape(E, cap, D)
            h = jnp.einsum('ecd,edf->ecf', disp, w1) + b1[:, None, :]
            y = (jnp.einsum('ecf,efd->ecd', h, w2) + b2[:, None, :]).reshape(E * cap, D)
            out = jnp.where(keep[:, None], gate_val[:, None] * y[jnp.minimum(slot, E * cap - 1)], 0.0)
            return out.reshape(L, N, D)
        y1 = _ln(x + _mha(x, in_proj_w, in_proj_b, out_proj_w, out_proj_b), ln1_g, ln1_b)
        y2 = _ln(y1 + _moe(y1, wg, w1, b1, w2, b2), ln2_g, ln2_b)
        return y2
    x = x + _L0_ffn_ref(_L0_cond_ref(x, cond_8, L0_cond_W_up, L0_cond_b_up, L0_cond_W_gate, L0_cond_b_gate, L0_cond_W_down, L0_cond_b_down), L0_ffn_w_q, L0_ffn_keys, L0_ffn_expert_down, L0_ffn_expert_up, L0_ffn_norm_w)
    x = x + _L1_ffn_ref(_L1_cond_ref(x, cond_8, L1_cond_W_base, L1_cond_b_base, L1_cond_As, L1_cond_Bs), L1_ffn_base_W, L1_ffn_base_b, L1_ffn_shared_A, L1_ffn_shared_B, L1_ffn_routed_A, L1_ffn_routed_B, L1_ffn_router_W, L1_ffn_router_b)
    x = x + _L2_ffn_ref(_L2_cond_ref(x, cond_8, L2_cond_skill_gate, L2_cond_skill_up, L2_cond_skill_down, L2_cond_shared_gate, L2_cond_shared_up, L2_cond_shared_down), L2_ffn_w_gate, L2_ffn_w_up, L2_ffn_w_down)
    x = x + _L3_ffn_ref(_L3_cond_ref(x, cond_8, L3_cond_weight, L3_cond_mask, L3_cond_bias), L3_ffn_in_proj_w, L3_ffn_in_proj_b, L3_ffn_out_proj_w, L3_ffn_out_proj_b, L3_ffn_ln1_g, L3_ffn_ln1_b, L3_ffn_ln2_g, L3_ffn_ln2_b, L3_ffn_wg, L3_ffn_w1, L3_ffn_b1, L3_ffn_w2, L3_ffn_b2)
    return x

_drawn_inputs = setup_inputs


def setup_inputs(seed=0):
    import zlib

    import numpy as np

    out = dict(_drawn_inputs(seed))
    spreads = {'L0_cond_b_up': (0.0, 0.1),
     'L0_cond_b_gate': (0.0, 0.1),
     'L0_cond_b_down': (0.0, 0.1),
     'L0_ffn_norm_w': (1.0, 0.2),
     'L3_ffn_in_proj_b': (0.0, 0.1),
     'L3_ffn_out_proj_b': (0.0, 0.1),
     'L3_ffn_ln1_g': (1.0, 0.2),
     'L3_ffn_ln1_b': (0.0, 0.1),
     'L3_ffn_ln2_g': (1.0, 0.2),
     'L3_ffn_ln2_b': (0.0, 0.1),
     'L3_ffn_b1': (0.0, 0.1),
     'L3_ffn_b2': (0.0, 0.1)}
    factors = {}
    for name, (base, spread) in spreads.items():
        noise = np.random.default_rng([zlib.crc32(name.encode()), seed]).standard_normal(out[name].shape)
        drawn = base * np.exp(spread * noise) if base else spread * noise
        out[name] = jnp.asarray(drawn.astype(out[name].dtype))
    for name, factor in factors.items():
        out[name] = (out[name] * factor).astype(out[name].dtype)
    return out
```

```python
from contextlib import ExitStack

import concourse.bass as bass
from concourse import mybir

F32 = mybir.dt.float32
U32 = mybir.dt.uint32
ALU = mybir.AluOpType
ACT = mybir.ActivationFunctionType
AX_X = mybir.AxisListType.X

P = 128
B, S, D = 2, 1024, 256
T = B * S
C = D // P
BLK = 512
NBLK = T // BLK
BPB = S // BLK
E8 = 8

H0 = 512
M0 = H0 // P
HEADS, DK, TOPK, NKEYS = 8, 128, 8, 64
NEXP = NKEYS * NKEYS
NG = 2 * HEADS
SLOTS = HEADS * TOPK
TPB = BLK // P
NJ = NEXP // P
COND0 = 2 * C * H0 + M0 * D
COND0_BIAS = 2 * M0 + C

R1 = 16
E1 = 6
R1ALL = (E1 + 1) * R1
I2 = 1024
M2 = I2 // P
Q2 = 768
MQ = Q2 // P
QB = 32
ROUND = 12582912.0
HD = 64
E3 = 8
FF = 1024
CAP = T // E3


class Steps:

    def __init__(self, sem, base=0):
        self.sem, self.base, self.n = sem, base, 0

    def did(self, instruction):
        instruction.then_inc(self.sem, 1)
        self.n += 1

    def settle(self, engine):
        engine.wait_ge(self.sem, self.base + self.n)


class Stage:

    def __init__(self, nc, name):
        self.nc, self.name, self.ctx = nc, name, ExitStack()

    def __enter__(self):
        self.ctx.__enter__()
        return self

    def __exit__(self, *e):
        return self.ctx.__exit__(*e)

    def sb(self, name, shape, dt=F32):
        return self.ctx.enter_context(self.nc.sbuf_tensor(f"{self.name}_{name}", shape, dt))

    def ps(self, name, shape):
        return self.ctx.enter_context(self.nc.psum_tensor(f"{self.name}_{name}", shape, F32))

    def sem(self, name):
        return self.ctx.enter_context(self.nc.semaphore(f"{self.name}_{name}"))

    def block(self):
        return self.ctx.enter_context(self.nc.Block())


def setup(nc, a, g):
    with Stage(nc, "setup") as st:
        sb, sem = st.sb, st.sem
        cond_row = sb("cond_row", [1, B * E8])
        top = sb("top", [1, B * 8])
        neg_max = sb("neg_max", [1, B])
        shifted = sb("shifted", [1, B * E8])
        ex = sb("ex", [1, B * E8])
        total = sb("total", [1, B])
        prob = sb("prob", [1, B * E8])
        ptop = sb("ptop", [1, B * 8])
        two = sb("two", [1, B])
        wpair = sb("wpair", [1, 2 * B])
        wlarge = sb("wlarge", [1, 2 * B])
        ones_row = sb("ones_row", [1, P])
        ps_pair = st.ps("ps_pair", [P, 2 * B])
        loads = sem("loads")
        ident_step = sem("ident_step")
        consts = sem("consts")
        d = sem("dve_step")
        exp_done = sem("exp_done")
        pair_ready = sem("pair_ready")
        pair_spread = sem("pair_spread")
        block = st.block()

        @block.sync
        def _(sp):
            sp.dma_start(cond_row[:], a["cond"].rearrange("b e -> (b e)").rearrange("(o n) -> o n", o=1)).then_inc(loads, 16)
            sp.dma_start(g.cond_all[:], a["cond"].rearrange("b e -> (b e)").partition_broadcast(P)).then_inc(loads, 16)
            sp.dma_start(g.x[:], a["x"]).then_inc(loads, 16)
            sp.wait_ge(loads, 48)

        @block.gpsimd
        def _(pool):
            pool.memset(g.ident[:], 0.0).then_inc(ident_step, 1)
            pool.wait_ge(ident_step, 1)
            pool.affine_select(out=g.ident[:], in_=g.ident[:], compare_op=ALU.not_equal, fill=1.0, base=0,
                               pattern=[[-1, P]], channel_multiplier=1).then_inc(ident_step, 1)
            for t, v in ((g.mean_w[:], 1.0 / D), (g.eps[:, 0:1], 1e-6), (g.eps[:, 1:2], 1e-5)):
                pool.memset(t, v).then_inc(consts, 1)
            pool.iota(g.iota_a[:], pattern=[[1, P]], base=0, channel_multiplier=0,
                      allow_small_or_imprecise_dtypes=True).then_inc(consts, 1)
            pool.wait_ge(consts, 4)
            for half in range(2):
                pool.iota(g.iota_b[64 * half:64 * half + 64, :], pattern=[[1, 64]], base=-32 * half,
                          channel_multiplier=0, allow_small_or_imprecise_dtypes=True).then_inc(consts, 1)
                pool.wait_ge(consts, 5 + half)

        @block.vector
        def _(dve):
            s = Steps(d)
            s.did(dve.memset(ones_row[:], 1.0))
            dve.wait_ge(loads, 48)
            for b in range(B):
                e = slice(8 * b, 8 * b + 8)
                s.did(dve.max(top[:, e], cond_row[:, e]))
            s.settle(dve)
            for b in range(B):
                e = slice(8 * b, 8 * b + 8)
                s.did(dve.max_index(g.best[:, e], top[:, e], cond_row[:, e]))
                s.did(dve.tensor_scalar(shifted[:, e], cond_row[:, e], top[:, 8 * b:8 * b + 1], None, ALU.subtract))
            assert s.n == 7
            dve.wait_ge(exp_done, B)
            for b in range(B):
                s.did(dve.reciprocal(two[:, b:b + 1], total[:, b:b + 1]))
            s.settle(dve)
            for b in range(B):
                e = slice(8 * b, 8 * b + 8)
                s.did(dve.tensor_scalar(prob[:, e], ex[:, e], two[:, b:b + 1], None, ALU.mult))
            s.settle(dve)
            for b in range(B):
                e = slice(8 * b, 8 * b + 8)
                s.did(dve.max(ptop[:, e], prob[:, e]))
            s.settle(dve)
            for b in range(B):
                e = slice(8 * b, 8 * b + 8)
                s.did(dve.max_index(g.pair_idx[:, e], ptop[:, e], prob[:, e]))
                s.did(dve.tensor_tensor(total[:, b:b + 1], ptop[:, 8 * b:8 * b + 1], ptop[:, 8 * b + 1:8 * b + 2], ALU.add))
            s.settle(dve)
            for b in range(B):
                s.did(dve.reciprocal(two[:, b:b + 1], total[:, b:b + 1]))
            s.settle(dve)
            for b in range(B):
                s.did(dve.tensor_scalar(wpair[:, 2 * b:2 * b + 2], ptop[:, 8 * b:8 * b + 2], two[:, b:b + 1], None, ALU.mult))
            s.settle(dve)
            s.did(dve.tensor_scalar(wlarge[:], wpair[:], 1.0 - 1.0 / 12, None, ALU.mult))
            s.settle(dve)
            dve.scalar_tensor_tensor(out=wpair[:], in0=wpair[:], scalar=1.0 / 12, in1=wlarge[:],
                                     op0=ALU.mult, op1=ALU.add).then_inc(pair_ready, 1)
            dve.wait_ge(pair_spread, 1)
            dve.tensor_copy(g.pair_w[:], ps_pair[:]).then_inc(pair_ready, 1)
            dve.wait_ge(pair_ready, 2)

        @block.scalar
        def _(act):
            act.wait_ge(d, 7)
            for b in range(B):
                e = slice(8 * b, 8 * b + 8)
                act.activation(ex[:, e], shifted[:, e], ACT.Exp, accum_out=total[:, b:b + 1]).then_inc(exp_done, 1)

        @block.tensor
        def _(pe):
            pe.wait_ge(pair_ready, 1)
            pe.matmul(ps_pair[:], ones_row[:], wpair[:], start=True, stop=True).then_inc(pair_spread, 1)


def keys_fold(nc, a, g):
    with Stage(nc, "fold") as st:
        wq = st.sb("wq", [P, NG, D])
        kt = st.sb("kt", [P, NG, NKEYS])
        ps = st.ps("ps", [P, C, NG * NKEYS])
        loads, folded, copied = st.sem("loads"), st.sem("folded"), st.sem("copied")
        block = st.block()

        @block.sync
        def _(sp):
            sp.dma_start(wq[:], a["wq"]).then_inc(loads, 16)
            sp.dma_start(kt[:], a["keys"]).then_inc(loads, 16)

        @block.tensor
        def _(pe):
            pe.wait_ge(loads, 32)
            for c in range(C):
                for q in range(NG):
                    mm = pe.matmul(ps[:, c, q * NKEYS:(q + 1) * NKEYS], wq[:, q, c * P:(c + 1) * P], kt[:, q, :],
                                   start=(q % 8 == 0), stop=True, skip_group_check=True)
                mm.then_inc(folded, 1)

        @block.vector
        def _(dve):
            for c in range(C):
                dve.wait_ge(folded, c + 1)
                dve.tensor_copy(g.key_map[:, c, :], ps[:, c, :]).then_inc(copied, 1)
            dve.wait_ge(copied, C)


def route(nc, a, g):
    with Stage(nc, "route") as st:
        sb, ps, sem = st.sb, st.ps, st.sem
        w = sb("w", [P, COND0 + COND0_BIAS])
        w_up = w[:, 0:C * H0].rearrange("p (c h) -> p c h", c=C)
        w_gate = w[:, C * H0:2 * C * H0].rearrange("p (c h) -> p c h", c=C)
        w_down = w[:, 2 * C * H0:COND0].rearrange("p (k d) -> p k d", k=M0)
        b_up = w[:, COND0:COND0 + M0]
        b_gate = w[:, COND0 + M0:COND0 + 2 * M0]
        b_down = w[:, COND0 + 2 * M0:COND0 + 2 * M0 + C]
        norm_w = sb("norm_w", [P, C])
        su = sb("su", [P, M0, BLK])
        hid = sb("hid", [P, M0, BLK])
        xc = sb("xc", [P, C, BLK])
        sq = sb("sq", [P, C, BLK])
        ms = sb("ms", [P, BLK])
        rms = sb("rms", [P, BLK])
        xn = sb("xn", [P, C, BLK])
        s8 = sb("s8", [P, NG, 8])
        i8 = sb("i8", [P, NG, 8], U32)
        i8f = sb("i8f", [P, NG, 8])
        sums = sb("sums", [P, HEADS, 8, 8])
        f8 = sb("f8", [P, SLOTS])
        p8 = sb("p8", [P, SLOTS], U32)
        rank = sb("rank", [P, 2, SLOTS], U32)
        rankf = sb("rankf", [P, 2, SLOTS])
        oneh = sb("oneh", [P, 2, SLOTS, 8])
        ij = sb("ij", [P, 2, SLOTS])
        ju = sb("ju", [P, SLOTS], U32)
        jb = sb("jb", [P, 2, SLOTS], U32)
        jf = sb("jf", [P, 2, SLOTS])
        codes = sb("codes", [P, 2, 3, SLOTS])
        ps_u = ps("ps_u", [P, BLK])
        ps_g = ps("ps_g", [P, BLK])
        ps_d = ps("ps_d", [P, BLK])
        ps_t = ps("ps_t", [P, BLK])
        ps_s = [ps(f"ps_s{i}", [P, 2, BLK]) for i in range(2)]
        wload, nload = sem("wload"), sem("nload")
        up_ready, gate_ready, su_done, hid_done = sem("up_ready"), sem("gate_ready"), sem("su_done"), sem("hid_done")
        down_ready, xc_done, sq_done = sem("down_ready"), sem("xc_done"), sem("sq_done")
        ms_ready, ms_done, rms_done, xn_done = sem("ms_ready"), sem("ms_done"), sem("rms_done"), sem("xn_done")
        xn_kept, sim_ready, sim_read = sem("xn_kept"), sem("sim_ready"), sem("sim_read")
        codes_done, turned, kept = sem("codes_done"), sem("turned"), sem("kept")
        vstep, seen = sem("vstep"), sem("seen")
        block = st.block()

        @block.sync
        def _(sp):
            sp.dma_start(norm_w[:], a["norm_w"]).then_inc(nload, 16)
            with sp.Fori(0, B) as b:
                e = sp.value_load(g.best[0:1, bass.ds(b * 8, 1)], min_val=0, max_val=E8 - 1)
                sp.wait_ge(xc_done, b * (BPB * C) + 1)
                sp.dma_start(w[:], a["cond0"][bass.ds(e, 1), :, :].rearrange("a p n -> p (a n)")).then_inc(wload, 16)

        @block.tensor
        def _(pe):
            pe.sem_inc(turned, 2)
            pe.sem_inc(down_ready, 1)
            def turn(q, t):
                n = q * TPB + t
                pe.wait_ge(codes_done, n + 1)
                pe.wait_ge(kept, n * 6 + 1)
                flat = codes[:, t % 2, :, :].rearrange("p a k -> p (a k)")
                pe.transpose(ps_t[:, 0:P], flat[:, 0:P], g.ident[:])
                pe.transpose(ps_t[0:SLOTS, P:2 * P], flat[:, P:P + SLOTS], g.ident[:]).then_inc(turned, 1)

            with pe.Fori(0, B) as b:
                pe.wait_ge(wload, b * 16 + 16)
                for k in range(BPB):
                    q = b * BPB + k
                    for m in range(M0):
                        pe.wait_ge(su_done, q * M0 + m + 1)
                        for c in range(C):
                            mm = pe.matmul(ps_u[:], w_up[:, c, m * P:(m + 1) * P], g.x[:, c, bass.ds(q * BLK, BLK)],
                                           start=(c == 0), stop=(c == C - 1))
                        mm.then_inc(up_ready, 1)
                        pe.wait_ge(hid_done, q * M0 + m + 1)
                        for c in range(C):
                            mm = pe.matmul(ps_g[:], w_gate[:, c, m * P:(m + 1) * P], g.x[:, c, bass.ds(q * BLK, BLK)],
                                           start=(c == 0), stop=(c == C - 1))
                        mm.then_inc(gate_ready, 1)
                    pe.wait_ge(hid_done, q * M0 + M0 + 1)
                    pe.wait_ge(ms_done, q + 1)
                    for c in range(C):
                        if c:
                            pe.wait_ge(xc_done, q * C + c + 1)
                        for m in range(M0):
                            mm = pe.matmul(ps_d[:], w_down[:, m, c * P:(c + 1) * P], hid[:, m, :],
                                           start=(m == 0), stop=(m == M0 - 1))
                        mm.then_inc(down_ready, 1)
                    pe.wait_ge(sq_done, q * C + C)
                    for c in range(C):
                        mm = pe.matmul(ps_d[:], g.mean_w[:], sq[:, c, :], start=(c == 0), stop=(c == C - 1))
                    mm.then_inc(ms_ready, 1)
                    pe.wait_ge(xn_done, q * C + C + 1)
                    for t in range(TPB):
                        n = q * TPB + t
                        pe.wait_ge(sim_read, n + 1)
                        for h in range(2):
                            for c in range(C):
                                mm = pe.matmul(ps_s[t % 2][:, h, :], xn[:, c, t * P:(t + 1) * P],
                                               g.key_map[:, c, h * BLK:(h + 1) * BLK], start=(c == 0), stop=(c == C - 1))
                        mm.then_inc(sim_ready, 1)
                        if t:
                            turn(q, t - 1)
                    turn(q, TPB - 1)

        @block.scalar
        def _(act):
            act.sem_inc(kept, 1)
            act.sem_inc(ms_done, 1)
            act.sem_inc(su_done, 1)
            act.sem_inc(xc_done, 1)
            with act.Fori(0, B) as b:
                act.wait_ge(wload, b * 16 + 16)
                for k in range(BPB):
                    q = b * BPB + k
                    act.wait_ge(hid_done, q * M0 + 1)
                    for m in range(M0):
                        act.wait_ge(up_ready, q * M0 + m + 1)
                        act.activation(su[:, m, :], ps_u[:], ACT.Silu, bias=b_up[:, m:m + 1]).then_inc(su_done, 1)
                    act.wait_ge(xn_done, q * C + 1)
                    for c in range(C):
                        act.wait_ge(down_ready, q * C + c + 2)
                        act.activation(xc[:, c, :], ps_d[:], ACT.Identity, bias=b_down[:, c:c + 1]).then_inc(xc_done, 1)
                        act.wait_ge(xc_done, q * C + c + 2)
                        act.activation(sq[:, c, :], xc[:, c, :], ACT.Square).then_inc(sq_done, 1)
                    act.wait_ge(ms_ready, q + 1)
                    act.activation(ms[:], ps_d[:], ACT.Sqrt, bias=g.eps[:, 0:1]).then_inc(ms_done, 1)
                    for t in range(TPB):
                        n = q * TPB + t
                        act.wait_ge(turned, n + 3)
                        col = bass.ds(n * 64, 64)
                        for half in range(2):
                            r = slice(64 * half, 64 * half + 64)
                            f = 64 * half
                            act.activation(g.code_a[r, col], ps_t[0:64, f:f + 64], ACT.Copy).then_inc(kept, 1)
                            act.activation(g.code_b[r, col], ps_t[64:128, f:f + 64], ACT.Copy).then_inc(kept, 1)
                            act.activation(g.weight[r, col], ps_t[0:64, P + f:P + f + 64], ACT.Copy).then_inc(kept, 1)
            act.wait_ge(kept, 6 * T // P + 1)

        @block.gpsimd
        def _(pool):
            pool.sem_inc(xn_kept, 1)
            with pool.Fori(0, NBLK) as q:
                pool.wait_ge(xn_done, q * C + C + 1)
                pool.tensor_copy(g.xn[:, :, bass.ds(q * BLK, BLK)], xn[:]).then_inc(xn_kept, 1)
            pool.wait_ge(xn_kept, NBLK + 1)

        per_tile = NG + 1 + 2 * HEADS + 3 + 1 + 2 + 2 + 2 + 1 + 2 + 1 + 2

        @block.vector
        def _(dve):
            dve.sem_inc(sim_read, 2)
            dve.sem_inc(hid_done, 1)
            dve.sem_inc(xn_done, 1)
            def pick(q, t):
                n = q * TPB + t
                s = Steps(vstep, n * per_tile)
                dve.wait_ge(sim_ready, n + 1)
                dve.sem_inc(seen, 1)
                groups = [ps_s[t % 2][:, j // 8, (j % 8) * NKEYS:(j % 8 + 1) * NKEYS] for j in range(NG)]
                for j in range(NG - 1):
                    s.did(dve.max(s8[:, j, :], groups[j]))
                s.did(dve.max(s8[:, NG - 1, :], groups[NG - 1]))
                s.settle(dve)
                dve.sem_inc(seen, 1)
                for j in range(NG - 1):
                    dve.max_index(i8[:, j, :], s8[:, j, :], groups[j])
                dve.max_index(i8[:, NG - 1, :], s8[:, NG - 1, :], groups[NG - 1]).then_inc(sim_read, 1)
                pair = s8[:].rearrange("p (h two) k -> p h two k", two=2)
                s.did(dve.tensor_tensor(sums[:], pair[:, :, 0, :].unsqueeze(3).to_broadcast([P, HEADS, 8, 8]),
                                        pair[:, :, 1, :].unsqueeze(2).to_broadcast([P, HEADS, 8, 8]), ALU.add))
                s.settle(dve)
                dve.sem_inc(seen, 1)
                cand = sums[:].rearrange("p h a b -> p h (a b)")
                for h in range(HEADS):
                    s.did(dve.max(f8[:, h * 8:h * 8 + 8], cand[:, h, :]))
                s.settle(dve)
                dve.sem_inc(seen, 1)
                for h in range(HEADS):
                    s.did(dve.max_index(p8[:, h * 8:h * 8 + 8], f8[:, h * 8:h * 8 + 8], cand[:, h, :]))
                s.settle(dve)
                s.did(dve.tensor_copy(i8f[:], i8[:]))
                s.did(dve.tensor_scalar(rank[:, 0, :], p8[:], 3, None, ALU.logical_shift_right))
                s.did(dve.tensor_scalar(rank[:, 1, :], p8[:], 7, None, ALU.bitwise_and))
                s.settle(dve)
                s.did(dve.tensor_copy(rankf[:], rank[:]))
                s.settle(dve)
                for z in range(2):
                    s.did(dve.tensor_tensor(oneh[:, z, :, :], rankf[:, z, :].unsqueeze(2).to_broadcast([P, SLOTS, 8]),
                                            g.iota_a[:, 0:8].unsqueeze(1).to_broadcast([P, SLOTS, 8]), ALU.is_equal))
                s.settle(dve)
                ids = i8f[:].rearrange("p (h two) k -> p h two k", two=2)
                for z in range(2):
                    o = oneh[:, z, :, :].rearrange("p (h k) a -> p h k a", h=HEADS)
                    s.did(dve.tensor_tensor(o, o, ids[:, :, z, :].unsqueeze(2).to_broadcast([P, HEADS, 8, 8]), ALU.mult))
                s.settle(dve)
                for z in range(2):
                    s.did(dve.tensor_reduce(ij[:, z, :], oneh[:, z, :, :], AX_X, ALU.add))
                s.settle(dve)
                s.did(dve.tensor_copy(ju[:], ij[:, 1, :]))
                s.settle(dve)
                s.did(dve.tensor_scalar(jb[:, 0, :], ju[:], 1, None, ALU.bitwise_and))
                s.did(dve.tensor_scalar(jb[:, 1, :], ju[:], 1, None, ALU.logical_shift_right))
                s.settle(dve)
                s.did(dve.tensor_copy(jf[:], jb[:]))
                s.settle(dve)
                dve.wait_ge(turned, n + 1)
                s.did(dve.tensor_copy(codes[:, t % 2, 1, :], jf[:, 1, :]))
                s.did(dve.tensor_scalar(codes[:, t % 2, 2, :], f8[:], 0.0, None, ALU.max))
                dve.scalar_tensor_tensor(out=codes[:, t % 2, 0, :], in0=jf[:, 0, :], scalar=64.0, in1=ij[:, 0, :],
                                         op0=ALU.mult, op1=ALU.add).then_inc(codes_done, 1)
                dve.wait_ge(codes_done, n + 1)
                assert s.n == per_tile, s.n

            dve.wait_ge(nload, 16)
            with dve.Fori(0, B) as b:
                dve.wait_ge(wload, b * 16 + 16)
                for k in range(BPB):
                    q = b * BPB + k
                    dve.wait_ge(down_ready, q * C + 1)
                    for m in range(M0):
                        dve.wait_ge(su_done, q * M0 + m + 2)
                        dve.wait_ge(gate_ready, q * M0 + m + 1)
                        dve.scalar_tensor_tensor(out=hid[:, m, :], in0=ps_g[:], scalar=b_gate[:, m:m + 1], in1=su[:, m, :],
                                                 op0=ALU.add, op1=ALU.mult).then_inc(hid_done, 1)
                    dve.wait_ge(ms_done, q + 2)
                    dve.reciprocal(rms[:], ms[:]).then_inc(rms_done, 1)
                    dve.wait_ge(rms_done, q + 1)
                    dve.wait_ge(xn_kept, q + 1)
                    dve.wait_ge(xc_done, q * C + C + 1)
                    for c in range(C):
                        dve.scalar_tensor_tensor(out=xn[:, c, :], in0=xc[:, c, :], scalar=norm_w[:, c:c + 1], in1=rms[:],
                                                 op0=ALU.mult, op1=ALU.mult).then_inc(xn_done, 1)
                    for t in range(TPB):
                        pick(q, t)


PB = 256
NPB = T // PB
PAIRS = 16
CHUNKS = PB // 2 // PAIRS
NGRP = NJ // 2


def peer(nc, a, g):
    with Stage(nc, "peer") as st:
        sb, ps, sem = st.sb, st.ps, st.sem
        down = sb("down", [P, C, NEXP])
        up = sb("up", [P, NJ, D])
        hg = [sb(f"hg{i}", [P, NJ, PB]) for i in range(2)]
        am = [sb(f"am{i}", [P, PAIRS, P]) for i in range(2)]
        bm = [sb(f"bm{i}", [P, PAIRS, 64]) for i in range(2)]
        ps_h = [ps(f"ps_h{i}", [P, 2, PB]) for i in range(2)]
        ps_w = [ps(f"ps_w{i}", [P, PAIRS, 64]) for i in range(2)]
        ps_o = ps("ps_o", [P, C, BLK])
        loads, uload = sem("loads"), sem("uload")
        h_ready, gelu_done = sem("h_ready"), sem("gelu_done")
        a_done, beq_done, b_done = sem("a_done"), sem("beq_done"), sem("b_done")
        w_ready, p_done, o_ready, x_done = sem("w_ready"), sem("p_done"), sem("o_ready"), sem("x_done")
        block = st.block()

        @block.sync
        def _(sp):
            sp.dma_start(down[:], a["down"]).then_inc(loads, 16)
            sp.dma_start(up[:], a["up"]).then_inc(uload, 16)

        @block.tensor
        def _(pe):
            def act_rows(i, group):
                n = i * NGRP + group
                pe.wait_ge(gelu_done, n)
                for r in range(2):
                    j = 2 * group + r
                    for c in range(C):
                        mm = pe.matmul(ps_h[group % 2][:, r, :], down[:, c, j * P:(j + 1) * P],
                                       g.xn[:, c, bass.ds(i * PB, PB)], start=(c == 0), stop=(c == C - 1))
                mm.then_inc(h_ready, 1)

            def weigh(i, c):
                n = i * CHUNKS + c
                pe.wait_ge(a_done, n + 1)
                pe.wait_ge(b_done, n + 1)
                pe.wait_ge(p_done, n)
                for m in range(PAIRS):
                    mm = pe.matmul(ps_w[c % 2][:, m, :], am[c % 2][:, m, :], bm[c % 2][:, m, :], start=True, stop=True)
                mm.then_inc(w_ready, 1)

            def combine(i, half):
                pe.wait_ge(p_done, i * CHUNKS + CHUNKS + 1)
                pe.wait_ge(x_done, i * C)
                for c in range(C):
                    for j in range(NJ):
                        mm = pe.matmul(ps_o[:, c, 0:PB], up[:, j, c * P:(c + 1) * P], hg[half][:, j, :],
                                       start=(j == 0), stop=(j == NJ - 1))
                mm.then_inc(o_ready, 1)

            def work(i, half, more):
                for c in range(CHUNKS):
                    weigh(i, c)
                    if more:
                        act_rows(i + 1, 2 * c)
                        act_rows(i + 1, 2 * c + 1)
                combine(i, half)

            pe.wait_ge(loads, 16)
            for group in range(NGRP):
                act_rows(0, group)
            pe.wait_ge(uload, 16)
            work(0, 0, True)
            with pe.Fori(0, NPB // 2 - 1) as r:
                work(r * 2 + 1, 1, True)
                work(r * 2 + 2, 0, True)
            work(NPB - 1, 1, False)

        @block.scalar
        def _(act):
            def gelu(i, half):
                for group in range(NGRP):
                    act.wait_ge(h_ready, i * NGRP + group + 1)
                    act.activation(hg[half][:, 2 * group:2 * group + 2, :], ps_h[group % 2][:], ACT.Gelu).then_inc(gelu_done, 1)

            act.sem_inc(gelu_done, 1)
            gelu(0, 0)
            gelu(1, 1)
            with act.Fori(1, NPB // 2) as r:
                for k in range(2):
                    act.wait_ge(o_ready, r * 2 + k - 1)
                    gelu(r * 2 + k, k)

        @block.gpsimd
        def _(pool):
            with pool.Fori(0, NPB * CHUNKS // 2) as r:
                for k in range(2):
                    n = r * 2 + k
                    pool.wait_ge(beq_done, n + 1)
                    pool.tensor_tensor(bm[k][:], bm[k][:],
                                       g.weight[:, bass.ds(n * PAIRS, PAIRS)].unsqueeze(2).to_broadcast([P, PAIRS, 64]),
                                       ALU.mult).then_inc(b_done, 1)

        @block.vector
        def _(dve):
            def build(n, k):
                col = bass.ds(n * PAIRS, PAIRS)
                dve.tensor_tensor(bm[k][:], g.iota_b[:].unsqueeze(1).to_broadcast([P, PAIRS, 64]),
                                  g.code_b[:, col].unsqueeze(2).to_broadcast([P, PAIRS, 64]), ALU.is_equal).then_inc(beq_done, 1)
                dve.tensor_tensor(am[k][:], g.iota_a[:].unsqueeze(1).to_broadcast([P, PAIRS, P]),
                                  g.code_a[:, col].unsqueeze(2).to_broadcast([P, PAIRS, P]), ALU.is_equal).then_inc(a_done, 1)

            def add_out(i):
                dve.wait_ge(o_ready, i + 1)
                for c in range(C):
                    xs = g.x[:, c, bass.ds(i * PB, PB)]
                    dve.tensor_tensor(xs, ps_o[:, c, 0:PB], xs, ALU.add).then_inc(x_done, 1)

            def work(i, half, first, last):
                for c in range(CHUNKS):
                    n = i * CHUNKS + c
                    if not (last and c == CHUNKS - 1):
                        dve.wait_ge(w_ready, n)
                        build(n + 1, (c + 1) % 2)
                    if c == 0 and not first:
                        add_out(i - 1)
                    if c == 0:
                        dve.wait_ge(gelu_done, i * NGRP + NGRP + 1)
                    dve.wait_ge(w_ready, n + 1)
                    t0 = c // 4 * P + c % 4 * PAIRS
                    for z in range(2):
                        act_z = hg[half][:, :, t0 + 64 * z:t0 + 64 * z + PAIRS]
                        w_z = ps_w[c % 2][:, :, 32 * z:32 * z + 32].rearrange("p m j -> p j m")
                        op = dve.tensor_tensor(act_z, w_z, act_z, ALU.mult)
                    op.then_inc(p_done, 1)

            dve.sem_inc(p_done, 1)
            build(0, 0)
            work(0, 0, True, False)
            with dve.Fori(0, NPB // 2 - 1) as r:
                work(r * 2 + 1, 1, False, False)
                work(r * 2 + 2, 0, False, False)
            work(NPB - 1, 1, False, True)
            add_out(NPB - 1)
            dve.wait_ge(x_done, NPB * C)


def lora(nc, a, g):
    with Stage(nc, "lora") as st:
        sb, ps, sem = st.sb, st.ps, st.sem
        a_rows = sb("a_rows", [P, D])
        b_rows = sb("b_rows", [P, D])
        w_rep = sb("w_rep", [P, B])
        b_scaled = sb("b_scaled", [P, D])
        w_base = sb("w_base", [P, C, D])
        w_eff = sb("w_eff", [P, C, D])
        cols = sb("cols", [P, 2 * C])
        base_w = sb("base_w", [P, C, D])
        ra = sb("ra", [P, C, R1ALL])
        rb = sb("rb", [R1ALL, D])
        rw = sb("rw", [P, C, E1])
        rbias = sb("rbias", [P, E1])
        xl = sb("xl", [P, C, BLK])
        logit = sb("logit", [P, TPB, E1])
        peak = sb("peak", [P, TPB])
        ex = sb("ex", [P, TPB, E1])
        gate = sb("gate", [P, TPB, 8])
        g8 = sb("g8", [P, TPB, 8])
        gi = sb("gi", [P, TPB, 8], U32)
        gif = sb("gif", [P, TPB, 8])
        hot = sb("hot", [P, 2, TPB, E1])
        sparse = sb("sparse", [P, TPB, E1])
        total = sb("total", [P, TPB])
        inv = sb("inv", [P, TPB])
        wide = sb("wide", [P, TPB, R1ALL])
        hs = sb("hs", [R1ALL, BLK])
        hw = sb("hw", [R1ALL, BLK])
        ps_a = ps("ps_a", [P, C, BLK])
        ps_l = ps("ps_l", [P, TPB, 8])
        ps_h = ps("ps_h", [P, BLK])
        ps_w = ps("ps_w", [P, BLK])
        ps_o = ps("ps_o", [P, C, BLK])
        loads, presets = sem("loads"), sem("presets")
        scaled, fold_ready, w_done = sem("scaled"), sem("fold_ready"), sem("w_done")
        xl_ready, xl_done, l_ready, ex_done = sem("xl_ready"), sem("xl_done"), sem("l_ready"), sem("ex_done")
        h_ready, hs_done, vstep, seen = sem("h_ready"), sem("hs_done"), sem("vstep"), sem("seen")
        wide_done, w_ready, hw_done, o_ready, x_done = sem("wide_done"), sem("w_ready"), sem("hw_done"), sem("o_ready"), sem("x_done")
        block = st.block()
        names = ["l1_a", "l1_b", "l1_w", "l1_wbase", "l1_cols", "l1_basew", "l1_ra", "l1_rb", "l1_rw"]
        bufs = [a_rows, b_rows, w_rep, w_base, cols, base_w, ra, rb, rw]
        n_loads = 16 * (len(names) + 1)
        per_block = 3 + 3 + 2 * TPB + 1 + 2 + 2 + 4

        @block.sync
        def _(sp):
            for name, buf in zip(names, bufs):
                sp.dma_start(buf[:], a[name]).then_inc(loads, 16)
            sp.dma_start(rbias[:], a["l1_rbias"].partition_broadcast(P)).then_inc(loads, 16)

        @block.gpsimd
        def _(pool):
            pool.memset(gate[:], -1.0).then_inc(presets, 1)
            pool.memset(wide[:], 1.0).then_inc(presets, 1)
            pool.wait_ge(presets, 2)

        @block.tensor
        def _(pe):
            pe.sem_inc(fold_ready, 1)
            pe.sem_inc(o_ready, 1)
            pe.wait_ge(loads, n_loads)
            with pe.Fori(0, B) as b:
                pe.wait_ge(scaled, b + 1)
                pe.wait_ge(xl_done, b * (BPB * C) + 1)
                for c in range(C):
                    mm = pe.matmul(ps_a[:, c, 0:D], a_rows[:, c * P:(c + 1) * P], b_scaled[:], start=True, stop=True)
                mm.then_inc(fold_ready, 1)
                pe.wait_ge(w_done, b + 1)
                for k in range(BPB):
                    q = b * BPB + k
                    pe.wait_ge(xl_done, q * C + 1)
                    for m in range(C):
                        for c in range(C):
                            mm = pe.matmul(ps_a[:, m, :], w_eff[:, c, m * P:(m + 1) * P], g.x[:, c, bass.ds(q * BLK, BLK)],
                                           start=(c == 0), stop=(c == C - 1))
                        mm.then_inc(xl_ready, 1)
                    pe.wait_ge(xl_done, q * C + C + 1)
                    pe.wait_ge(x_done, q * C + 1)
                    for t in range(TPB):
                        for c in range(C):
                            mm = pe.matmul(ps_l[:, t, 0:E1], xl[:, c, t * P:(t + 1) * P], rw[:, c, :],
                                           start=(c == 0), stop=(c == C - 1))
                    mm.then_inc(l_ready, 1)
                    for c in range(C):
                        mm = pe.matmul(ps_h[0:R1ALL, :], ra[:, c, :], xl[:, c, :], start=(c == 0), stop=(c == C - 1))
                    mm.then_inc(h_ready, 1)
                    for m in range(C):
                        for c in range(C):
                            pe.matmul(ps_o[:, m, :], base_w[:, c, m * P:(m + 1) * P], xl[:, c, :], start=(c == 0), stop=False)
                    pe.wait_ge(wide_done, q + 1)
                    for t in range(TPB):
                        mm = pe.matmul(ps_w[0:R1ALL, t * P:(t + 1) * P], wide[:, t, :], g.ident[:], start=True, stop=True)
                    mm.then_inc(w_ready, 1)
                    pe.wait_ge(hw_done, q + 1)
                    for m in range(C):
                        mm = pe.matmul(ps_o[:, m, :], rb[:, m * P:(m + 1) * P], hw[:], start=False, stop=True)
                    mm.then_inc(o_ready, 1)

        @block.scalar
        def _(act):
            act.sem_inc(xl_done, 1)
            act.wait_ge(loads, n_loads)
            with act.Fori(0, NBLK) as q:
                act.wait_ge(o_ready, q + 1)
                for m in range(C):
                    act.wait_ge(xl_ready, q * C + m + 1)
                    act.activation(xl[:, m, :], ps_a[:, m, :], ACT.Identity, bias=cols[:, m:m + 1]).then_inc(xl_done, 1)
                act.wait_ge(h_ready, q + 1)
                act.activation(hs[:], ps_h[0:R1ALL, :], ACT.Copy).then_inc(hs_done, 1)
                act.wait_ge(vstep, q * per_block + 3)
                act.activation(ex[:], logit[:], ACT.Exp).then_inc(ex_done, 1)

        @block.vector
        def _(dve):
            dve.sem_inc(x_done, 1)
            dve.wait_ge(presets, 2)
            dve.wait_ge(loads, n_loads)
            with dve.Fori(0, B) as b:
                dve.wait_ge(fold_ready, b + 1)
                dve.tensor_scalar(b_scaled[:], b_rows[:], w_rep[:, bass.ds(b, 1)], 2.0, ALU.mult, ALU.mult).then_inc(scaled, 1)
                dve.wait_ge(fold_ready, b + 2)
                dve.tensor_tensor(w_eff[:], ps_a[:, :, 0:D], w_base[:], ALU.add).then_inc(w_done, 1)
                for k in range(BPB):
                    q = b * BPB + k
                    s = Steps(vstep, q * per_block)
                    dve.wait_ge(l_ready, q + 1)
                    s.did(dve.tensor_tensor(logit[:], ps_l[:, :, 0:E1], rbias[:].unsqueeze(1).to_broadcast([P, TPB, E1]), ALU.add))
                    s.settle(dve)
                    s.did(dve.tensor_reduce(peak[:], logit[:], AX_X, ALU.max))
                    s.settle(dve)
                    s.did(dve.tensor_tensor(logit[:], logit[:], peak[:].unsqueeze(2).to_broadcast([P, TPB, E1]), ALU.subtract))
                    dve.wait_ge(ex_done, q + 1)
                    s.did(dve.tensor_reduce(total[:], ex[:], AX_X, ALU.add))
                    s.settle(dve)
                    s.did(dve.reciprocal(inv[:], total[:]))
                    s.settle(dve)
                    s.did(dve.tensor_tensor(gate[:, :, 0:E1], ex[:], inv[:].unsqueeze(2).to_broadcast([P, TPB, E1]), ALU.mult))
                    s.settle(dve)
                    dve.sem_inc(seen, 1)
                    for t in range(TPB):
                        s.did(dve.max(g8[:, t, :], gate[:, t, :]))
                    s.settle(dve)
                    dve.sem_inc(seen, 1)
                    for t in range(TPB):
                        s.did(dve.max_index(gi[:, t, :], g8[:, t, :], gate[:, t, :]))
                    s.settle(dve)
                    s.did(dve.tensor_copy(gif[:], gi[:]))
                    s.settle(dve)
                    for z in range(2):
                        s.did(dve.tensor_tensor(hot[:, z, :, :], g.iota_a[:, 0:E1].unsqueeze(1).to_broadcast([P, TPB, E1]),
                                                gif[:, :, z:z + 1].to_broadcast([P, TPB, E1]), ALU.is_equal))
                    s.settle(dve)
                    s.did(dve.tensor_tensor(sparse[:], hot[:, 0, :, :], hot[:, 1, :, :], ALU.add))
                    s.settle(dve)
                    s.did(dve.tensor_tensor(sparse[:], sparse[:], gate[:, :, 0:E1], ALU.mult))
                    s.settle(dve)
                    s.did(dve.tensor_reduce(total[:], sparse[:], AX_X, ALU.add))
                    s.settle(dve)
                    s.did(dve.tensor_scalar(total[:], total[:], 1e-6, None, ALU.add))
                    s.settle(dve)
                    s.did(dve.reciprocal(inv[:], total[:]))
                    s.settle(dve)
                    s.did(dve.tensor_tensor(sparse[:], sparse[:], inv[:].unsqueeze(2).to_broadcast([P, TPB, E1]), ALU.mult))
                    s.settle(dve)
                    assert s.n == per_block, s.n
                    dve.tensor_copy(wide[:, :, 0:E1 * R1].rearrange("p t (e r) -> p t e r", r=R1),
                                    sparse[:].unsqueeze(3).to_broadcast([P, TPB, E1, R1])).then_inc(wide_done, 1)
                    dve.wait_ge(w_ready, q + 1)
                    dve.wait_ge(hs_done, q + 1)
                    dve.tensor_tensor(hw[:], ps_w[0:R1ALL, :], hs[:], ALU.mult).then_inc(hw_done, 1)
                    dve.wait_ge(o_ready, q + 2)
                    for m in range(C):
                        xs = g.x[:, m, bass.ds(q * BLK, BLK)]
                        dve.scalar_tensor_tensor(out=xs, in0=ps_o[:, m, :], scalar=cols[:, C + m:C + m + 1], in1=xs,
                                                 op0=ALU.add, op1=ALU.add).then_inc(x_done, 1)
            dve.wait_ge(x_done, NBLK * C + 1)


def skills(nc, a, g):
    with Stage(nc, "skills") as st:
        sb, ps, sem = st.sb, st.ps, st.sem
        nw = 2 * C * I2 + M2 * D
        w = [sb(f"w{i}", [P, nw]) for i in range(3)]
        w_gate = [x[:, 0:C * I2].rearrange("p (c i) -> p c i", c=C) for x in w]
        w_up = [x[:, C * I2:2 * C * I2].rearrange("p (c i) -> p c i", c=C) for x in w]
        w_down = [x[:, 2 * C * I2:nw].rearrange("p (m d) -> p m d", m=M2) for x in w]
        act_g = [sb(f"act_g{i}", [P, BLK]) for i in range(2)]
        hid = [sb(f"hid{i}", [P, BLK]) for i in range(4)]
        ps_g = [ps(f"ps_g{i}", [P, BLK]) for i in range(2)]
        ps_u = [ps(f"ps_u{i}", [P, BLK]) for i in range(2)]
        acc = [[ps(f"acc{k}{c}", [P, BLK]) for c in range(C)] for k in range(BPB)]
        wload = [sem(f"wload{i}") for i in range(3)]
        g_ready, u_ready, gelu_done, hid_done = sem("g_ready"), sem("u_ready"), sem("gelu_done"), sem("hid_done")
        d_ready, y_done = sem("d_ready"), sem("y_done")
        block = st.block()
        plan = [(s, k, m) for s in range(3) for k in range(BPB) for m in range(M2)]
        n_b = len(plan)

        @block.sync
        def _(sp):
            with sp.Fori(0, B) as b:
                for s in range(2):
                    e = sp.value_load(g.pair_idx[0:1, bass.ds(b * 8 + s, 1)], min_val=0, max_val=E8 - 1)
                    sp.wait_ge(d_ready, b * n_b + 1)
                    sp.dma_start(w[s][:], a["skills"][bass.ds(e, 1), :, :].rearrange("a p n -> p (a n)")).then_inc(wload[s], 16)
                sp.dma_start(w[2][:], a["skill_shared"]).then_inc(wload[2], 16)

        @block.tensor
        def _(pe):
            pe.sem_inc(d_ready, 1)
            def down(b, j):
                s, k, m = plan[j]
                n = b * n_b + j
                pe.wait_ge(hid_done, n + 3)
                if j == 0:
                    pe.wait_ge(y_done, b * (BPB * C) + 1)
                for c in range(C):
                    mm = pe.matmul(acc[k][c][:], w_down[s][:, m, c * P:(c + 1) * P], hid[j % 4][:],
                                   start=(s == 0 and m == 0), stop=(s == 2 and m == M2 - 1))
                mm.then_inc(d_ready, 1)

            with pe.Fori(0, B) as b:
                for j, (s, k, m) in enumerate(plan):
                    n = b * n_b + j
                    if k == 0 and m == 0:
                        pe.wait_ge(wload[s], b * 16 + 16)
                    for weight, bank, free, ready in ((w_gate[s], ps_g[j % 2], gelu_done, g_ready),
                                                      (w_up[s], ps_u[j % 2], hid_done, u_ready)):
                        pe.wait_ge(free, n + 1)
                        for c in range(C):
                            mm = pe.matmul(bank[:], weight[:, c, m * P:(m + 1) * P],
                                           g.x[:, c, bass.ds((b * BPB + k) * BLK, BLK)], start=(c == 0), stop=(c == C - 1))
                        mm.then_inc(ready, 1)
                    if j:
                        down(b, j - 1)
                down(b, n_b - 1)

        @block.scalar
        def _(act):
            act.sem_inc(gelu_done, 2)
            act.sem_inc(y_done, 1)
            with act.Fori(0, B) as b:
                for j in range(n_b):
                    n = b * n_b + j
                    act.wait_ge(g_ready, n + 1)
                    act.wait_ge(hid_done, n + 1)
                    act.activation(act_g[j % 2][:], ps_g[j % 2][:], ACT.Gelu_apprx_tanh).then_inc(gelu_done, 1)
                act.wait_ge(d_ready, b * n_b + n_b + 1)
                for k in range(BPB):
                    for c in range(C):
                        act.activation(g.y[:, c, bass.ds((b * BPB + k) * BLK, BLK)], acc[k][c][:], ACT.Copy).then_inc(y_done, 1)
            act.wait_ge(y_done, NBLK * C + 1)

        @block.vector
        def _(dve):
            dve.sem_inc(hid_done, 2)
            with dve.Fori(0, B) as b:
                for j, (s, k, m) in enumerate(plan):
                    n = b * n_b + j
                    dve.wait_ge(gelu_done, n + 3)
                    dve.wait_ge(u_ready, n + 1)
                    if j >= 4:
                        dve.wait_ge(d_ready, n - 3 + 1)
                    else:
                        dve.wait_ge(d_ready, b * n_b + 1)
                    scale = g.pair_w[:, bass.ds(b * 2 + s, 1)] if s < 2 else 1.0
                    dve.scalar_tensor_tensor(out=hid[j % 4][:], in0=ps_u[j % 2][:], scalar=scale, in1=act_g[j % 2][:],
                                             op0=ALU.mult, op1=ALU.mult).then_inc(hid_done, 1)


NQW = C * Q2
NQB = 3 * NQW // QB


def weights4(nc, a, g):
    with Stage(nc, "weights4") as st:
        sb, ps, sem = st.sb, st.ps, st.sem
        w = sb("w", [P, NQB, QB])
        peak = sb("peak", [P, NQB])
        scale = sb("scale", [P, NQB])
        inv = sb("inv", [P, NQB])
        bank = [ps(f"bank{i}", [P, 4, P]) for i in range(2)]
        loads, vstep, turned, kept = sem("loads"), sem("vstep"), sem("turned"), sem("kept")
        block = st.block()
        flat = w[:].rearrange("p n q -> p (n q)")

        @block.sync
        def _(sp):
            sp.dma_start(flat, a["q_w"]).then_inc(loads, 16)

        @block.vector
        def _(dve):
            s = Steps(vstep)
            dve.wait_ge(loads, 16)
            for op in (
                lambda: dve.tensor_reduce(peak[:], w[:], AX_X, ALU.max, apply_absolute_value=True),
                lambda: dve.tensor_scalar(scale[:], peak[:], 1.0 / 7, 1e-12, ALU.mult, ALU.max),
                lambda: dve.reciprocal(inv[:], scale[:]),
                lambda: dve.tensor_tensor(w[:], w[:], inv[:].unsqueeze(2).to_broadcast([P, NQB, QB]), ALU.mult),
                lambda: dve.tensor_scalar(flat, flat, ROUND, ROUND, ALU.add, ALU.subtract),
                lambda: dve.tensor_scalar(flat, flat, -8.0, 7.0, ALU.max, ALU.min),
                lambda: dve.tensor_tensor(w[:], w[:], scale[:].unsqueeze(2).to_broadcast([P, NQB, QB]), ALU.mult),
            ):
                s.did(op())
                s.settle(dve)

        turns = [(flat[:, (z * MQ + m) * D + c * P:(z * MQ + m) * D + (c + 1) * P], z, c, m)
                 for z in range(2) for c in range(C) for m in range(MQ)]
        turns += [(flat[:, 2 * NQW + c * Q2 + m * P:2 * NQW + c * Q2 + (m + 1) * P], 2, m, c)
                  for m in range(MQ) for c in range(C)]

        @block.tensor
        def _(pe):
            pe.wait_ge(vstep, 7)
            for n, (src, *_) in enumerate(turns):
                r = n // 4
                if n % 4 == 0 and r >= 2:
                    pe.wait_ge(kept, r - 1)
                mm = pe.transpose(bank[r % 2][:, n % 4, :], src, g.ident[:])
                if n % 4 == 3:
                    mm.then_inc(turned, 1)

        @block.scalar
        def _(act):
            dst = g.qw[:].rearrange("p (r n) -> p r n", n=4 * P)
            for r in range(len(turns) // 4):
                act.wait_ge(turned, r + 1)
                act.activation(dst[:, r, :], bank[r % 2][:].rearrange("p a b -> p (a b)"), ACT.Copy).then_inc(kept, 1)
            act.wait_ge(kept, len(turns) // 4)


def quant_ffn(nc, a, g):
    with Stage(nc, "quant") as st:
        sb, ps, sem = st.sb, st.ps, st.sem
        wt = [g.qw[:, z * NQW:(z + 1) * NQW].rearrange("p (c i) -> p c i", c=C) for z in range(2)]
        wd = g.qw[:, 2 * NQW:3 * NQW].rearrange("p (m d) -> p m d", m=MQ)
        up = sb("up", [P, MQ, T])
        gate = sb("gate", [P, MQ, T])
        sig = sb("sig", [P, T])
        peaks = sb("peaks", [P, 16])
        top = sb("top", [P, 8])
        alltop = sb("alltop", [P, 8])
        scale = sb("scale", [P, 8])
        inv = sb("inv", [P, 8])
        ps_m = [ps(f"ps_m{i}", [P, BLK]) for i in range(8)]
        vstep, spread, mm_ready, kept = sem("vstep"), sem("spread"), sem("mm_ready"), sem("kept")
        sig_done, sigq_done, x_done, d_ready = sem("sig_done"), sem("sigq_done"), sem("x_done"), sem("d_ready")
        block = st.block()
        marks = {}

        def quant(dve, s, t, n):
            s.did(dve.tensor_scalar(t, t, inv[:, n:n + 1], ROUND, ALU.mult, ALU.add))
            s.settle(dve)
            s.did(dve.tensor_scalar(t, t, ROUND, 32767.0, ALU.subtract, ALU.min))
            s.settle(dve)
            s.did(dve.tensor_scalar(t, t, -32768.0, scale[:, n:n + 1], ALU.max, ALU.mult))

        def scales(dve, s, n, count):
            s.settle(dve)
            s.did(dve.tensor_reduce(top[:, n:n + 1], peaks[:, 0:count], AX_X, ALU.max))
            marks["top", n] = s.n
            dve.wait_ge(spread, n + 1)
            s.did(dve.tensor_scalar(scale[:, n:n + 1], alltop[:, n:n + 1], 1.0 / 32767, 1e-12, ALU.mult, ALU.max))
            s.settle(dve)
            s.did(dve.reciprocal(inv[:, n:n + 1], scale[:, n:n + 1]))
            s.settle(dve)

        def peak(dve, s, t, n):
            s.did(dve.tensor_reduce(peaks[:, n:n + 1], t, AX_X, ALU.max, apply_absolute_value=True))

        @block.vector
        def _(dve):
            s = Steps(vstep)
            for c in range(C):
                peak(dve, s, g.y[:, c, :], c)
            scales(dve, s, 0, C)
            for c in range(C):
                quant(dve, s, g.y[:, c, :], 0)
            marks["x"] = s.n
            for z, t in enumerate((up, gate)):
                for m in range(MQ):
                    dve.wait_ge(kept, NBLK * (z * MQ + m + 1))
                    peak(dve, s, t[:, m, :], m)
                scales(dve, s, 1 + z, MQ)
                for m in range(MQ):
                    quant(dve, s, t[:, m, :], 1 + z)
                    marks[z, m] = s.n
            for m in range(MQ):
                dve.wait_ge(sig_done, m + 1)
                s.did(dve.tensor_scalar(sig[:], sig[:], 65536.0, ROUND, ALU.mult, ALU.add))
                s.settle(dve)
                s.did(dve.tensor_scalar(sig[:], sig[:], ROUND, 65535.0, ALU.subtract, ALU.min))
                s.settle(dve)
                s.did(dve.tensor_scalar(sig[:], sig[:], 0.0, 1.0 / 65536, ALU.max, ALU.mult))
                s.settle(dve)
                dve.tensor_tensor(gate[:, m, :], gate[:, m, :], sig[:], ALU.mult).then_inc(sigq_done, 1)
                dve.wait_ge(sigq_done, m + 1)
                peak(dve, s, gate[:, m, :], m)
            scales(dve, s, 3, MQ)
            for m in range(MQ):
                quant(dve, s, gate[:, m, :], 3)
                s.settle(dve)
                s.did(dve.tensor_tensor(gate[:, m, :], gate[:, m, :], up[:, m, :], ALU.mult))
                s.settle(dve)
                peak(dve, s, gate[:, m, :], m)
            scales(dve, s, 4, MQ)
            for m in range(MQ):
                quant(dve, s, gate[:, m, :], 4)
                marks["o", m] = s.n
            for q in range(NBLK):
                for c in range(C):
                    dve.wait_ge(d_ready, q * C + c + 1)
                    xs = g.x[:, c, q * BLK:(q + 1) * BLK]
                    dve.tensor_tensor(xs, ps_m[(q * C + c) % 8][:], xs, ALU.add).then_inc(x_done, 1)
            dve.wait_ge(x_done, NBLK * C)

        @block.gpsimd
        def _(pool):
            for n in range(5):
                pool.wait_ge(vstep, marks["top", n])
                pool.partition_all_reduce(alltop[:, n:n + 1], top[:, n:n + 1], P, bass.bass_isa.ReduceOp.max).then_inc(spread, 1)
            pool.wait_ge(spread, 5)

        @block.tensor
        def _(pe):
            pe.wait_ge(vstep, marks["x"])
            n = 0
            for z in range(2):
                for m in range(MQ):
                    for q in range(NBLK):
                        if n >= 8:
                            pe.wait_ge(kept, n - 7)
                        for c in range(C):
                            mm = pe.matmul(ps_m[n % 8][:], wt[z][:, c, m * P:(m + 1) * P], g.y[:, c, q * BLK:(q + 1) * BLK],
                                           start=(c == 0), stop=(c == C - 1))
                        mm.then_inc(mm_ready, 1)
                        n += 1
            pe.wait_ge(kept, n)
            for m in range(MQ):
                pe.wait_ge(vstep, marks["o", m])
                for q in range(NBLK):
                    for c in range(C):
                        mm = pe.matmul(ps_m[(q * C + c) % 8][:], wd[:, m, c * P:(c + 1) * P], gate[:, m, q * BLK:(q + 1) * BLK],
                                       start=(m == 0), stop=(m == MQ - 1))
                        if m == MQ - 1:
                            mm.then_inc(d_ready, 1)

        @block.scalar
        def _(act):
            n = 0
            for t in (up, gate):
                for m in range(MQ):
                    for q in range(NBLK):
                        act.wait_ge(mm_ready, n + 1)
                        act.activation(t[:, m, q * BLK:(q + 1) * BLK], ps_m[n % 8][:], ACT.Copy).then_inc(kept, 1)
                        n += 1
            for m in range(MQ):
                act.wait_ge(vstep, marks[1, m])
                act.wait_ge(sigq_done, m)
                act.activation(sig[:], gate[:, m, :], ACT.Sigmoid).then_inc(sig_done, 1)


NQKV = 3 * C
NP3 = S // BLK


def attend(nc, a, g):
    with Stage(nc, "attend") as st:
        sb, ps, sem = st.sb, st.ps, st.sem
        ws = sb("ws", [P, E3, C * D])
        mask = sb("mask", [P, C * D])
        wb = sb("wb", [P, B, C * D])
        w_bot = wb[:].rearrange("p b (c o) -> p b c o", c=C)
        w_in = sb("w_in", [P, C, 3 * D])
        b_in = sb("b_in", [P, NQKV])
        qkv = sb("qkv", [P, NQKV, T])
        heads = sb("heads", [P, P])
        prod = sb("prod", [P, B, B, BLK])
        sc = sb("sc", [P, B, B, BLK])
        peak = sb("peak", [P, B, BLK])
        total = sb("total", [P, B, BLK])
        ps_m = [ps(f"ps_m{i}", [P, BLK]) for i in range(4)]
        ps_s = ps("ps_s", [P, 4, BLK])
        loads, presets, w_step = sem("loads"), sem("presets"), sem("w_step")
        x_ready, x_done, q_ready, q_done = sem("x_ready"), sem("x_done"), sem("q_ready"), sem("q_done")
        vstep, s_ready, sc_done, ex_done = sem("vstep"), sem("s_ready"), sem("sc_done"), sem("ex_done")
        block = st.block()
        names, bufs = ["l3_w", "l3_mask", "l3_win", "l3_bin", "l3_bbot"], [ws, mask, w_in, b_in, g.b_bot]
        per_step = 8

        @block.sync
        def _(sp):
            for name, buf in zip(names, bufs):
                sp.dma_start(buf[:], a[name]).then_inc(loads, 16)

        @block.gpsimd
        def _(pool):
            pool.memset(heads[:], 0.0).then_inc(presets, 1)
            pool.wait_ge(presets, 1)
            for r in (slice(0, HD), slice(HD, P)):
                pool.memset(heads[r, r], 1.0).then_inc(presets, 1)
            pool.wait_ge(presets, 3)

        @block.tensor
        def _(pe):
            pe.sem_inc(s_ready, 1)
            pe.wait_ge(loads, 16 * len(names))
            pe.wait_ge(w_step, B * (E3 + 1))
            for b in range(B):
                for k in range(BPB):
                    for m in range(C):
                        n = (b * BPB + k) * C + m
                        if n >= 4:
                            pe.wait_ge(x_done, n - 3)
                        for c in range(C):
                            mm = pe.matmul(ps_m[n % 4][:], w_bot[:, b, c, m * P:(m + 1) * P],
                                           g.x[:, c, (b * BPB + k) * BLK:(b * BPB + k + 1) * BLK],
                                           start=(c == 0), stop=(c == C - 1))
                        mm.then_inc(x_ready, 1)
            pe.wait_ge(x_done, NBLK * C)
            with pe.Fori(0, NBLK) as q:
                for m in range(NQKV):
                    n = q * NQKV + m
                    pe.wait_ge(q_done, n - min(m, 3) + 1)
                    for c in range(C):
                        mm = pe.matmul(ps_m[m % 4][:], w_in[:, c, m * P:(m + 1) * P], g.y[:, c, bass.ds(q * BLK, BLK)],
                                       start=(c == 0), stop=(c == C - 1))
                    mm.then_inc(q_ready, 1)
            pe.wait_ge(presets, 3)
            with pe.Fori(0, NP3) as r:
                for c in range(C):
                    n = r * C + c
                    pe.wait_ge(vstep, n * per_step + 2)
                    pe.wait_ge(sc_done, n + 1)
                    for z in range(4):
                        mm = pe.matmul(ps_s[:, z, :], heads[:], prod[:, z // B, z % B, :], start=True, stop=True)
                    mm.then_inc(s_ready, 1)

        @block.scalar
        def _(act):
            act.sem_inc(q_done, 1)
            act.sem_inc(sc_done, 1)
            act.wait_ge(loads, 16 * len(names))
            for n in range(NBLK * C):
                q, m = n // C, n % C
                act.wait_ge(x_ready, n + 1)
                act.activation(g.y[:, m, q * BLK:(q + 1) * BLK], ps_m[n % 4][:], ACT.Identity,
                               bias=g.b_bot[:, m:m + 1]).then_inc(x_done, 1)
            with act.Fori(0, NBLK) as q:
                for m in range(NQKV):
                    act.wait_ge(q_ready, q * NQKV + m + 1)
                    act.activation(qkv[:, m, bass.ds(q * BLK, BLK)], ps_m[m % 4][:], ACT.Identity,
                                   bias=b_in[:, m:m + 1]).then_inc(q_done, 1)
            with act.Fori(0, NP3) as r:
                for c in range(C):
                    n = r * C + c
                    act.wait_ge(s_ready, n + 2)
                    act.wait_ge(vstep, n * per_step + 1)
                    act.activation(sc[:].rearrange("p l m t -> p (l m) t"), ps_s[:], ACT.Copy,
                                   scale=1.0 / 8).then_inc(sc_done, 1)
                    act.wait_ge(vstep, n * per_step + 4)
                    act.activation(sc[:], sc[:], ACT.Exp).then_inc(ex_done, 1)

        @block.vector
        def _(dve):
            dve.sem_inc(vstep, 1)
            s = Steps(w_step)
            dve.wait_ge(loads, 16 * len(names))
            for b in range(B):
                for e in range(E3):
                    y = g.cond_all[:, b * E8 + e:b * E8 + e + 1]
                    s.settle(dve)
                    if e == 0:
                        s.did(dve.tensor_scalar(wb[:, b, :], ws[:, 0, :], y, None, ALU.mult))
                    else:
                        s.did(dve.scalar_tensor_tensor(out=wb[:, b, :], in0=ws[:, e, :], scalar=y, in1=wb[:, b, :],
                                                       op0=ALU.mult, op1=ALU.add))
                s.settle(dve)
                s.did(dve.tensor_tensor(wb[:, b, :], wb[:, b, :], mask[:], ALU.mult))
            dve.wait_ge(q_done, NBLK * NQKV + 1)
            with dve.Fori(0, NP3) as r:
                for c in range(C):
                    n = r * C + c
                    s = Steps(vstep, n * per_step + 1)

                    def rows(m):
                        return qkv[:, m, :].rearrange("p (b t) -> p b t", b=B)[:, :, bass.ds(r * BLK, BLK)]

                    dve.wait_ge(s_ready, n + 1)
                    s.did(dve.tensor_tensor(prod[:], rows(c).unsqueeze(2).to_broadcast([P, B, B, BLK]),
                                            rows(C + c).unsqueeze(1).to_broadcast([P, B, B, BLK]), ALU.mult))
                    dve.wait_ge(sc_done, n + 2)
                    s.did(dve.tensor_tensor(peak[:], sc[:, :, 0, :], sc[:, :, 1, :], ALU.max))
                    s.settle(dve)
                    s.did(dve.tensor_tensor(sc[:], sc[:], peak[:].unsqueeze(2).to_broadcast([P, B, B, BLK]), ALU.subtract))
                    dve.wait_ge(ex_done, n + 1)
                    s.did(dve.tensor_tensor(total[:], sc[:, :, 0, :], sc[:, :, 1, :], ALU.add))
                    s.settle(dve)
                    s.did(dve.reciprocal(total[:], total[:]))
                    v = rows(2 * C + c).unsqueeze(1).to_broadcast([P, B, B, BLK])
                    s.did(dve.tensor_tensor(sc[:], sc[:], v, ALU.mult))
                    s.settle(dve)
                    s.did(dve.tensor_tensor(peak[:], sc[:, :, 0, :], sc[:, :, 1, :], ALU.add))
                    s.settle(dve)
                    o = g.o[:, c, :].rearrange("p (b t) -> p b t", b=B)[:, :, bass.ds(r * BLK, BLK)]
                    s.did(dve.tensor_tensor(o, peak[:], total[:], ALU.mult))
                    s.settle(dve)
                    assert s.n == per_step


def norm(nc, a, g):
    with Stage(nc, "norm") as st:
        sb, ps, sem = st.sb, st.ps, st.sem
        w_out = sb("w_out", [P, C, D])
        wg = sb("wg", [P, C, E3])
        cols = sb("cols", [P, 3 * C])
        r = sb("r", [P, C, BLK])
        sq = sb("sq", [P, C, BLK])
        sd = sb("sd", [P, BLK])
        y = sb("y", [P, C, BLK])
        ps_m = ps("ps_m", [P, C, BLK])
        ps_v = ps("ps_v", [P, 2, BLK])
        ps_l = ps("ps_l", [P, TPB, E3])
        loads, m_ready, mean_ready, var_ready = sem("loads"), sem("m_ready"), sem("mean_ready"), sem("var_ready")
        sq_done, sd_done, vstep, y_done, l_ready, l_done, y_kept = (
            sem("sq_done"), sem("sd_done"), sem("vstep"), sem("y_done"), sem("l_ready"), sem("l_done"), sem("y_kept"))
        block = st.block()
        names, bufs = ["l3_wout", "l3_wg", "l3_cols"], [w_out, wg, cols]
        per_block = 4 * C + 1

        @block.sync
        def _(sp):
            for name, buf in zip(names, bufs):
                sp.dma_start(buf[:], a[name]).then_inc(loads, 16)

        @block.tensor
        def _(pe):
            pe.sem_inc(l_ready, 1)
            pe.sem_inc(var_ready, 1)
            pe.wait_ge(loads, 16 * len(names))
            with pe.Fori(0, NBLK) as q:
                pe.wait_ge(vstep, q * per_block + 1)
                for m in range(C):
                    for c in range(C):
                        mm = pe.matmul(ps_m[:, m, :], w_out[:, c, m * P:(m + 1) * P], g.o[:, c, bass.ds(q * BLK, BLK)],
                                       start=(c == 0), stop=(c == C - 1))
                    mm.then_inc(m_ready, 1)
                pe.wait_ge(vstep, q * per_block + C + 1)
                for c in range(C):
                    mm = pe.matmul(ps_v[:, 0, :], g.mean_w[:], r[:, c, :], start=(c == 0), stop=(c == C - 1))
                mm.then_inc(mean_ready, 1)
                pe.wait_ge(sq_done, q * C + C)
                for c in range(C):
                    mm = pe.matmul(ps_v[:, 1, :], g.mean_w[:], sq[:, c, :], start=(c == 0), stop=(c == C - 1))
                mm.then_inc(var_ready, 1)
                pe.wait_ge(y_done, q * C + C + 1)
                pe.wait_ge(l_done, q + 1)
                for t in range(TPB):
                    for c in range(C):
                        mm = pe.matmul(ps_l[:, t, :], y[:, c, t * P:(t + 1) * P], wg[:, c, :], start=(c == 0), stop=(c == C - 1))
                mm.then_inc(l_ready, 1)

        @block.scalar
        def _(act):
            act.sem_inc(l_done, 1)
            act.sem_inc(y_done, 1)
            act.wait_ge(loads, 16 * len(names))
            with act.Fori(0, NBLK) as q:
                act.wait_ge(var_ready, q + 1)
                for c in range(C):
                    act.wait_ge(vstep, q * per_block + C + c + 2)
                    act.activation(sq[:, c, :], r[:, c, :], ACT.Square).then_inc(sq_done, 1)
                act.wait_ge(var_ready, q + 2)
                act.activation(sd[:], ps_v[:, 1, :], ACT.Sqrt, bias=g.eps[:, 1:2]).then_inc(sd_done, 1)
                act.wait_ge(l_ready, q + 1)
                act.wait_ge(y_kept, q + 1)
                for c in range(C):
                    act.wait_ge(vstep, q * per_block + 3 * C + 1 + c + 2)
                    act.activation(y[:, c, :], r[:, c, :], ACT.Identity, bias=cols[:, 2 * C + c:2 * C + c + 1]).then_inc(y_done, 1)
                act.wait_ge(l_ready, q + 2)
                act.activation(g.logit[:, bass.ds(q * TPB, TPB), :], ps_l[:], ACT.Copy).then_inc(l_done, 1)
            act.wait_ge(l_done, NBLK + 1)

        @block.gpsimd
        def _(pool):
            pool.sem_inc(y_kept, 1)
            with pool.Fori(0, NBLK) as q:
                pool.wait_ge(y_done, q * C + C + 1)
                pool.tensor_copy(g.y[:, :, bass.ds(q * BLK, BLK)], y[:]).then_inc(y_kept, 1)
            pool.wait_ge(y_kept, NBLK + 1)

        @block.vector
        def _(dve):
            dve.sem_inc(vstep, 1)
            dve.wait_ge(loads, 16 * len(names))
            with dve.Fori(0, NBLK) as q:
                s = Steps(vstep, q * per_block + 1)
                dve.wait_ge(y_done, q * C + 1)
                for c in range(C):
                    dve.wait_ge(m_ready, q * C + c + 1)
                    s.did(dve.scalar_tensor_tensor(out=r[:, c, :], in0=ps_m[:, c, :], scalar=cols[:, c:c + 1],
                                                   in1=g.y[:, c, bass.ds(q * BLK, BLK)], op0=ALU.add, op1=ALU.add))
                dve.wait_ge(mean_ready, q + 1)
                for c in range(C):
                    s.did(dve.tensor_tensor(r[:, c, :], r[:, c, :], ps_v[:, 0, :], ALU.subtract))
                dve.wait_ge(sd_done, q + 1)
                s.did(dve.reciprocal(sd[:], sd[:]))
                for c in range(C):
                    s.did(dve.tensor_scalar(r[:, c, :], r[:, c, :], cols[:, C + c:C + c + 1], None, ALU.mult))
                s.settle(dve)
                for c in range(C):
                    s.did(dve.tensor_tensor(r[:, c, :], r[:, c, :], sd[:], ALU.mult))
                assert s.n == per_block


NT = T // P


def experts(nc, a, g):
    with Stage(nc, "experts") as st:
        sb, ps, sem = st.sb, st.ps, st.sem
        n_f = FF // P
        w1 = [sb(f"w1{i}", [P, n_f, D]) for i in range(2)]
        w2 = [sb(f"w2{i}", [P, n_f, D]) for i in range(2)]
        b1 = sb("b1", [P, n_f * E3])
        b2 = sb("b2", [P, C, E3])
        bc = sb("bc", [P, C, E3])
        ps_w = [ps(f"ps_w{i}", [P, C, D]) for i in range(2)]
        ps_b = [ps(f"ps_b{i}", [P, E3]) for i in range(C)]
        ps_c = ps("ps_c", [P, D])
        bload, loads = sem("bload"), [sem(f"loads{i}") for i in range(2)]
        folded, kept, turned = sem("folded"), sem("kept"), sem("turned")
        block = st.block()

        @block.sync
        def _(sp):
            sp.dma_start(b1[:], a["l3_b1"]).then_inc(bload, 16)
            sp.dma_start(b2[:], a["l3_b2"]).then_inc(bload, 16)
            for e in range(E3):
                if e >= 2:
                    sp.wait_ge(folded, e - 1)
                sp.dma_start(w1[e % 2][:], a["l3_w1"][e]).then_inc(loads[e % 2], 16)
                sp.dma_start(w2[e % 2][:], a["l3_w2"][e]).then_inc(loads[e % 2], 16)

        @block.tensor
        def _(pe):
            pe.wait_ge(bload, 32)
            for e in range(E3):
                pe.wait_ge(loads[e % 2], 32 * (e // 2 + 1))
                if e >= 2:
                    pe.wait_ge(kept, e - 1)
                for c in range(C):
                    for f in range(n_f):
                        pe.matmul(ps_w[e % 2][:, c, :], w1[e % 2][:, f, c * P:(c + 1) * P], w2[e % 2][:, f, :],
                                  start=(f == 0), stop=(f == n_f - 1))
                for c in range(C):
                    for f in range(n_f):
                        mm = pe.matmul(ps_b[c][:, e:e + 1], w2[e % 2][:, f, c * P:(c + 1) * P],
                                       b1[:, f * E3 + e:f * E3 + e + 1], start=(f == 0), stop=(f == n_f - 1))
                mm.then_inc(folded, 1)
            pe.wait_ge(kept, E3 + C)
            for c in range(C):
                mm = pe.transpose(ps_c[0:E3, c * P:(c + 1) * P], bc[:, c, :], g.ident[:])
            mm.then_inc(turned, 1)

        @block.vector
        def _(dve):
            for e in range(E3):
                dve.wait_ge(folded, e + 1)
                dve.tensor_copy(g.w12[:, e, :, :], ps_w[e % 2][:]).then_inc(kept, 1)
            for c in range(C):
                dve.tensor_tensor(bc[:, c, :], ps_b[c][:], b2[:, c, :], ALU.add).then_inc(kept, 1)
            dve.wait_ge(turned, 1)
            dve.tensor_copy(g.c12[:], ps_c[0:E3, :]).then_inc(kept, 1)
            dve.wait_ge(kept, E3 + C + 1)


def gates(nc, a, g):
    with Stage(nc, "gates") as st:
        sb, ps, sem = st.sb, st.ps, st.sem
        peak = sb("peak", [P, NT])
        total = sb("total", [P, NT])
        ex = sb("ex", [P, NT, E3])
        g8 = sb("g8", [P, NT, 8])
        gi = sb("gi", [P, NT, 8], U32)
        gif = sb("gif", [P, NT, 8])
        hot = sb("hot", [P, NT, E3])
        before = sb("before", [P, NT, E3])
        keep = sb("keep", [P, NT, E3])
        upto = sb("upto", [P, P])
        ones = sb("ones", [P, P])
        ps_c = ps("ps_c", [P, NT, E3])
        ps_n = ps("ps_n", [P, NT, E3])
        ps_t = ps("ps_t", [P, NT * P])
        presets, vstep, ex_done, counted, turned, kept = (
            sem("presets"), sem("vstep"), sem("ex_done"), sem("counted"), sem("turned"), sem("kept"))
        block = st.block()
        marks = {}
        wide = [P, NT, E3]

        @block.gpsimd
        def _(pool):
            pool.memset(ones[:], 1.0).then_inc(presets, 1)
            pool.memset(upto[:], 1.0).then_inc(presets, 1)
            pool.wait_ge(presets, 2)
            pool.affine_select(out=upto[:], in_=upto[:], compare_op=ALU.is_ge, fill=0.0, base=0,
                               pattern=[[1, P]], channel_multiplier=-1).then_inc(presets, 1)
            pool.wait_ge(presets, 3)

        @block.vector
        def _(dve):
            s = Steps(vstep)

            def then(*ops):
                for op in ops:
                    s.did(op)
                s.settle(dve)

            then(dve.tensor_reduce(peak[:], g.logit[:], AX_X, ALU.max))
            then(dve.tensor_tensor(g.logit[:], g.logit[:], peak[:].unsqueeze(2).to_broadcast(wide), ALU.subtract))
            marks["shifted"] = s.n
            dve.wait_ge(ex_done, 1)
            then(dve.tensor_reduce(total[:], ex[:], AX_X, ALU.add))
            then(dve.reciprocal(total[:], total[:]))
            then(dve.tensor_tensor(ex[:], ex[:], total[:].unsqueeze(2).to_broadcast(wide), ALU.mult))
            then(*[dve.max(g8[:, t, :], ex[:, t, :]) for t in range(NT)])
            then(*[dve.max_index(gi[:, t, :], g8[:, t, :], ex[:, t, :]) for t in range(NT)])
            then(dve.tensor_copy(gif[:], gi[:]))
            then(dve.tensor_tensor(hot[:], g.iota_a[:, 0:E3].unsqueeze(1).to_broadcast(wide),
                                   gif[:, :, 0:1].to_broadcast(wide), ALU.is_equal))
            marks["hot"] = s.n
            then(dve.memset(before[:, 0, :], 0.0))
            dve.wait_ge(counted, 2)
            for t in range(1, NT):
                then(dve.tensor_tensor(before[:, t, :], ps_n[:, t - 1, :], before[:, t - 1, :], ALU.add))
            then(dve.tensor_tensor(keep[:], ps_c[:], before[:], ALU.add))
            then(dve.scalar_tensor_tensor(out=hot[:], in0=keep[:], scalar=float(CAP), in1=hot[:],
                                          op0=ALU.is_le, op1=ALU.mult))
            then(dve.tensor_tensor(hot[:], hot[:], g8[:, :, 0:1].to_broadcast(wide), ALU.mult))
            marks["weight"] = s.n
            for b in range(4):
                dve.wait_ge(turned, b + 1)
                dve.tensor_copy(g.weight8[:, b * BLK:(b + 1) * BLK], ps_t[0:E3, b * BLK:(b + 1) * BLK]).then_inc(kept, 1)
            dve.wait_ge(kept, 4)

        @block.scalar
        def _(act):
            act.wait_ge(vstep, marks["shifted"])
            act.activation(ex[:], g.logit[:], ACT.Exp).then_inc(ex_done, 1)

        @block.tensor
        def _(pe):
            pe.wait_ge(presets, 3)
            pe.wait_ge(vstep, marks["hot"])
            flat = hot[:].rearrange("p t e -> p (t e)")
            pe.matmul(ps_c[:].rearrange("p t e -> p (t e)"), upto[:], flat, start=True, stop=True).then_inc(counted, 1)
            pe.matmul(ps_n[:].rearrange("p t e -> p (t e)"), ones[:], flat, start=True, stop=True).then_inc(counted, 1)
            pe.wait_ge(vstep, marks["weight"])
            for t in range(NT):
                mm = pe.transpose(ps_t[0:E3, t * P:(t + 1) * P], hot[:, t, :], g.ident[:])
                if t % 4 == 3:
                    mm.then_inc(turned, 1)


def moe(nc, a, g, out):
    with Stage(nc, "moe") as st:
        sb, ps, sem = st.sb, st.ps, st.sem
        sel = sb("sel", [E3, E3, P])
        cols = sb("cols", [P, 2 * C])
        xm = [sb(f"xm{i}", [P, C, BLK]) for i in range(2)]
        r = sb("r", [P, C, BLK])
        sq = sb("sq", [P, C, BLK])
        sd = sb("sd", [P, BLK])
        o = sb("o", [P, C, BLK])
        ps_b = [ps(f"ps_b{i}", [P, BLK]) for i in range(2)]
        ps_y = ps("ps_y", [P, C, BLK])
        ps_v = ps("ps_v", [P, 2, BLK])
        loads, presets, b_ready, xm_done = sem("loads"), sem("presets"), sem("b_ready"), sem("xm_done")
        xm_read, y_ready, mean_ready, var_ready = sem("xm_read"), sem("y_ready"), sem("mean_ready"), sem("var_ready")
        sq_done, sd_done, vstep, o_done, stored = sem("sq_done"), sem("sd_done"), sem("vstep"), sem("o_done"), sem("stored")
        seen = sem("seen")
        block = st.block()
        per_block = 4 * C + 1

        @block.sync
        def _(sp):
            sp.sem_inc(stored, 1)
            sp.dma_start(cols[:], a["l3_cols2"]).then_inc(loads, 16)
            with sp.Fori(0, NBLK) as q:
                sp.wait_ge(o_done, q * C + C + 1)
                sp.dma_start(out[:, :, bass.ds(q * BLK, BLK)], o[:]).then_inc(stored, 16)
            sp.wait_ge(stored, 16 * NBLK + 1)

        @block.gpsimd
        def _(pool):
            pool.memset(sel[:], 0.0).then_inc(presets, 1)
            pool.wait_ge(presets, 1)
            pool.affine_select(out=sel[:], in_=sel[:], compare_op=ALU.not_equal, fill=1.0, base=0,
                               pattern=[[-1, E3], [0, P]], channel_multiplier=1).then_inc(presets, 1)
            pool.wait_ge(presets, 2)

        @block.tensor
        def _(pe):
            pe.sem_inc(var_ready, 1)
            pe.sem_inc(xm_read, 1)
            def spread(q, e):
                pe.wait_ge(xm_done, q * E3 + e + 1)
                pe.sem_inc(seen, 1)
                pe.matmul(ps_b[e % 2][:], sel[:, e, :], g.weight8[:, bass.ds(q * BLK, BLK)],
                          start=True, stop=True).then_inc(b_ready, 1)

            pe.wait_ge(presets, 2)
            with pe.Fori(0, NBLK) as q:
                spread(q, 0)
                pe.wait_ge(vstep, q * per_block + 1)
                for e in range(E3):
                    if e + 1 < E3:
                        spread(q, e + 1)
                    pe.wait_ge(xm_done, q * E3 + e + 3)
                    for m in range(C):
                        for c in range(C):
                            mm = pe.matmul(ps_y[:, m, :], g.w12[:, e, c, m * P:(m + 1) * P], xm[e % 2][:, c, :],
                                           start=(e == 0 and c == 0), stop=False)
                    mm.then_inc(xm_read, 1)
                for m in range(C):
                    mm = pe.matmul(ps_y[:, m, :], g.c12[:, m * P:(m + 1) * P], g.weight8[:, bass.ds(q * BLK, BLK)],
                                   start=False, stop=True)
                mm.then_inc(y_ready, 1)
                pe.wait_ge(vstep, q * per_block + C + 1)
                for c in range(C):
                    mm = pe.matmul(ps_v[:, 0, :], g.mean_w[:], r[:, c, :], start=(c == 0), stop=(c == C - 1))
                mm.then_inc(mean_ready, 1)
                pe.wait_ge(sq_done, q * C + C)
                for c in range(C):
                    mm = pe.matmul(ps_v[:, 1, :], g.mean_w[:], sq[:, c, :], start=(c == 0), stop=(c == C - 1))
                mm.then_inc(var_ready, 1)

        @block.scalar
        def _(act):
            act.wait_ge(loads, 16)
            with act.Fori(0, NBLK) as q:
                act.wait_ge(var_ready, q + 1)
                for c in range(C):
                    act.wait_ge(vstep, q * per_block + C + c + 2)
                    act.activation(sq[:, c, :], r[:, c, :], ACT.Square).then_inc(sq_done, 1)
                act.wait_ge(var_ready, q + 2)
                act.activation(sd[:], ps_v[:, 1, :], ACT.Sqrt, bias=g.eps[:, 1:2]).then_inc(sd_done, 1)

        @block.vector
        def _(dve):
            dve.sem_inc(o_done, 1)
            dve.sem_inc(vstep, 1)
            dve.sem_inc(xm_done, 2)
            dve.wait_ge(loads, 16)
            with dve.Fori(0, NBLK) as q:
                for e in range(E3):
                    dve.wait_ge(b_ready, q * E3 + e + 1)
                    if e < 2:
                        dve.wait_ge(xm_read, q * E3 + 1)
                    else:
                        dve.wait_ge(xm_read, q * E3 + e)
                    dve.tensor_tensor(xm[e % 2][:], ps_b[e % 2][:].unsqueeze(1).to_broadcast([P, C, BLK]),
                                      g.y[:, :, bass.ds(q * BLK, BLK)], ALU.mult).then_inc(xm_done, 1)
                s = Steps(vstep, q * per_block + 1)
                dve.wait_ge(y_ready, q + 1)
                dve.wait_ge(o_done, q * C + 1)
                for c in range(C):
                    s.did(dve.tensor_tensor(r[:, c, :], ps_y[:, c, :], g.y[:, c, bass.ds(q * BLK, BLK)], ALU.add))
                dve.wait_ge(mean_ready, q + 1)
                for c in range(C):
                    s.did(dve.tensor_tensor(r[:, c, :], r[:, c, :], ps_v[:, 0, :], ALU.subtract))
                dve.wait_ge(sd_done, q + 1)
                s.did(dve.reciprocal(sd[:], sd[:]))
                for c in range(C):
                    s.did(dve.tensor_scalar(r[:, c, :], r[:, c, :], cols[:, c:c + 1], None, ALU.mult))
                s.settle(dve)
                for c in range(C):
                    s.did(dve.tensor_tensor(r[:, c, :], r[:, c, :], sd[:], ALU.mult))
                s.settle(dve)
                assert s.n == per_block
                dve.wait_ge(stored, q * 16 + 1)
                for c in range(C):
                    dve.scalar_tensor_tensor(out=o[:, c, :], in0=r[:, c, :], scalar=cols[:, C + c:C + c + 1],
                                             in1=g.x[:, c, bass.ds(q * BLK, BLK)], op0=ALU.add, op1=ALU.add).then_inc(o_done, 1)


class Held:
    pass


def program(nc, a, out):
    g = Held()
    with ExitStack() as ctx:
        g.x = ctx.enter_context(nc.sbuf_tensor("all_x", [P, C, T], F32))
        g.cond_all = ctx.enter_context(nc.sbuf_tensor("all_cond_all", [P, B * E8], F32))
        g.best = ctx.enter_context(nc.sbuf_tensor("all_best", [1, B * 8], U32))
        g.pair_idx = ctx.enter_context(nc.sbuf_tensor("all_pair_idx", [1, B * 8], U32))
        g.pair_w = ctx.enter_context(nc.sbuf_tensor("all_pair_w", [P, 2 * B], F32))
        g.ident = ctx.enter_context(nc.sbuf_tensor("all_ident", [P, P], F32))
        g.mean_w = ctx.enter_context(nc.sbuf_tensor("all_mean_w", [P, P], F32))
        g.eps = ctx.enter_context(nc.sbuf_tensor("all_eps", [P, 2], F32))
        g.iota_a = ctx.enter_context(nc.sbuf_tensor("all_iota_a", [P, P], F32))
        g.iota_b = ctx.enter_context(nc.sbuf_tensor("all_iota_b", [P, 64], F32))
        setup(nc, a, g)
        with ExitStack() as layer:
            g.xn = layer.enter_context(nc.sbuf_tensor("layer0_xn", [P, C, T], F32))
            g.code_a = layer.enter_context(nc.sbuf_tensor("layer0_code_a", [P, T // 2], F32))
            g.code_b = layer.enter_context(nc.sbuf_tensor("layer0_code_b", [P, T // 2], F32))
            g.weight = layer.enter_context(nc.sbuf_tensor("layer0_weight", [P, T // 2], F32))
            with ExitStack() as keys:
                g.key_map = keys.enter_context(nc.sbuf_tensor("layer0_key_map", [P, C, NG * NKEYS], F32))
                keys_fold(nc, a, g)
                route(nc, a, g)
            peer(nc, a, g)
        lora(nc, a, g)
        with ExitStack() as layer:
            g.y = layer.enter_context(nc.sbuf_tensor("layer2_y", [P, C, T], F32))
            g.qw = layer.enter_context(nc.sbuf_tensor("layer2_qw", [P, 3 * NQW], F32))
            skills(nc, a, g)
            weights4(nc, a, g)
            quant_ffn(nc, a, g)
        with ExitStack() as layer:
            g.y = layer.enter_context(nc.sbuf_tensor("layer3_y", [P, C, T], F32))
            g.b_bot = layer.enter_context(nc.sbuf_tensor("layer3_b_bot", [P, C], F32))
            g.logit = layer.enter_context(nc.sbuf_tensor("layer3_logit", [P, NT, E3], F32))
            with ExitStack() as attention:
                g.o = attention.enter_context(nc.sbuf_tensor("layer3_o", [P, C, T], F32))
                attend(nc, a, g)
                norm(nc, a, g)
            g.w12 = layer.enter_context(nc.sbuf_tensor("layer3_w12", [P, E3, C, D], F32))
            g.c12 = layer.enter_context(nc.sbuf_tensor("layer3_c12", [E3, D], F32))
            g.weight8 = layer.enter_context(nc.sbuf_tensor("layer3_weight8", [E3, T], F32))
            experts(nc, a, g)
            gates(nc, a, g)
            moe(nc, a, g, out)


def columns(v):
    return v.reshape(v.shape[:-1] + (-1, P)).swapaxes(-1, -2)


def rows(w):
    return w.reshape(w.shape[:-2] + (-1, P, w.shape[-1])).swapaxes(-3, -2)


def lay_out(np, z):
    def turn(name):
        return z[name].swapaxes(-1, -2)

    def flat(w, keep):
        return w.reshape(w.shape[:keep] + (-1,))

    def by_row_of_experts(w):
        return w.reshape(NKEYS, NKEYS // 2, 2, D).transpose(1, 2, 0, 3).reshape(NEXP, D)

    return {
        "x": rows(z["x"].reshape(T, D).T),
        "cond": z["cond_8"],
        "cond0": np.concatenate(
            [flat(rows(turn("L0_cond_W_" + k)), 2) for k in ("up", "gate", "down")]
            + [columns(z["L0_cond_b_" + k]) for k in ("up", "gate", "down")], axis=-1),
        "norm_w": columns(z["L0_ffn_norm_w"]),
        "wq": rows(z["L0_ffn_w_q"]),
        "keys": z["L0_ffn_keys"].transpose(3, 0, 2, 1).reshape(P, NG, NKEYS),
        "down": rows(by_row_of_experts(z["L0_ffn_expert_down"]).T),
        "up": rows(by_row_of_experts(z["L0_ffn_expert_up"])),
        "l1_a": z["L1_cond_As"].reshape(P, D),
        "l1_b": z["L1_cond_Bs"].transpose(0, 2, 1).reshape(P, D),
        "l1_w": np.repeat(z["cond_8"], R1, axis=1).T,
        "l1_wbase": rows(turn("L1_cond_W_base")),
        "l1_cols": np.concatenate([columns(z["L1_cond_b_base"]), columns(z["L1_ffn_base_b"])], axis=-1),
        "l1_basew": rows(turn("L1_ffn_base_W")),
        "l1_ra": rows(np.concatenate([z["L1_ffn_routed_A"].reshape(E1 * R1, D), z["L1_ffn_shared_A"]]).T),
        "l1_rb": np.concatenate([z["L1_ffn_routed_B"].transpose(0, 2, 1).reshape(E1 * R1, D), turn("L1_ffn_shared_B")]),
        "l1_rw": rows(turn("L1_ffn_router_W")),
        "l1_rbias": z["L1_ffn_router_b"],
        "skills": np.concatenate([flat(rows(z["L2_cond_skill_" + k]), 2) for k in ("gate", "up", "down")], axis=-1),
        "skill_shared": np.concatenate([flat(rows(z["L2_cond_shared_" + k]), 1) for k in ("gate", "up", "down")], axis=-1),
        "q_w": np.concatenate([flat(rows(z["L2_ffn_" + k]), 1) for k in ("w_up", "w_gate", "w_down")], axis=-1),
        "l3_w": rows(turn("L3_cond_weight")).swapaxes(0, 1).reshape(P, E3, C * D),
        "l3_mask": flat(rows(turn("L3_cond_mask")), 1),
        "l3_win": rows(turn("L3_ffn_in_proj_w")),
        "l3_bin": columns(z["L3_ffn_in_proj_b"]),
        "l3_bbot": columns(z["L3_cond_bias"]),
        "l3_wout": rows(turn("L3_ffn_out_proj_w")),
        "l3_wg": rows(z["L3_ffn_wg"]),
        "l3_cols": np.concatenate([columns(z["L3_ffn_" + k]) for k in ("out_proj_b", "ln1_g", "ln1_b")], axis=-1),
        "l3_cols2": np.concatenate([columns(z["L3_ffn_" + k]) for k in ("ln2_g", "ln2_b")], axis=-1),
        "l3_w1": rows(turn("L3_ffn_w1")),
        "l3_w2": rows(z["L3_ffn_w2"]),
        "l3_b1": flat(rows(z["L3_ffn_b1"].T), 1),
        "l3_b2": rows(z["L3_ffn_b2"].T),
    }


def kernel(**inputs):
    import numpy as np
    import concourse.bacc as bacc
    from concourse.bass_utils import run_bass_kernel_spmd

    laid = lay_out(np, {name: np.asarray(v) for name, v in inputs.items()})
    arrays = {f"in_{name}": np.ascontiguousarray(v) for name, v in laid.items()}
    nc = bacc.Bacc("TRN2", target_bir_lowering=False, num_devices=1)
    a = {name: nc.dram_tensor(f"in_{name}", v.shape, F32, kind="ExternalInput").ap() for name, v in laid.items()}
    out = nc.dram_tensor("out", (P, C, T), F32, kind="ExternalOutput").ap()
    program(nc, a, out)
    result = run_bass_kernel_spmd(nc, [arrays], core_ids=[0])
    return result.results[0]["out"].transpose(2, 1, 0).reshape(B, S, D)
```

```python
from contextlib import ExitStack

import concourse.bass as bass
from concourse import mybir

F32 = mybir.dt.float32
U32 = mybir.dt.uint32
ALU = mybir.AluOpType
ACT = mybir.ActivationFunctionType
AX_X = mybir.AxisListType.X

P = 128
B, S, D = 2, 1024, 256
T = B * S
C = D // P
BLK = 512
NBLK = T // BLK
BPB = S // BLK
E8 = 8

H0 = 512
M0 = H0 // P
HEADS, DK, TOPK, NKEYS = 8, 128, 8, 64
NEXP = NKEYS * NKEYS
NG = 2 * HEADS
SLOTS = HEADS * TOPK
TPB = BLK // P
NJ = NEXP // P
COND0 = 2 * C * H0 + M0 * D
COND0_BIAS = 2 * M0 + C

R1 = 16
E1 = 6
R1ALL = (E1 + 1) * R1
I2 = 1024
M2 = I2 // P
Q2 = 768
MQ = Q2 // P
QB = 32
ROUND = 12582912.0
HD = 64
E3 = 8
FF = 1024
CAP = T // E3


class Steps:

    def __init__(self, sem, base=0):
        self.sem, self.base, self.n = sem, base, 0

    def did(self, instruction):
        instruction.then_inc(self.sem, 1)
        self.n += 1

    def settle(self, engine):
        engine.wait_ge(self.sem, self.base + self.n)


class Stage:

    def __init__(self, nc, name):
        self.nc, self.name, self.ctx = nc, name, ExitStack()

    def __enter__(self):
        self.ctx.__enter__()
        return self

    def __exit__(self, *e):
        return self.ctx.__exit__(*e)

    def sb(self, name, shape, dt=F32):
        return self.ctx.enter_context(self.nc.sbuf_tensor(f"{self.name}_{name}", shape, dt))

    def ps(self, name, shape):
        return self.ctx.enter_context(self.nc.psum_tensor(f"{self.name}_{name}", shape, F32))

    def sem(self, name):
        return self.ctx.enter_context(self.nc.semaphore(f"{self.name}_{name}"))

    def block(self):
        return self.ctx.enter_context(self.nc.Block())


def setup(nc, a, g):
    with Stage(nc, "setup") as st:
        sb, sem = st.sb, st.sem
        cond_row = sb("cond_row", [1, B * E8])
        top = sb("top", [1, B * 8])
        neg_max = sb("neg_max", [1, B])
        shifted = sb("shifted", [1, B * E8])
        ex = sb("ex", [1, B * E8])
        total = sb("total", [1, B])
        prob = sb("prob", [1, B * E8])
        ptop = sb("ptop", [1, B * 8])
        two = sb("two", [1, B])
        wpair = sb("wpair", [1, 2 * B])
        wlarge = sb("wlarge", [1, 2 * B])
        ones_row = sb("ones_row", [1, P])
        ps_pair = st.ps("ps_pair", [P, 2 * B])
        loads = sem("loads")
        ident_step = sem("ident_step")
        consts = sem("consts")
        d = sem("dve_step")
        exp_done = sem("exp_done")
        pair_ready = sem("pair_ready")
        pair_spread = sem("pair_spread")
        block = st.block()

        @block.sync
        def _(sp):
            sp.dma_start(cond_row[:], a["cond"].rearrange("b e -> (b e)").rearrange("(o n) -> o n", o=1)).then_inc(loads, 16)
            sp.dma_start(g.cond_all[:], a["cond"].rearrange("b e -> (b e)").partition_broadcast(P)).then_inc(loads, 16)

        @block.gpsimd
        def _(pool):
            pool.memset(g.ident[:], 0.0).then_inc(ident_step, 1)
            pool.wait_ge(ident_step, 1)
            pool.affine_select(out=g.ident[:], in_=g.ident[:], compare_op=ALU.not_equal, fill=1.0, base=0,
                               pattern=[[-1, P]], channel_multiplier=1).then_inc(ident_step, 1)
            for t, v in ((g.mean_w[:], 1.0 / D), (g.eps[:, 0:1], 1e-6), (g.eps[:, 1:2], 1e-5)):
                pool.memset(t, v).then_inc(consts, 1)
            pool.iota(g.iota_a[:], pattern=[[1, P]], base=0, channel_multiplier=0,
                      allow_small_or_imprecise_dtypes=True).then_inc(consts, 1)
            pool.wait_ge(consts, 4)
            for half in range(2):
                pool.iota(g.iota_b[64 * half:64 * half + 64, :], pattern=[[1, 64]], base=-32 * half,
                          channel_multiplier=0, allow_small_or_imprecise_dtypes=True).then_inc(consts, 1)
                pool.wait_ge(consts, 5 + half)

        @block.vector
        def _(dve):
            s = Steps(d)
            s.did(dve.memset(ones_row[:], 1.0))
            dve.wait_ge(loads, 32)
            for b in range(B):
                e = slice(8 * b, 8 * b + 8)
                s.did(dve.max(top[:, e], cond_row[:, e]))
            s.settle(dve)
            for b in range(B):
                e = slice(8 * b, 8 * b + 8)
                s.did(dve.max_index(g.best[:, e], top[:, e], cond_row[:, e]))
                s.did(dve.tensor_scalar(shifted[:, e], cond_row[:, e], top[:, 8 * b:8 * b + 1], None, ALU.subtract))
            assert s.n == 7
            dve.wait_ge(exp_done, B)
            for b in range(B):
                s.did(dve.reciprocal(two[:, b:b + 1], total[:, b:b + 1]))
            s.settle(dve)
            for b in range(B):
                e = slice(8 * b, 8 * b + 8)
                s.did(dve.tensor_scalar(prob[:, e], ex[:, e], two[:, b:b + 1], None, ALU.mult))
            s.settle(dve)
            for b in range(B):
                e = slice(8 * b, 8 * b + 8)
                s.did(dve.max(ptop[:, e], prob[:, e]))
            s.settle(dve)
            for b in range(B):
                e = slice(8 * b, 8 * b + 8)
                s.did(dve.max_index(g.pair_idx[:, e], ptop[:, e], prob[:, e]))
                s.did(dve.tensor_tensor(total[:, b:b + 1], ptop[:, 8 * b:8 * b + 1], ptop[:, 8 * b + 1:8 * b + 2], ALU.add))
            s.settle(dve)
            for b in range(B):
                s.did(dve.reciprocal(two[:, b:b + 1], total[:, b:b + 1]))
            s.settle(dve)
            for b in range(B):
                s.did(dve.tensor_scalar(wpair[:, 2 * b:2 * b + 2], ptop[:, 8 * b:8 * b + 2], two[:, b:b + 1], None, ALU.mult))
            s.settle(dve)
            s.did(dve.tensor_scalar(wlarge[:], wpair[:], 1.0 - 1.0 / 12, None, ALU.mult))
            s.settle(dve)
            dve.scalar_tensor_tensor(out=wpair[:], in0=wpair[:], scalar=1.0 / 12, in1=wlarge[:],
                                     op0=ALU.mult, op1=ALU.add).then_inc(pair_ready, 1)
            dve.wait_ge(pair_spread, 1)
            dve.tensor_copy(g.pair_w[:], ps_pair[:]).then_inc(pair_ready, 1)
            dve.wait_ge(pair_ready, 2)

        @block.scalar
        def _(act):
            act.wait_ge(d, 7)
            for b in range(B):
                e = slice(8 * b, 8 * b + 8)
                act.activation(ex[:, e], shifted[:, e], ACT.Exp, accum_out=total[:, b:b + 1]).then_inc(exp_done, 1)

        @block.tensor
        def _(pe):
            pe.wait_ge(pair_ready, 1)
            pe.matmul(ps_pair[:], ones_row[:], wpair[:], start=True, stop=True).then_inc(pair_spread, 1)


def keys_fold(nc, a, g):
    with Stage(nc, "fold") as st:
        wq = st.sb("wq", [P, NG, D])
        kt = st.sb("kt", [P, NG, NKEYS])
        ps = st.ps("ps", [P, C, NG * NKEYS])
        loads, folded, copied = st.sem("loads"), st.sem("folded"), st.sem("copied")
        block = st.block()

        @block.sync
        def _(sp):
            sp.dma_start(wq[:], a["wq"]).then_inc(loads, 16)
            sp.dma_start(kt[:], a["keys"]).then_inc(loads, 16)

        @block.tensor
        def _(pe):
            pe.wait_ge(loads, 32)
            for c in range(C):
                for q in range(NG):
                    mm = pe.matmul(ps[:, c, q * NKEYS:(q + 1) * NKEYS], wq[:, q, c * P:(c + 1) * P], kt[:, q, :],
                                   start=(q % 8 == 0), stop=True, skip_group_check=True)
                mm.then_inc(folded, 1)

        @block.vector
        def _(dve):
            for c in range(C):
                dve.wait_ge(folded, c + 1)
                dve.tensor_copy(g.key_map[:, c, :], ps[:, c, :]).then_inc(copied, 1)
            dve.wait_ge(copied, C)


def swiglu(nc, a, g):
    with Stage(nc, "swiglu") as st:
        sb, ps, sem = st.sb, st.ps, st.sem
        x = sb("x", [P, C, T])
        w = sb("w", [P, COND0 + COND0_BIAS])
        w_up = w[:, 0:C * H0].rearrange("p (c h) -> p c h", c=C)
        w_gate = w[:, C * H0:2 * C * H0].rearrange("p (c h) -> p c h", c=C)
        w_down = w[:, 2 * C * H0:COND0].rearrange("p (k d) -> p k d", k=M0)
        b_up = w[:, COND0:COND0 + M0]
        b_gate = w[:, COND0 + M0:COND0 + 2 * M0]
        b_down = w[:, COND0 + 2 * M0:COND0 + 2 * M0 + C]
        norm_w = sb("norm_w", [P, C])
        su = sb("su", [P, M0, BLK])
        hid = sb("hid", [P, M0, BLK])
        xc = sb("xc", [P, C, BLK])
        sq = sb("sq", [P, C, BLK])
        ms = sb("ms", [P, BLK])
        rms = sb("rms", [P, BLK])
        ps_u = [ps(f"ps_u{i}", [P, BLK]) for i in range(2)]
        ps_g = [ps(f"ps_g{i}", [P, BLK]) for i in range(2)]
        ps_d = ps("ps_d", [P, C, BLK])
        ps_v = ps("ps_v", [P, BLK])
        wload, nload, xload = sem("wload"), sem("nload"), sem("xload")
        up_ready, gate_ready, su_done, hid_done = sem("up_ready"), sem("gate_ready"), sem("su_done"), sem("hid_done")
        down_ready, xc_done, sq_done = sem("down_ready"), sem("xc_done"), sem("sq_done")
        ms_ready, ms_done, rms_done, xn_done = sem("ms_ready"), sem("ms_done"), sem("rms_done"), sem("xn_done")
        block = st.block()

        @block.sync
        def _(sp):
            sp.dma_start(norm_w[:], a["norm_w"]).then_inc(nload, 16)
            sp.dma_start(x[:], a["x"]).then_inc(xload, 16)
            with sp.Fori(0, B) as b:
                e = sp.value_load(g.best[0:1, bass.ds(b * 8, 1)], min_val=0, max_val=E8 - 1)
                sp.wait_ge(xc_done, b * (BPB * C) + 1)
                sp.dma_start(w[:], a["cond0"][bass.ds(e, 1), :, :].rearrange("a p n -> p (a n)")).then_inc(wload, 16)

        @block.tensor
        def _(pe):
            pe.sem_inc(down_ready, 1)
            pe.wait_ge(xload, 16)
            with pe.Fori(0, B) as b:
                pe.wait_ge(wload, b * 16 + 16)
                for k in range(BPB):
                    q = b * BPB + k
                    for m in range(M0):
                        for weight, bank, free, ready in ((w_up, ps_u, su_done, up_ready), (w_gate, ps_g, hid_done, gate_ready)):
                            pe.wait_ge(free, q * M0 + m + 1)
                            for c in range(C):
                                mm = pe.matmul(bank[m % 2][:], weight[:, c, m * P:(m + 1) * P], x[:, c, bass.ds(q * BLK, BLK)],
                                               start=(c == 0), stop=(c == C - 1))
                            mm.then_inc(ready, 1)
                    pe.wait_ge(hid_done, q * M0 + M0 + 2)
                    pe.wait_ge(xc_done, q * C + 1)
                    for c in range(C):
                        for m in range(M0):
                            mm = pe.matmul(ps_d[:, c, :], w_down[:, m, c * P:(c + 1) * P], hid[:, m, :],
                                           start=(m == 0), stop=(m == M0 - 1))
                        mm.then_inc(down_ready, 1)
                    pe.wait_ge(ms_done, q + 1)
                    pe.wait_ge(sq_done, q * C + C)
                    for c in range(C):
                        mm = pe.matmul(ps_v[:], g.mean_w[:], sq[:, c, :], start=(c == 0), stop=(c == C - 1))
                    mm.then_inc(ms_ready, 1)

        @block.scalar
        def _(act):
            act.sem_inc(su_done, 2)
            act.sem_inc(ms_done, 1)
            act.sem_inc(xc_done, 1)
            with act.Fori(0, B) as b:
                act.wait_ge(wload, b * 16 + 16)
                for k in range(BPB):
                    q = b * BPB + k
                    act.wait_ge(hid_done, q * M0 + 2)
                    for m in range(M0):
                        act.wait_ge(up_ready, q * M0 + m + 1)
                        act.activation(su[:, m, :], ps_u[m % 2][:], ACT.Silu, bias=b_up[:, m:m + 1]).then_inc(su_done, 1)
                    act.wait_ge(xn_done, q * C + 1)
                    for c in range(C):
                        act.wait_ge(down_ready, q * C + c + 2)
                        act.activation(xc[:, c, :], ps_d[:, c, :], ACT.Identity, bias=b_down[:, c:c + 1]).then_inc(xc_done, 1)
                        act.wait_ge(xc_done, q * C + c + 2)
                        act.activation(sq[:, c, :], xc[:, c, :], ACT.Square).then_inc(sq_done, 1)
                    act.wait_ge(ms_ready, q + 1)
                    act.activation(ms[:], ps_v[:], ACT.Sqrt, bias=g.eps[:, 0:1]).then_inc(ms_done, 1)

        @block.vector
        def _(dve):
            dve.sem_inc(hid_done, 2)
            dve.sem_inc(xn_done, 1)
            dve.wait_ge(nload, 16)
            with dve.Fori(0, B) as b:
                dve.wait_ge(wload, b * 16 + 16)
                for k in range(BPB):
                    q = b * BPB + k
                    dve.wait_ge(down_ready, q * C + 1)
                    for m in range(M0):
                        dve.wait_ge(su_done, q * M0 + m + 3)
                        dve.wait_ge(gate_ready, q * M0 + m + 1)
                        dve.scalar_tensor_tensor(out=hid[:, m, :], in0=ps_g[m % 2][:], scalar=b_gate[:, m:m + 1], in1=su[:, m, :],
                                                 op0=ALU.add, op1=ALU.mult).then_inc(hid_done, 1)
                    dve.wait_ge(ms_done, q + 2)
                    dve.reciprocal(rms[:], ms[:]).then_inc(rms_done, 1)
                    dve.wait_ge(rms_done, q + 1)
                    for c in range(C):
                        dve.scalar_tensor_tensor(out=g.x[:, c, bass.ds(q * BLK, BLK)], in0=xc[:, c, :], scalar=norm_w[:, c:c + 1],
                                                 in1=rms[:], op0=ALU.mult, op1=ALU.mult).then_inc(xn_done, 1)
            dve.wait_ge(xn_done, NBLK * C + 1)


PB = 256
NPB = T // PB
PT = PB // P
PAIRS = 8
CHUNKS = PB // 2 // PAIRS
CPT = CHUNKS // PT
RING = 4
NGRP = NJ // 2


def peer(nc, a, g):
    with Stage(nc, "peer") as st:
        sb, ps, sem = st.sb, st.ps, st.sem
        down = sb("down", [P, C, NEXP])
        up = sb("up", [P, NJ, D])
        hg = [sb(f"hg{i}", [P, NJ, PB]) for i in range(2)]
        am = [sb(f"am{i}", [P, PAIRS, P]) for i in range(RING)]
        bm = [sb(f"bm{i}", [P, PAIRS, 64]) for i in range(RING)]
        xin = [sb(f"xin{i}", [P, C, PB]) for i in range(2)]
        xt = sb("xt", [P, C, PB])
        slots = [sb(f"slots{i}", [P, 3, PB // 2]) for i in range(2)]
        s8 = sb("s8", [P, NG, 8])
        i8 = sb("i8", [P, NG, 8], U32)
        i8f = sb("i8f", [P, NG, 8])
        sums = sb("sums", [P, HEADS, 8, 8])
        f8 = sb("f8", [P, SLOTS])
        p8 = sb("p8", [P, SLOTS], U32)
        rank = sb("rank", [P, 2, SLOTS], U32)
        rankf = sb("rankf", [P, 2, SLOTS])
        oneh = sb("oneh", [P, SLOTS, 8])
        ij = sb("ij", [P, 2, SLOTS])
        ju = sb("ju", [P, SLOTS], U32)
        jb = sb("jb", [P, 2, SLOTS], U32)
        jf = sb("jf", [P, 2, SLOTS])
        codes = sb("codes", [P, 3, SLOTS])
        ps_h = [ps(f"ps_h{i}", [P, 2, PB]) for i in range(2)]
        ps_w = [ps(f"ps_w{i}", [P, PAIRS, 64]) for i in range(2)]
        ps_o = ps("ps_o", [P, C, PB])
        ps_s = ps("ps_s", [P, 2, BLK])
        ps_t = ps("ps_t", [P, BLK])
        loads, uload, xload = sem("loads"), sem("uload"), [sem(f"xload{i}") for i in range(2)]
        xt_done, sim_ready, sim_read, vstep, seen = sem("xt_done"), sem("sim_ready"), sem("sim_read"), sem("vstep"), sem("seen")
        codes_done, turned, kept = sem("codes_done"), sem("turned"), sem("kept")
        h_ready, gelu_done = sem("h_ready"), sem("gelu_done")
        a_done, beq_done, b_done = sem("a_done"), sem("beq_done"), sem("b_done")
        w_ready, p_done, o_ready, x_done = sem("w_ready"), sem("p_done"), sem("o_ready"), sem("x_done")
        block = st.block()
        per_tile = NG + 1 + 2 * HEADS + 3 + 1 + 2 * 3 + 1 + 2 + 1 + 2

        @block.sync
        def _(sp):
            def load_x(i, k):
                sp.dma_start(xin[k][:], a["x"][:, :, bass.ds(i * PB, PB)]).then_inc(xload[k], 16)

            sp.dma_start(down[:], a["down"]).then_inc(loads, 16)
            sp.dma_start(up[:], a["up"]).then_inc(uload, 16)
            for k in range(2):
                load_x(k, k)
            with sp.Fori(1, NPB // 2) as r:
                for k in range(2):
                    sp.wait_ge(x_done, r * 2 + k - 1)
                    load_x(r * 2 + k, k)

        @block.tensor
        def _(pe):
            def scores(i, t):
                n = i * PT + t
                if t == 0:
                    pe.wait_ge(xt_done, i + 1)
                pe.wait_ge(sim_read, n)
                for h in range(2):
                    for c in range(C):
                        mm = pe.matmul(ps_s[:, h, :], xt[:, c, t * P:(t + 1) * P],
                                       g.key_map[:, c, h * BLK:(h + 1) * BLK], start=(c == 0), stop=(c == C - 1))
                mm.then_inc(sim_ready, 1)

            def turn(i, t):
                n = i * PT + t
                pe.wait_ge(codes_done, n + 1)
                pe.wait_ge(kept, n * 6)
                flat = codes[:].rearrange("p a k -> p (a k)")
                pe.transpose(ps_t[:, 0:P], flat[:, 0:P], g.ident[:])
                pe.transpose(ps_t[0:SLOTS, P:2 * P], flat[:, P:P + SLOTS], g.ident[:]).then_inc(turned, 1)

            def act_rows(i, group):
                n = i * NGRP + group
                pe.wait_ge(gelu_done, n)
                for r in range(2):
                    j = 2 * group + r
                    for c in range(C):
                        mm = pe.matmul(ps_h[group % 2][:, r, :], down[:, c, j * P:(j + 1) * P],
                                       g.x[:, c, bass.ds(i * PB, PB)], start=(c == 0), stop=(c == C - 1))
                mm.then_inc(h_ready, 1)

            def weigh(i, c):
                n = i * CHUNKS + c
                pe.wait_ge(a_done, n + 1)
                pe.wait_ge(b_done, n + 1)
                pe.wait_ge(p_done, n)
                for m in range(PAIRS):
                    mm = pe.matmul(ps_w[c % 2][:, m, :], am[c % RING][:, m, :], bm[c % RING][:, m, :], start=True, stop=True)
                mm.then_inc(w_ready, 1)

            def work(i, half, more):
                for c in range(CHUNKS):
                    weigh(i, c)
                    if more:
                        if c % CPT == 0:
                            scores(i + 1, c // CPT)
                        act_rows(i + 1, c)
                        if c == CPT + 1:
                            turn(i + 1, 0)
                pe.wait_ge(p_done, i * CHUNKS + CHUNKS + 1)
                pe.wait_ge(x_done, i)
                for c in range(C):
                    for j in range(NJ):
                        mm = pe.matmul(ps_o[:, c, :], up[:, j, c * P:(c + 1) * P], hg[half][:, j, :],
                                       start=(j == 0), stop=(j == NJ - 1))
                    if more and c == 0:
                        turn(i + 1, 1)
                mm.then_inc(o_ready, 1)

            scores(0, 0)
            pe.wait_ge(loads, 16)
            for group in range(NGRP):
                act_rows(0, group)
                if group == 3:
                    scores(0, 1)
                if group == 5:
                    turn(0, 0)
            turn(0, 1)
            pe.wait_ge(uload, 16)
            work(0, 0, True)
            with pe.Fori(0, NPB // 2 - 1) as r:
                work(r * 2 + 1, 1, True)
                work(r * 2 + 2, 0, True)
            work(NPB - 1, 1, False)

        @block.scalar
        def _(act):
            def stage_x(i):
                act.activation(xt[:], g.x[:, :, bass.ds(i * PB, PB)], ACT.Copy).then_inc(xt_done, 1)

            def gelu(i, half, group):
                act.wait_ge(h_ready, i * NGRP + group + 1)
                act.activation(hg[half][:, 2 * group:2 * group + 2, :], ps_h[group % 2][:], ACT.Gelu).then_inc(gelu_done, 1)

            def keep(i, half, t):
                act.wait_ge(turned, i * PT + t + 1)
                for z in range(2):
                    r, f, col = slice(64 * z, 64 * z + 64), 64 * z, slice(64 * t, 64 * t + 64)
                    act.activation(slots[half][r, 0, col], ps_t[0:64, f:f + 64], ACT.Copy).then_inc(kept, 1)
                    act.activation(slots[half][r, 1, col], ps_t[64:128, f:f + 64], ACT.Copy).then_inc(kept, 1)
                    act.activation(slots[half][r, 2, col], ps_t[0:64, P + f:P + f + 64], ACT.Copy).then_inc(kept, 1)

            def ahead(i, half):
                act.wait_ge(sim_ready, i * PT)
                stage_x(i)
                act.wait_ge(o_ready, i - 1)
                for group in range(NGRP):
                    gelu(i, half, group)
                    if group == CPT + 1:
                        act.wait_ge(a_done, (i - 1) * CHUNKS)
                        act.wait_ge(b_done, (i - 1) * CHUNKS)
                        keep(i, half, 0)
                keep(i, half, 1)

            act.sem_inc(gelu_done, 1)
            stage_x(0)
            for group in range(NGRP):
                gelu(0, 0, group)
                if group == 5:
                    keep(0, 0, 0)
            keep(0, 0, 1)
            ahead(1, 1)
            with act.Fori(0, NPB // 2 - 1) as r:
                ahead(r * 2 + 2, 0)
                ahead(r * 2 + 3, 1)

        @block.gpsimd
        def _(pool):
            def weights(n, c, half):
                pool.wait_ge(beq_done, n + 1)
                pool.tensor_tensor(bm[c % RING][:], bm[c % RING][:],
                                   slots[half][:, 2, c * PAIRS:(c + 1) * PAIRS].unsqueeze(2).to_broadcast([P, PAIRS, 64]),
                                   ALU.mult).then_inc(b_done, 1)

            with pool.Fori(0, NPB // 2) as r:
                for half in range(2):
                    for c in range(CHUNKS):
                        weights((r * 2 + half) * CHUNKS + c, c, half)

        @block.vector
        def _(dve):
            def pick(i, t):
                n = i * PT + t
                s = Steps(vstep, n * per_tile)
                groups = [ps_s[:, j // 8, (j % 8) * NKEYS:(j % 8 + 1) * NKEYS] for j in range(NG)]
                pair = s8[:].rearrange("p (h two) k -> p h two k", two=2)
                cand = sums[:].rearrange("p h a b -> p h (a b)")
                dve.wait_ge(sim_ready, n + 1)
                dve.sem_inc(seen, 1)
                for j in range(NG // 2):
                    s.did(dve.max(s8[:, j, :], groups[j]))
                yield
                for j in range(NG // 2, NG):
                    s.did(dve.max(s8[:, j, :], groups[j]))
                yield
                s.settle(dve)
                dve.sem_inc(seen, 1)
                for j in range(NG // 2):
                    dve.max_index(i8[:, j, :], s8[:, j, :], groups[j])
                yield
                for j in range(NG // 2, NG - 1):
                    dve.max_index(i8[:, j, :], s8[:, j, :], groups[j])
                dve.max_index(i8[:, NG - 1, :], s8[:, NG - 1, :], groups[NG - 1]).then_inc(sim_read, 1)
                s.did(dve.tensor_tensor(sums[:], pair[:, :, 0, :].unsqueeze(3).to_broadcast([P, HEADS, 8, 8]),
                                        pair[:, :, 1, :].unsqueeze(2).to_broadcast([P, HEADS, 8, 8]), ALU.add))
                yield
                s.settle(dve)
                dve.sem_inc(seen, 1)
                for h in range(HEADS):
                    s.did(dve.max(f8[:, h * 8:h * 8 + 8], cand[:, h, :]))
                yield
                s.settle(dve)
                dve.sem_inc(seen, 1)
                for h in range(HEADS):
                    s.did(dve.max_index(p8[:, h * 8:h * 8 + 8], f8[:, h * 8:h * 8 + 8], cand[:, h, :]))
                s.settle(dve)
                s.did(dve.tensor_copy(i8f[:], i8[:]))
                s.did(dve.tensor_scalar(rank[:, 0, :], p8[:], 3, None, ALU.logical_shift_right))
                s.did(dve.tensor_scalar(rank[:, 1, :], p8[:], 7, None, ALU.bitwise_and))
                s.settle(dve)
                s.did(dve.tensor_copy(rankf[:], rank[:]))
                yield
                ids = i8f[:].rearrange("p (h two) k -> p h two k", two=2)
                for z in range(2):
                    s.settle(dve)
                    s.did(dve.tensor_tensor(oneh[:], rankf[:, z, :].unsqueeze(2).to_broadcast([P, SLOTS, 8]),
                                            g.iota_a[:, 0:8].unsqueeze(1).to_broadcast([P, SLOTS, 8]), ALU.is_equal))
                    s.settle(dve)
                    o = oneh[:].rearrange("p (h k) a -> p h k a", h=HEADS)
                    s.did(dve.tensor_tensor(o, o, ids[:, :, z, :].unsqueeze(2).to_broadcast([P, HEADS, 8, 8]), ALU.mult))
                    s.settle(dve)
                    s.did(dve.tensor_reduce(ij[:, z, :], oneh[:], AX_X, ALU.add))
                    if z == 0:
                        yield
                s.settle(dve)
                s.did(dve.tensor_copy(ju[:], ij[:, 1, :]))
                s.settle(dve)
                s.did(dve.tensor_scalar(jb[:, 0, :], ju[:], 1, None, ALU.bitwise_and))
                s.did(dve.tensor_scalar(jb[:, 1, :], ju[:], 1, None, ALU.logical_shift_right))
                s.settle(dve)
                s.did(dve.tensor_copy(jf[:], jb[:]))
                s.settle(dve)
                dve.wait_ge(turned, n)
                s.did(dve.tensor_copy(codes[:, 1, :], jf[:, 1, :]))
                s.did(dve.tensor_scalar(codes[:, 2, :], f8[:], 0.0, None, ALU.max))
                dve.scalar_tensor_tensor(out=codes[:, 0, :], in0=jf[:, 0, :], scalar=64.0, in1=ij[:, 0, :],
                                         op0=ALU.mult, op1=ALU.add).then_inc(codes_done, 1)
                dve.wait_ge(codes_done, n + 1)
                assert s.n == per_tile, s.n
                yield

            def build(i, c, half):
                if c % CPT == 0:
                    dve.wait_ge(kept, (i * PT + c // CPT + 1) * 6)
                col = slice(c * PAIRS, (c + 1) * PAIRS)
                dve.tensor_tensor(bm[c % RING][:], g.iota_b[:].unsqueeze(1).to_broadcast([P, PAIRS, 64]),
                                  slots[half][:, 1, col].unsqueeze(2).to_broadcast([P, PAIRS, 64]), ALU.is_equal).then_inc(beq_done, 1)
                dve.tensor_tensor(am[c % RING][:], g.iota_a[:].unsqueeze(1).to_broadcast([P, PAIRS, P]),
                                  slots[half][:, 0, col].unsqueeze(2).to_broadcast([P, PAIRS, P]), ALU.is_equal).then_inc(a_done, 1)

            def add_out(i, half, n_load):
                dve.wait_ge(xload[half], n_load * 16 + 16)
                dve.wait_ge(o_ready, i + 1)
                dve.tensor_tensor(g.x[:, :, bass.ds(i * PB, PB)], ps_o[:], xin[half][:], ALU.add).then_inc(x_done, 1)

            def work(i, half, r, first=False, last=False):
                for c in range(CHUNKS):
                    n = i * CHUNKS + c
                    at = c + RING - 1
                    if not (last and at >= CHUNKS):
                        dve.wait_ge(w_ready, n)
                        build(i + at // CHUNKS, at % CHUNKS, (half + at // CHUNKS) % 2)
                    if c == 0 and not first:
                        add_out(i - 1, 1 - half, r)
                    if not last:
                        if c % CPT == 0:
                            parts = pick(i + 1, c // CPT)
                        next(parts)
                    if c == 0:
                        dve.wait_ge(gelu_done, i * NGRP + NGRP + 1)
                    dve.wait_ge(w_ready, n + 1)
                    t0 = c // CPT * P + c % CPT * PAIRS
                    h = hg[half][:].rearrange("p j (z m) -> p z j m", z=PT * 2)
                    z0, m0 = 2 * (c // CPT), c % CPT * PAIRS
                    acts = h[:, z0:z0 + 2, :, m0:m0 + PAIRS]
                    dve.tensor_tensor(acts, ps_w[c % 2][:].rearrange("p m (z j) -> p z j m", z=2), acts, ALU.mult).then_inc(p_done, 1)

            dve.sem_inc(p_done, 1)
            for t in range(PT):
                for _ in pick(0, t):
                    pass
            for c in range(RING - 1):
                build(0, c, 0)
            work(0, 0, 0, first=True)
            with dve.Fori(0, NPB // 2 - 1) as r:
                work(r * 2 + 1, 1, r)
                work(r * 2 + 2, 0, r)
            work(NPB - 1, 1, NPB // 2 - 1, last=True)
            add_out(NPB - 1, 1, NPB // 2 - 1)
            dve.wait_ge(x_done, NPB)


def lora(nc, a, g):
    with Stage(nc, "lora") as st:
        sb, ps, sem = st.sb, st.ps, st.sem
        a_rows = sb("a_rows", [P, D])
        b_rows = sb("b_rows", [P, D])
        w_rep = sb("w_rep", [P, B])
        b_scaled = sb("b_scaled", [P, D])
        w_base = sb("w_base", [P, C, D])
        w_eff = sb("w_eff", [P, C, D])
        cols = sb("cols", [P, 2 * C])
        base_w = sb("base_w", [P, C, D])
        ra = sb("ra", [P, C, R1ALL])
        rb = sb("rb", [R1ALL, D])
        rw = sb("rw", [P, C, E1])
        rbias = sb("rbias", [P, E1])
        xl = sb("xl", [P, C, BLK])
        logit = sb("logit", [P, TPB, E1])
        peak = sb("peak", [P, TPB])
        ex = sb("ex", [P, TPB, E1])
        gate = sb("gate", [P, TPB, 8])
        g8 = sb("g8", [P, TPB, 8])
        gi = sb("gi", [P, TPB, 8], U32)
        gif = sb("gif", [P, TPB, 8])
        hot = sb("hot", [P, 2, TPB, E1])
        sparse = sb("sparse", [P, TPB, E1])
        total = sb("total", [P, TPB])
        inv = sb("inv", [P, TPB])
        wide = sb("wide", [P, TPB, R1ALL])
        hs = sb("hs", [R1ALL, BLK])
        hw = sb("hw", [R1ALL, BLK])
        ps_a = ps("ps_a", [P, C, BLK])
        ps_l = ps("ps_l", [P, TPB, 8])
        ps_h = ps("ps_h", [P, BLK])
        ps_w = ps("ps_w", [P, BLK])
        ps_o = ps("ps_o", [P, C, BLK])
        loads, presets = sem("loads"), sem("presets")
        scaled, fold_ready, w_done = sem("scaled"), sem("fold_ready"), sem("w_done")
        xl_ready, xl_done, l_ready, ex_done = sem("xl_ready"), sem("xl_done"), sem("l_ready"), sem("ex_done")
        h_ready, hs_done, vstep, seen = sem("h_ready"), sem("hs_done"), sem("vstep"), sem("seen")
        wide_done, w_ready, hw_done, o_ready, x_done = sem("wide_done"), sem("w_ready"), sem("hw_done"), sem("o_ready"), sem("x_done")
        block = st.block()
        names = ["l1_a", "l1_b", "l1_w", "l1_wbase", "l1_cols", "l1_basew", "l1_ra", "l1_rb", "l1_rw"]
        bufs = [a_rows, b_rows, w_rep, w_base, cols, base_w, ra, rb, rw]
        n_loads = 16 * (len(names) + 1)
        per_block = 3 + 3 + 2 * TPB + 1 + 2 + 2 + 4

        @block.sync
        def _(sp):
            for name, buf in zip(names, bufs):
                sp.dma_start(buf[:], a[name]).then_inc(loads, 16)
            sp.dma_start(rbias[:], a["l1_rbias"].partition_broadcast(P)).then_inc(loads, 16)

        @block.gpsimd
        def _(pool):
            pool.memset(gate[:], -1.0).then_inc(presets, 1)
            pool.memset(wide[:], 1.0).then_inc(presets, 1)
            pool.wait_ge(presets, 2)

        @block.tensor
        def _(pe):
            pe.sem_inc(fold_ready, 1)
            pe.sem_inc(o_ready, 1)
            pe.wait_ge(loads, n_loads)
            with pe.Fori(0, B) as b:
                pe.wait_ge(scaled, b + 1)
                pe.wait_ge(xl_done, b * (BPB * C) + 1)
                for c in range(C):
                    mm = pe.matmul(ps_a[:, c, 0:D], a_rows[:, c * P:(c + 1) * P], b_scaled[:], start=True, stop=True)
                mm.then_inc(fold_ready, 1)
                pe.wait_ge(w_done, b + 1)
                for k in range(BPB):
                    q = b * BPB + k
                    pe.wait_ge(xl_done, q * C + 1)
                    for m in range(C):
                        for c in range(C):
                            mm = pe.matmul(ps_a[:, m, :], w_eff[:, c, m * P:(m + 1) * P], g.x[:, c, bass.ds(q * BLK, BLK)],
                                           start=(c == 0), stop=(c == C - 1))
                        mm.then_inc(xl_ready, 1)
                    pe.wait_ge(xl_done, q * C + C + 1)
                    pe.wait_ge(x_done, q * C + 1)
                    for t in range(TPB):
                        for c in range(C):
                            mm = pe.matmul(ps_l[:, t, 0:E1], xl[:, c, t * P:(t + 1) * P], rw[:, c, :],
                                           start=(c == 0), stop=(c == C - 1))
                    mm.then_inc(l_ready, 1)
                    for c in range(C):
                        mm = pe.matmul(ps_h[0:R1ALL, :], ra[:, c, :], xl[:, c, :], start=(c == 0), stop=(c == C - 1))
                    mm.then_inc(h_ready, 1)
                    for m in range(C):
                        for c in range(C):
                            pe.matmul(ps_o[:, m, :], base_w[:, c, m * P:(m + 1) * P], xl[:, c, :], start=(c == 0), stop=False)
                    pe.wait_ge(wide_done, q + 1)
                    for t in range(TPB):
                        mm = pe.matmul(ps_w[0:R1ALL, t * P:(t + 1) * P], wide[:, t, :], g.ident[:], start=True, stop=True)
                    mm.then_inc(w_ready, 1)
                    pe.wait_ge(hw_done, q + 1)
                    for m in range(C):
                        mm = pe.matmul(ps_o[:, m, :], rb[:, m * P:(m + 1) * P], hw[:], start=False, stop=True)
                    mm.then_inc(o_ready, 1)

        @block.scalar
        def _(act):
            act.sem_inc(xl_done, 1)
            act.wait_ge(loads, n_loads)
            with act.Fori(0, NBLK) as q:
                act.wait_ge(o_ready, q + 1)
                for m in range(C):
                    act.wait_ge(xl_ready, q * C + m + 1)
                    act.activation(xl[:, m, :], ps_a[:, m, :], ACT.Identity, bias=cols[:, m:m + 1]).then_inc(xl_done, 1)
                act.wait_ge(h_ready, q + 1)
                act.activation(hs[:], ps_h[0:R1ALL, :], ACT.Copy).then_inc(hs_done, 1)
                act.wait_ge(vstep, q * per_block + 3)
                act.activation(ex[:], logit[:], ACT.Exp).then_inc(ex_done, 1)

        @block.vector
        def _(dve):
            dve.sem_inc(x_done, 1)
            dve.wait_ge(presets, 2)
            dve.wait_ge(loads, n_loads)
            with dve.Fori(0, B) as b:
                dve.wait_ge(fold_ready, b + 1)
                dve.tensor_scalar(b_scaled[:], b_rows[:], w_rep[:, bass.ds(b, 1)], 2.0, ALU.mult, ALU.mult).then_inc(scaled, 1)
                dve.wait_ge(fold_ready, b + 2)
                dve.tensor_tensor(w_eff[:], ps_a[:, :, 0:D], w_base[:], ALU.add).then_inc(w_done, 1)
                for k in range(BPB):
                    q = b * BPB + k
                    s = Steps(vstep, q * per_block)
                    dve.wait_ge(l_ready, q + 1)
                    s.did(dve.tensor_tensor(logit[:], ps_l[:, :, 0:E1], rbias[:].unsqueeze(1).to_broadcast([P, TPB, E1]), ALU.add))
                    s.settle(dve)
                    s.did(dve.tensor_reduce(peak[:], logit[:], AX_X, ALU.max))
                    s.settle(dve)
                    s.did(dve.tensor_tensor(logit[:], logit[:], peak[:].unsqueeze(2).to_broadcast([P, TPB, E1]), ALU.subtract))
                    dve.wait_ge(ex_done, q + 1)
                    s.did(dve.tensor_reduce(total[:], ex[:], AX_X, ALU.add))
                    s.settle(dve)
                    s.did(dve.reciprocal(inv[:], total[:]))
                    s.settle(dve)
                    s.did(dve.tensor_tensor(gate[:, :, 0:E1], ex[:], inv[:].unsqueeze(2).to_broadcast([P, TPB, E1]), ALU.mult))
                    s.settle(dve)
                    dve.sem_inc(seen, 1)
                    for t in range(TPB):
                        s.did(dve.max(g8[:, t, :], gate[:, t, :]))
                    s.settle(dve)
                    dve.sem_inc(seen, 1)
                    for t in range(TPB):
                        s.did(dve.max_index(gi[:, t, :], g8[:, t, :], gate[:, t, :]))
                    s.settle(dve)
                    s.did(dve.tensor_copy(gif[:], gi[:]))
                    s.settle(dve)
                    for z in range(2):
                        s.did(dve.tensor_tensor(hot[:, z, :, :], g.iota_a[:, 0:E1].unsqueeze(1).to_broadcast([P, TPB, E1]),
                                                gif[:, :, z:z + 1].to_broadcast([P, TPB, E1]), ALU.is_equal))
                    s.settle(dve)
                    s.did(dve.tensor_tensor(sparse[:], hot[:, 0, :, :], hot[:, 1, :, :], ALU.add))
                    s.settle(dve)
                    s.did(dve.tensor_tensor(sparse[:], sparse[:], gate[:, :, 0:E1], ALU.mult))
                    s.settle(dve)
                    s.did(dve.tensor_reduce(total[:], sparse[:], AX_X, ALU.add))
                    s.settle(dve)
                    s.did(dve.tensor_scalar(total[:], total[:], 1e-6, None, ALU.add))
                    s.settle(dve)
                    s.did(dve.reciprocal(inv[:], total[:]))
                    s.settle(dve)
                    s.did(dve.tensor_tensor(sparse[:], sparse[:], inv[:].unsqueeze(2).to_broadcast([P, TPB, E1]), ALU.mult))
                    s.settle(dve)
                    assert s.n == per_block, s.n
                    dve.tensor_copy(wide[:, :, 0:E1 * R1].rearrange("p t (e r) -> p t e r", r=R1),
                                    sparse[:].unsqueeze(3).to_broadcast([P, TPB, E1, R1])).then_inc(wide_done, 1)
                    dve.wait_ge(w_ready, q + 1)
                    dve.wait_ge(hs_done, q + 1)
                    dve.tensor_tensor(hw[:], ps_w[0:R1ALL, :], hs[:], ALU.mult).then_inc(hw_done, 1)
                    dve.wait_ge(o_ready, q + 2)
                    for m in range(C):
                        xs = g.x[:, m, bass.ds(q * BLK, BLK)]
                        dve.scalar_tensor_tensor(out=xs, in0=ps_o[:, m, :], scalar=cols[:, C + m:C + m + 1], in1=xs,
                                                 op0=ALU.add, op1=ALU.add).then_inc(x_done, 1)
            dve.wait_ge(x_done, NBLK * C + 1)


def skills(nc, a, g):
    with Stage(nc, "skills") as st:
        sb, ps, sem = st.sb, st.ps, st.sem
        nw = 2 * C * I2 + M2 * D
        w = [sb(f"w{i}", [P, nw]) for i in range(3)]
        w_gate = [x[:, 0:C * I2].rearrange("p (c i) -> p c i", c=C) for x in w]
        w_up = [x[:, C * I2:2 * C * I2].rearrange("p (c i) -> p c i", c=C) for x in w]
        w_down = [x[:, 2 * C * I2:nw].rearrange("p (m d) -> p m d", m=M2) for x in w]
        act_g = [sb(f"act_g{i}", [P, BLK]) for i in range(2)]
        hid = [sb(f"hid{i}", [P, BLK]) for i in range(4)]
        ps_g = [ps(f"ps_g{i}", [P, BLK]) for i in range(2)]
        ps_u = [ps(f"ps_u{i}", [P, BLK]) for i in range(2)]
        acc = [[ps(f"acc{k}{c}", [P, BLK]) for c in range(C)] for k in range(BPB)]
        wload = [sem(f"wload{i}") for i in range(3)]
        g_ready, u_ready, gelu_done, hid_done = sem("g_ready"), sem("u_ready"), sem("gelu_done"), sem("hid_done")
        d_ready, y_done = sem("d_ready"), sem("y_done")
        block = st.block()
        plan = [(s, k, m) for s in range(3) for k in range(BPB) for m in range(M2)]
        n_b = len(plan)

        @block.sync
        def _(sp):
            with sp.Fori(0, B) as b:
                for s in range(2):
                    e = sp.value_load(g.pair_idx[0:1, bass.ds(b * 8 + s, 1)], min_val=0, max_val=E8 - 1)
                    sp.wait_ge(d_ready, b * n_b + 1)
                    sp.dma_start(w[s][:], a["skills"][bass.ds(e, 1), :, :].rearrange("a p n -> p (a n)")).then_inc(wload[s], 16)
                sp.dma_start(w[2][:], a["skill_shared"]).then_inc(wload[2], 16)

        @block.tensor
        def _(pe):
            pe.sem_inc(d_ready, 1)
            def down(b, j):
                s, k, m = plan[j]
                n = b * n_b + j
                pe.wait_ge(hid_done, n + 3)
                if j == 0:
                    pe.wait_ge(y_done, b * (BPB * C) + 1)
                for c in range(C):
                    mm = pe.matmul(acc[k][c][:], w_down[s][:, m, c * P:(c + 1) * P], hid[j % 4][:],
                                   start=(s == 0 and m == 0), stop=(s == 2 and m == M2 - 1))
                mm.then_inc(d_ready, 1)

            with pe.Fori(0, B) as b:
                for j, (s, k, m) in enumerate(plan):
                    n = b * n_b + j
                    if k == 0 and m == 0:
                        pe.wait_ge(wload[s], b * 16 + 16)
                    for weight, bank, free, ready in ((w_gate[s], ps_g[j % 2], gelu_done, g_ready),
                                                      (w_up[s], ps_u[j % 2], hid_done, u_ready)):
                        pe.wait_ge(free, n + 1)
                        for c in range(C):
                            mm = pe.matmul(bank[:], weight[:, c, m * P:(m + 1) * P],
                                           g.x[:, c, bass.ds((b * BPB + k) * BLK, BLK)], start=(c == 0), stop=(c == C - 1))
                        mm.then_inc(ready, 1)
                    if j:
                        down(b, j - 1)
                down(b, n_b - 1)

        @block.scalar
        def _(act):
            act.sem_inc(gelu_done, 2)
            act.sem_inc(y_done, 1)
            with act.Fori(0, B) as b:
                for j in range(n_b):
                    n = b * n_b + j
                    act.wait_ge(g_ready, n + 1)
                    act.wait_ge(hid_done, n + 1)
                    act.activation(act_g[j % 2][:], ps_g[j % 2][:], ACT.Gelu_apprx_tanh).then_inc(gelu_done, 1)
                act.wait_ge(d_ready, b * n_b + n_b + 1)
                for k in range(BPB):
                    for c in range(C):
                        act.activation(g.y[:, c, bass.ds((b * BPB + k) * BLK, BLK)], acc[k][c][:], ACT.Copy).then_inc(y_done, 1)
            act.wait_ge(y_done, NBLK * C + 1)

        @block.vector
        def _(dve):
            dve.sem_inc(hid_done, 2)
            with dve.Fori(0, B) as b:
                for j, (s, k, m) in enumerate(plan):
                    n = b * n_b + j
                    dve.wait_ge(gelu_done, n + 3)
                    dve.wait_ge(u_ready, n + 1)
                    if j >= 4:
                        dve.wait_ge(d_ready, n - 3 + 1)
                    else:
                        dve.wait_ge(d_ready, b * n_b + 1)
                    scale = g.pair_w[:, bass.ds(b * 2 + s, 1)] if s < 2 else 1.0
                    dve.scalar_tensor_tensor(out=hid[j % 4][:], in0=ps_u[j % 2][:], scalar=scale, in1=act_g[j % 2][:],
                                             op0=ALU.mult, op1=ALU.mult).then_inc(hid_done, 1)


NQW = C * Q2
NQB = 3 * NQW // QB


def weights4(nc, a, g):
    with Stage(nc, "weights4") as st:
        sb, ps, sem = st.sb, st.ps, st.sem
        w = sb("w", [P, NQB, QB])
        peak = sb("peak", [P, NQB])
        scale = sb("scale", [P, NQB])
        inv = sb("inv", [P, NQB])
        bank = [ps(f"bank{i}", [P, 4, P]) for i in range(2)]
        loads, vstep, turned, kept = sem("loads"), sem("vstep"), sem("turned"), sem("kept")
        block = st.block()
        flat = w[:].rearrange("p n q -> p (n q)")

        @block.sync
        def _(sp):
            sp.dma_start(flat, a["q_w"]).then_inc(loads, 16)

        @block.vector
        def _(dve):
            s = Steps(vstep)
            dve.wait_ge(loads, 16)
            for op in (
                lambda: dve.tensor_reduce(peak[:], w[:], AX_X, ALU.max, apply_absolute_value=True),
                lambda: dve.tensor_scalar(scale[:], peak[:], 1.0 / 7, 1e-12, ALU.mult, ALU.max),
                lambda: dve.reciprocal(inv[:], scale[:]),
                lambda: dve.tensor_tensor(w[:], w[:], inv[:].unsqueeze(2).to_broadcast([P, NQB, QB]), ALU.mult),
                lambda: dve.tensor_scalar(flat, flat, ROUND, ROUND, ALU.add, ALU.subtract),
                lambda: dve.tensor_scalar(flat, flat, -8.0, 7.0, ALU.max, ALU.min),
                lambda: dve.tensor_tensor(w[:], w[:], scale[:].unsqueeze(2).to_broadcast([P, NQB, QB]), ALU.mult),
            ):
                s.did(op())
                s.settle(dve)

        turns = [(flat[:, (z * MQ + m) * D + c * P:(z * MQ + m) * D + (c + 1) * P], z, c, m)
                 for z in range(2) for c in range(C) for m in range(MQ)]
        turns += [(flat[:, 2 * NQW + c * Q2 + m * P:2 * NQW + c * Q2 + (m + 1) * P], 2, m, c)
                  for m in range(MQ) for c in range(C)]

        @block.tensor
        def _(pe):
            pe.wait_ge(vstep, 7)
            for n, (src, *_) in enumerate(turns):
                r = n // 4
                if n % 4 == 0 and r >= 2:
                    pe.wait_ge(kept, r - 1)
                mm = pe.transpose(bank[r % 2][:, n % 4, :], src, g.ident[:])
                if n % 4 == 3:
                    mm.then_inc(turned, 1)

        @block.scalar
        def _(act):
            dst = g.qw[:].rearrange("p (r n) -> p r n", n=4 * P)
            for r in range(len(turns) // 4):
                act.wait_ge(turned, r + 1)
                act.activation(dst[:, r, :], bank[r % 2][:].rearrange("p a b -> p (a b)"), ACT.Copy).then_inc(kept, 1)
            act.wait_ge(kept, len(turns) // 4)


def quant_ffn(nc, a, g):
    with Stage(nc, "quant") as st:
        sb, ps, sem = st.sb, st.ps, st.sem
        wt = [g.qw[:, z * NQW:(z + 1) * NQW].rearrange("p (c i) -> p c i", c=C) for z in range(2)]
        wd = g.qw[:, 2 * NQW:3 * NQW].rearrange("p (m d) -> p m d", m=MQ)
        up = sb("up", [P, MQ, T])
        gate = sb("gate", [P, MQ, T])
        sig = sb("sig", [P, T])
        peaks = sb("peaks", [P, 16])
        top = sb("top", [P, 8])
        alltop = sb("alltop", [P, 8])
        scale = sb("scale", [P, 8])
        inv = sb("inv", [P, 8])
        ps_m = [ps(f"ps_m{i}", [P, BLK]) for i in range(8)]
        vstep, spread, mm_ready, kept = sem("vstep"), sem("spread"), sem("mm_ready"), sem("kept")
        sig_done, sigq_done, x_done, d_ready = sem("sig_done"), sem("sigq_done"), sem("x_done"), sem("d_ready")
        block = st.block()
        marks = {}

        def quant(dve, s, t, n):
            s.did(dve.tensor_scalar(t, t, inv[:, n:n + 1], ROUND, ALU.mult, ALU.add))
            s.settle(dve)
            s.did(dve.tensor_scalar(t, t, ROUND, 32767.0, ALU.subtract, ALU.min))
            s.settle(dve)
            s.did(dve.tensor_scalar(t, t, -32768.0, scale[:, n:n + 1], ALU.max, ALU.mult))

        def scales(dve, s, n, count):
            s.settle(dve)
            s.did(dve.tensor_reduce(top[:, n:n + 1], peaks[:, 0:count], AX_X, ALU.max))
            marks["top", n] = s.n
            dve.wait_ge(spread, n + 1)
            s.did(dve.tensor_scalar(scale[:, n:n + 1], alltop[:, n:n + 1], 1.0 / 32767, 1e-12, ALU.mult, ALU.max))
            s.settle(dve)
            s.did(dve.reciprocal(inv[:, n:n + 1], scale[:, n:n + 1]))
            s.settle(dve)

        def peak(dve, s, t, n):
            s.did(dve.tensor_reduce(peaks[:, n:n + 1], t, AX_X, ALU.max, apply_absolute_value=True))

        @block.vector
        def _(dve):
            s = Steps(vstep)
            for c in range(C):
                peak(dve, s, g.y[:, c, :], c)
            scales(dve, s, 0, C)
            for c in range(C):
                quant(dve, s, g.y[:, c, :], 0)
            marks["x"] = s.n
            for z, t in enumerate((up, gate)):
                for m in range(MQ):
                    dve.wait_ge(kept, NBLK * (z * MQ + m + 1))
                    peak(dve, s, t[:, m, :], m)
                scales(dve, s, 1 + z, MQ)
                for m in range(MQ):
                    quant(dve, s, t[:, m, :], 1 + z)
                    marks[z, m] = s.n
            for m in range(MQ):
                dve.wait_ge(sig_done, m + 1)
                s.did(dve.tensor_scalar(sig[:], sig[:], 65536.0, ROUND, ALU.mult, ALU.add))
                s.settle(dve)
                s.did(dve.tensor_scalar(sig[:], sig[:], ROUND, 65535.0, ALU.subtract, ALU.min))
                s.settle(dve)
                s.did(dve.tensor_scalar(sig[:], sig[:], 0.0, 1.0 / 65536, ALU.max, ALU.mult))
                s.settle(dve)
                dve.tensor_tensor(gate[:, m, :], gate[:, m, :], sig[:], ALU.mult).then_inc(sigq_done, 1)
                dve.wait_ge(sigq_done, m + 1)
                peak(dve, s, gate[:, m, :], m)
            scales(dve, s, 3, MQ)
            for m in range(MQ):
                quant(dve, s, gate[:, m, :], 3)
                s.settle(dve)
                s.did(dve.tensor_tensor(gate[:, m, :], gate[:, m, :], up[:, m, :], ALU.mult))
                s.settle(dve)
                peak(dve, s, gate[:, m, :], m)
            scales(dve, s, 4, MQ)
            for m in range(MQ):
                quant(dve, s, gate[:, m, :], 4)
                marks["o", m] = s.n
            for q in range(NBLK):
                for c in range(C):
                    dve.wait_ge(d_ready, q * C + c + 1)
                    xs = g.x[:, c, q * BLK:(q + 1) * BLK]
                    dve.tensor_tensor(xs, ps_m[(q * C + c) % 8][:], xs, ALU.add).then_inc(x_done, 1)
            dve.wait_ge(x_done, NBLK * C)

        @block.gpsimd
        def _(pool):
            for n in range(5):
                pool.wait_ge(vstep, marks["top", n])
                pool.partition_all_reduce(alltop[:, n:n + 1], top[:, n:n + 1], P, bass.bass_isa.ReduceOp.max).then_inc(spread, 1)
            pool.wait_ge(spread, 5)

        @block.tensor
        def _(pe):
            pe.wait_ge(vstep, marks["x"])
            n = 0
            for z in range(2):
                for m in range(MQ):
                    for q in range(NBLK):
                        if n >= 8:
                            pe.wait_ge(kept, n - 7)
                        for c in range(C):
                            mm = pe.matmul(ps_m[n % 8][:], wt[z][:, c, m * P:(m + 1) * P], g.y[:, c, q * BLK:(q + 1) * BLK],
                                           start=(c == 0), stop=(c == C - 1))
                        mm.then_inc(mm_ready, 1)
                        n += 1
            pe.wait_ge(kept, n)
            for m in range(MQ):
                pe.wait_ge(vstep, marks["o", m])
                for q in range(NBLK):
                    for c in range(C):
                        mm = pe.matmul(ps_m[(q * C + c) % 8][:], wd[:, m, c * P:(c + 1) * P], gate[:, m, q * BLK:(q + 1) * BLK],
                                       start=(m == 0), stop=(m == MQ - 1))
                        if m == MQ - 1:
                            mm.then_inc(d_ready, 1)

        @block.scalar
        def _(act):
            n = 0
            for t in (up, gate):
                for m in range(MQ):
                    for q in range(NBLK):
                        act.wait_ge(mm_ready, n + 1)
                        act.activation(t[:, m, q * BLK:(q + 1) * BLK], ps_m[n % 8][:], ACT.Copy).then_inc(kept, 1)
                        n += 1
            for m in range(MQ):
                act.wait_ge(vstep, marks[1, m])
                act.wait_ge(sigq_done, m)
                act.activation(sig[:], gate[:, m, :], ACT.Sigmoid).then_inc(sig_done, 1)


NQKV = 3 * C
NP3 = S // BLK


def attend(nc, a, g):
    with Stage(nc, "attend") as st:
        sb, ps, sem = st.sb, st.ps, st.sem
        ws = sb("ws", [P, E3, C * D])
        mask = sb("mask", [P, C * D])
        wb = sb("wb", [P, B, C * D])
        w_bot = wb[:].rearrange("p b (c o) -> p b c o", c=C)
        w_in = sb("w_in", [P, C, 3 * D])
        b_in = sb("b_in", [P, NQKV])
        qkv = sb("qkv", [P, NQKV, T])
        heads = sb("heads", [P, P])
        prod = sb("prod", [P, B, B, BLK])
        sc = sb("sc", [P, B, B, BLK])
        peak = sb("peak", [P, B, BLK])
        total = sb("total", [P, B, BLK])
        ps_m = [ps(f"ps_m{i}", [P, BLK]) for i in range(4)]
        ps_s = ps("ps_s", [P, 4, BLK])
        loads, presets, w_step = sem("loads"), sem("presets"), sem("w_step")
        x_ready, x_done, q_ready, q_done = sem("x_ready"), sem("x_done"), sem("q_ready"), sem("q_done")
        vstep, s_ready, sc_done, ex_done = sem("vstep"), sem("s_ready"), sem("sc_done"), sem("ex_done")
        block = st.block()
        names, bufs = ["l3_w", "l3_mask", "l3_win", "l3_bin", "l3_bbot"], [ws, mask, w_in, b_in, g.b_bot]
        per_step = 8

        @block.sync
        def _(sp):
            for name, buf in zip(names, bufs):
                sp.dma_start(buf[:], a[name]).then_inc(loads, 16)

        @block.gpsimd
        def _(pool):
            pool.memset(heads[:], 0.0).then_inc(presets, 1)
            pool.wait_ge(presets, 1)
            for r in (slice(0, HD), slice(HD, P)):
                pool.memset(heads[r, r], 1.0).then_inc(presets, 1)
            pool.wait_ge(presets, 3)

        @block.tensor
        def _(pe):
            pe.sem_inc(s_ready, 1)
            pe.wait_ge(loads, 16 * len(names))
            pe.wait_ge(w_step, B * (E3 + 1))
            for b in range(B):
                for k in range(BPB):
                    for m in range(C):
                        n = (b * BPB + k) * C + m
                        if n >= 4:
                            pe.wait_ge(x_done, n - 3)
                        for c in range(C):
                            mm = pe.matmul(ps_m[n % 4][:], w_bot[:, b, c, m * P:(m + 1) * P],
                                           g.x[:, c, (b * BPB + k) * BLK:(b * BPB + k + 1) * BLK],
                                           start=(c == 0), stop=(c == C - 1))
                        mm.then_inc(x_ready, 1)
            pe.wait_ge(x_done, NBLK * C)
            with pe.Fori(0, NBLK) as q:
                for m in range(NQKV):
                    n = q * NQKV + m
                    pe.wait_ge(q_done, n - min(m, 3) + 1)
                    for c in range(C):
                        mm = pe.matmul(ps_m[m % 4][:], w_in[:, c, m * P:(m + 1) * P], g.y[:, c, bass.ds(q * BLK, BLK)],
                                       start=(c == 0), stop=(c == C - 1))
                    mm.then_inc(q_ready, 1)
            pe.wait_ge(presets, 3)
            with pe.Fori(0, NP3) as r:
                for c in range(C):
                    n = r * C + c
                    pe.wait_ge(vstep, n * per_step + 2)
                    pe.wait_ge(sc_done, n + 1)
                    for z in range(4):
                        mm = pe.matmul(ps_s[:, z, :], heads[:], prod[:, z // B, z % B, :], start=True, stop=True)
                    mm.then_inc(s_ready, 1)

        @block.scalar
        def _(act):
            act.sem_inc(q_done, 1)
            act.sem_inc(sc_done, 1)
            act.wait_ge(loads, 16 * len(names))
            for n in range(NBLK * C):
                q, m = n // C, n % C
                act.wait_ge(x_ready, n + 1)
                act.activation(g.y[:, m, q * BLK:(q + 1) * BLK], ps_m[n % 4][:], ACT.Identity,
                               bias=g.b_bot[:, m:m + 1]).then_inc(x_done, 1)
            with act.Fori(0, NBLK) as q:
                for m in range(NQKV):
                    act.wait_ge(q_ready, q * NQKV + m + 1)
                    act.activation(qkv[:, m, bass.ds(q * BLK, BLK)], ps_m[m % 4][:], ACT.Identity,
                                   bias=b_in[:, m:m + 1]).then_inc(q_done, 1)
            with act.Fori(0, NP3) as r:
                for c in range(C):
                    n = r * C + c
                    act.wait_ge(s_ready, n + 2)
                    act.wait_ge(vstep, n * per_step + 1)
                    act.activation(sc[:].rearrange("p l m t -> p (l m) t"), ps_s[:], ACT.Copy,
                                   scale=1.0 / 8).then_inc(sc_done, 1)
                    act.wait_ge(vstep, n * per_step + 4)
                    act.activation(sc[:], sc[:], ACT.Exp).then_inc(ex_done, 1)

        @block.vector
        def _(dve):
            dve.sem_inc(vstep, 1)
            s = Steps(w_step)
            dve.wait_ge(loads, 16 * len(names))
            for b in range(B):
                for e in range(E3):
                    y = g.cond_all[:, b * E8 + e:b * E8 + e + 1]
                    s.settle(dve)
                    if e == 0:
                        s.did(dve.tensor_scalar(wb[:, b, :], ws[:, 0, :], y, None, ALU.mult))
                    else:
                        s.did(dve.scalar_tensor_tensor(out=wb[:, b, :], in0=ws[:, e, :], scalar=y, in1=wb[:, b, :],
                                                       op0=ALU.mult, op1=ALU.add))
                s.settle(dve)
                s.did(dve.tensor_tensor(wb[:, b, :], wb[:, b, :], mask[:], ALU.mult))
            dve.wait_ge(q_done, NBLK * NQKV + 1)
            with dve.Fori(0, NP3) as r:
                for c in range(C):
                    n = r * C + c
                    s = Steps(vstep, n * per_step + 1)

                    def rows(m):
                        return qkv[:, m, :].rearrange("p (b t) -> p b t", b=B)[:, :, bass.ds(r * BLK, BLK)]

                    dve.wait_ge(s_ready, n + 1)
                    s.did(dve.tensor_tensor(prod[:], rows(c).unsqueeze(2).to_broadcast([P, B, B, BLK]),
                                            rows(C + c).unsqueeze(1).to_broadcast([P, B, B, BLK]), ALU.mult))
                    dve.wait_ge(sc_done, n + 2)
                    s.did(dve.tensor_tensor(peak[:], sc[:, :, 0, :], sc[:, :, 1, :], ALU.max))
                    s.settle(dve)
                    s.did(dve.tensor_tensor(sc[:], sc[:], peak[:].unsqueeze(2).to_broadcast([P, B, B, BLK]), ALU.subtract))
                    dve.wait_ge(ex_done, n + 1)
                    s.did(dve.tensor_tensor(total[:], sc[:, :, 0, :], sc[:, :, 1, :], ALU.add))
                    s.settle(dve)
                    s.did(dve.reciprocal(total[:], total[:]))
                    v = rows(2 * C + c).unsqueeze(1).to_broadcast([P, B, B, BLK])
                    s.did(dve.tensor_tensor(sc[:], sc[:], v, ALU.mult))
                    s.settle(dve)
                    s.did(dve.tensor_tensor(peak[:], sc[:, :, 0, :], sc[:, :, 1, :], ALU.add))
                    s.settle(dve)
                    o = g.o[:, c, :].rearrange("p (b t) -> p b t", b=B)[:, :, bass.ds(r * BLK, BLK)]
                    s.did(dve.tensor_tensor(o, peak[:], total[:], ALU.mult))
                    s.settle(dve)
                    assert s.n == per_step


def norm(nc, a, g):
    with Stage(nc, "norm") as st:
        sb, ps, sem = st.sb, st.ps, st.sem
        w_out = sb("w_out", [P, C, D])
        wg = sb("wg", [P, C, E3])
        cols = sb("cols", [P, 3 * C])
        r = sb("r", [P, C, BLK])
        sq = sb("sq", [P, C, BLK])
        sd = sb("sd", [P, BLK])
        y = sb("y", [P, C, BLK])
        ps_m = ps("ps_m", [P, C, BLK])
        ps_v = ps("ps_v", [P, 2, BLK])
        ps_l = ps("ps_l", [P, TPB, E3])
        loads, m_ready, mean_ready, var_ready = sem("loads"), sem("m_ready"), sem("mean_ready"), sem("var_ready")
        sq_done, sd_done, vstep, y_done, l_ready, l_done, y_kept = (
            sem("sq_done"), sem("sd_done"), sem("vstep"), sem("y_done"), sem("l_ready"), sem("l_done"), sem("y_kept"))
        block = st.block()
        names, bufs = ["l3_wout", "l3_wg", "l3_cols"], [w_out, wg, cols]
        per_block = 4 * C + 1

        @block.sync
        def _(sp):
            for name, buf in zip(names, bufs):
                sp.dma_start(buf[:], a[name]).then_inc(loads, 16)

        @block.tensor
        def _(pe):
            pe.sem_inc(l_ready, 1)
            pe.sem_inc(var_ready, 1)
            pe.wait_ge(loads, 16 * len(names))
            with pe.Fori(0, NBLK) as q:
                pe.wait_ge(vstep, q * per_block + 1)
                for m in range(C):
                    for c in range(C):
                        mm = pe.matmul(ps_m[:, m, :], w_out[:, c, m * P:(m + 1) * P], g.o[:, c, bass.ds(q * BLK, BLK)],
                                       start=(c == 0), stop=(c == C - 1))
                    mm.then_inc(m_ready, 1)
                pe.wait_ge(vstep, q * per_block + C + 1)
                for c in range(C):
                    mm = pe.matmul(ps_v[:, 0, :], g.mean_w[:], r[:, c, :], start=(c == 0), stop=(c == C - 1))
                mm.then_inc(mean_ready, 1)
                pe.wait_ge(sq_done, q * C + C)
                for c in range(C):
                    mm = pe.matmul(ps_v[:, 1, :], g.mean_w[:], sq[:, c, :], start=(c == 0), stop=(c == C - 1))
                mm.then_inc(var_ready, 1)
                pe.wait_ge(y_done, q * C + C + 1)
                pe.wait_ge(l_done, q + 1)
                for t in range(TPB):
                    for c in range(C):
                        mm = pe.matmul(ps_l[:, t, :], y[:, c, t * P:(t + 1) * P], wg[:, c, :], start=(c == 0), stop=(c == C - 1))
                mm.then_inc(l_ready, 1)

        @block.scalar
        def _(act):
            act.sem_inc(l_done, 1)
            act.sem_inc(y_done, 1)
            act.wait_ge(loads, 16 * len(names))
            with act.Fori(0, NBLK) as q:
                act.wait_ge(var_ready, q + 1)
                for c in range(C):
                    act.wait_ge(vstep, q * per_block + C + c + 2)
                    act.activation(sq[:, c, :], r[:, c, :], ACT.Square).then_inc(sq_done, 1)
                act.wait_ge(var_ready, q + 2)
                act.activation(sd[:], ps_v[:, 1, :], ACT.Sqrt, bias=g.eps[:, 1:2]).then_inc(sd_done, 1)
                act.wait_ge(l_ready, q + 1)
                act.wait_ge(y_kept, q + 1)
                for c in range(C):
                    act.wait_ge(vstep, q * per_block + 3 * C + 1 + c + 2)
                    act.activation(y[:, c, :], r[:, c, :], ACT.Identity, bias=cols[:, 2 * C + c:2 * C + c + 1]).then_inc(y_done, 1)
                act.wait_ge(l_ready, q + 2)
                act.activation(g.logit[:, bass.ds(q * TPB, TPB), :], ps_l[:], ACT.Copy).then_inc(l_done, 1)
            act.wait_ge(l_done, NBLK + 1)

        @block.gpsimd
        def _(pool):
            pool.sem_inc(y_kept, 1)
            with pool.Fori(0, NBLK) as q:
                pool.wait_ge(y_done, q * C + C + 1)
                pool.tensor_copy(g.y[:, :, bass.ds(q * BLK, BLK)], y[:]).then_inc(y_kept, 1)
            pool.wait_ge(y_kept, NBLK + 1)

        @block.vector
        def _(dve):
            dve.sem_inc(vstep, 1)
            dve.wait_ge(loads, 16 * len(names))
            with dve.Fori(0, NBLK) as q:
                s = Steps(vstep, q * per_block + 1)
                dve.wait_ge(y_done, q * C + 1)
                for c in range(C):
                    dve.wait_ge(m_ready, q * C + c + 1)
                    s.did(dve.scalar_tensor_tensor(out=r[:, c, :], in0=ps_m[:, c, :], scalar=cols[:, c:c + 1],
                                                   in1=g.y[:, c, bass.ds(q * BLK, BLK)], op0=ALU.add, op1=ALU.add))
                dve.wait_ge(mean_ready, q + 1)
                for c in range(C):
                    s.did(dve.tensor_tensor(r[:, c, :], r[:, c, :], ps_v[:, 0, :], ALU.subtract))
                dve.wait_ge(sd_done, q + 1)
                s.did(dve.reciprocal(sd[:], sd[:]))
                for c in range(C):
                    s.did(dve.tensor_scalar(r[:, c, :], r[:, c, :], cols[:, C + c:C + c + 1], None, ALU.mult))
                s.settle(dve)
                for c in range(C):
                    s.did(dve.tensor_tensor(r[:, c, :], r[:, c, :], sd[:], ALU.mult))
                assert s.n == per_block


NT = T // P


def experts(nc, a, g):
    with Stage(nc, "experts") as st:
        sb, ps, sem = st.sb, st.ps, st.sem
        n_f = FF // P
        w1 = [sb(f"w1{i}", [P, n_f, D]) for i in range(2)]
        w2 = [sb(f"w2{i}", [P, n_f, D]) for i in range(2)]
        b1 = sb("b1", [P, n_f * E3])
        b2 = sb("b2", [P, C, E3])
        bc = sb("bc", [P, C, E3])
        ps_w = [ps(f"ps_w{i}", [P, C, D]) for i in range(2)]
        ps_b = [ps(f"ps_b{i}", [P, E3]) for i in range(C)]
        ps_c = ps("ps_c", [P, D])
        bload, loads = sem("bload"), [sem(f"loads{i}") for i in range(2)]
        folded, kept, turned = sem("folded"), sem("kept"), sem("turned")
        block = st.block()

        @block.sync
        def _(sp):
            sp.dma_start(b1[:], a["l3_b1"]).then_inc(bload, 16)
            sp.dma_start(b2[:], a["l3_b2"]).then_inc(bload, 16)
            for e in range(E3):
                if e >= 2:
                    sp.wait_ge(folded, e - 1)
                sp.dma_start(w1[e % 2][:], a["l3_w1"][e]).then_inc(loads[e % 2], 16)
                sp.dma_start(w2[e % 2][:], a["l3_w2"][e]).then_inc(loads[e % 2], 16)

        @block.tensor
        def _(pe):
            pe.wait_ge(bload, 32)
            for e in range(E3):
                pe.wait_ge(loads[e % 2], 32 * (e // 2 + 1))
                if e >= 2:
                    pe.wait_ge(kept, e - 1)
                for c in range(C):
                    for f in range(n_f):
                        pe.matmul(ps_w[e % 2][:, c, :], w1[e % 2][:, f, c * P:(c + 1) * P], w2[e % 2][:, f, :],
                                  start=(f == 0), stop=(f == n_f - 1))
                for c in range(C):
                    for f in range(n_f):
                        mm = pe.matmul(ps_b[c][:, e:e + 1], w2[e % 2][:, f, c * P:(c + 1) * P],
                                       b1[:, f * E3 + e:f * E3 + e + 1], start=(f == 0), stop=(f == n_f - 1))
                mm.then_inc(folded, 1)
            pe.wait_ge(kept, E3 + C)
            for c in range(C):
                mm = pe.transpose(ps_c[0:E3, c * P:(c + 1) * P], bc[:, c, :], g.ident[:])
            mm.then_inc(turned, 1)

        @block.vector
        def _(dve):
            for e in range(E3):
                dve.wait_ge(folded, e + 1)
                dve.tensor_copy(g.w12[:, e, :, :], ps_w[e % 2][:]).then_inc(kept, 1)
            for c in range(C):
                dve.tensor_tensor(bc[:, c, :], ps_b[c][:], b2[:, c, :], ALU.add).then_inc(kept, 1)
            dve.wait_ge(turned, 1)
            dve.tensor_copy(g.c12[:], ps_c[0:E3, :]).then_inc(kept, 1)
            dve.wait_ge(kept, E3 + C + 1)


def gates(nc, a, g):
    with Stage(nc, "gates") as st:
        sb, ps, sem = st.sb, st.ps, st.sem
        peak = sb("peak", [P, NT])
        total = sb("total", [P, NT])
        ex = sb("ex", [P, NT, E3])
        g8 = sb("g8", [P, NT, 8])
        gi = sb("gi", [P, NT, 8], U32)
        gif = sb("gif", [P, NT, 8])
        hot = sb("hot", [P, NT, E3])
        before = sb("before", [P, NT, E3])
        keep = sb("keep", [P, NT, E3])
        upto = sb("upto", [P, P])
        ones = sb("ones", [P, P])
        ps_c = ps("ps_c", [P, NT, E3])
        ps_n = ps("ps_n", [P, NT, E3])
        ps_t = ps("ps_t", [P, NT * P])
        presets, vstep, ex_done, counted, turned, kept = (
            sem("presets"), sem("vstep"), sem("ex_done"), sem("counted"), sem("turned"), sem("kept"))
        block = st.block()
        marks = {}
        wide = [P, NT, E3]

        @block.gpsimd
        def _(pool):
            pool.memset(ones[:], 1.0).then_inc(presets, 1)
            pool.memset(upto[:], 1.0).then_inc(presets, 1)
            pool.wait_ge(presets, 2)
            pool.affine_select(out=upto[:], in_=upto[:], compare_op=ALU.is_ge, fill=0.0, base=0,
                               pattern=[[1, P]], channel_multiplier=-1).then_inc(presets, 1)
            pool.wait_ge(presets, 3)

        @block.vector
        def _(dve):
            s = Steps(vstep)

            def then(*ops):
                for op in ops:
                    s.did(op)
                s.settle(dve)

            then(dve.tensor_reduce(peak[:], g.logit[:], AX_X, ALU.max))
            then(dve.tensor_tensor(g.logit[:], g.logit[:], peak[:].unsqueeze(2).to_broadcast(wide), ALU.subtract))
            marks["shifted"] = s.n
            dve.wait_ge(ex_done, 1)
            then(dve.tensor_reduce(total[:], ex[:], AX_X, ALU.add))
            then(dve.reciprocal(total[:], total[:]))
            then(dve.tensor_tensor(ex[:], ex[:], total[:].unsqueeze(2).to_broadcast(wide), ALU.mult))
            then(*[dve.max(g8[:, t, :], ex[:, t, :]) for t in range(NT)])
            then(*[dve.max_index(gi[:, t, :], g8[:, t, :], ex[:, t, :]) for t in range(NT)])
            then(dve.tensor_copy(gif[:], gi[:]))
            then(dve.tensor_tensor(hot[:], g.iota_a[:, 0:E3].unsqueeze(1).to_broadcast(wide),
                                   gif[:, :, 0:1].to_broadcast(wide), ALU.is_equal))
            marks["hot"] = s.n
            then(dve.memset(before[:, 0, :], 0.0))
            dve.wait_ge(counted, 2)
            for t in range(1, NT):
                then(dve.tensor_tensor(before[:, t, :], ps_n[:, t - 1, :], before[:, t - 1, :], ALU.add))
            then(dve.tensor_tensor(keep[:], ps_c[:], before[:], ALU.add))
            then(dve.scalar_tensor_tensor(out=hot[:], in0=keep[:], scalar=float(CAP), in1=hot[:],
                                          op0=ALU.is_le, op1=ALU.mult))
            then(dve.tensor_tensor(hot[:], hot[:], g8[:, :, 0:1].to_broadcast(wide), ALU.mult))
            marks["weight"] = s.n
            for b in range(4):
                dve.wait_ge(turned, b + 1)
                dve.tensor_copy(g.weight8[:, b * BLK:(b + 1) * BLK], ps_t[0:E3, b * BLK:(b + 1) * BLK]).then_inc(kept, 1)
            dve.wait_ge(kept, 4)

        @block.scalar
        def _(act):
            act.wait_ge(vstep, marks["shifted"])
            act.activation(ex[:], g.logit[:], ACT.Exp).then_inc(ex_done, 1)

        @block.tensor
        def _(pe):
            pe.wait_ge(presets, 3)
            pe.wait_ge(vstep, marks["hot"])
            flat = hot[:].rearrange("p t e -> p (t e)")
            pe.matmul(ps_c[:].rearrange("p t e -> p (t e)"), upto[:], flat, start=True, stop=True).then_inc(counted, 1)
            pe.matmul(ps_n[:].rearrange("p t e -> p (t e)"), ones[:], flat, start=True, stop=True).then_inc(counted, 1)
            pe.wait_ge(vstep, marks["weight"])
            for t in range(NT):
                mm = pe.transpose(ps_t[0:E3, t * P:(t + 1) * P], hot[:, t, :], g.ident[:])
                if t % 4 == 3:
                    mm.then_inc(turned, 1)


def moe(nc, a, g, out):
    with Stage(nc, "moe") as st:
        sb, ps, sem = st.sb, st.ps, st.sem
        sel = sb("sel", [E3, E3, P])
        cols = sb("cols", [P, 2 * C])
        xm = [sb(f"xm{i}", [P, C, BLK]) for i in range(2)]
        r = sb("r", [P, C, BLK])
        sq = sb("sq", [P, C, BLK])
        sd = sb("sd", [P, BLK])
        o = sb("o", [P, C, BLK])
        ps_b = [ps(f"ps_b{i}", [P, BLK]) for i in range(2)]
        ps_y = ps("ps_y", [P, C, BLK])
        ps_v = ps("ps_v", [P, 2, BLK])
        loads, presets, b_ready, xm_done = sem("loads"), sem("presets"), sem("b_ready"), sem("xm_done")
        xm_read, y_ready, mean_ready, var_ready = sem("xm_read"), sem("y_ready"), sem("mean_ready"), sem("var_ready")
        sq_done, sd_done, vstep, o_done, stored = sem("sq_done"), sem("sd_done"), sem("vstep"), sem("o_done"), sem("stored")
        seen = sem("seen")
        block = st.block()
        per_block = 4 * C + 1

        @block.sync
        def _(sp):
            sp.sem_inc(stored, 1)
            sp.dma_start(cols[:], a["l3_cols2"]).then_inc(loads, 16)
            with sp.Fori(0, NBLK) as q:
                sp.wait_ge(o_done, q * C + C + 1)
                sp.dma_start(out[:, :, bass.ds(q * BLK, BLK)], o[:]).then_inc(stored, 16)
            sp.wait_ge(stored, 16 * NBLK + 1)

        @block.gpsimd
        def _(pool):
            pool.memset(sel[:], 0.0).then_inc(presets, 1)
            pool.wait_ge(presets, 1)
            pool.affine_select(out=sel[:], in_=sel[:], compare_op=ALU.not_equal, fill=1.0, base=0,
                               pattern=[[-1, E3], [0, P]], channel_multiplier=1).then_inc(presets, 1)
            pool.wait_ge(presets, 2)

        @block.tensor
        def _(pe):
            pe.sem_inc(var_ready, 1)
            pe.sem_inc(xm_read, 1)
            def spread(q, e):
                pe.wait_ge(xm_done, q * E3 + e + 1)
                pe.sem_inc(seen, 1)
                pe.matmul(ps_b[e % 2][:], sel[:, e, :], g.weight8[:, bass.ds(q * BLK, BLK)],
                          start=True, stop=True).then_inc(b_ready, 1)

            pe.wait_ge(presets, 2)
            with pe.Fori(0, NBLK) as q:
                spread(q, 0)
                pe.wait_ge(vstep, q * per_block + 1)
                for e in range(E3):
                    if e + 1 < E3:
                        spread(q, e + 1)
                    pe.wait_ge(xm_done, q * E3 + e + 3)
                    for m in range(C):
                        for c in range(C):
                            mm = pe.matmul(ps_y[:, m, :], g.w12[:, e, c, m * P:(m + 1) * P], xm[e % 2][:, c, :],
                                           start=(e == 0 and c == 0), stop=False)
                    mm.then_inc(xm_read, 1)
                for m in range(C):
                    mm = pe.matmul(ps_y[:, m, :], g.c12[:, m * P:(m + 1) * P], g.weight8[:, bass.ds(q * BLK, BLK)],
                                   start=False, stop=True)
                mm.then_inc(y_ready, 1)
                pe.wait_ge(vstep, q * per_block + C + 1)
                for c in range(C):
                    mm = pe.matmul(ps_v[:, 0, :], g.mean_w[:], r[:, c, :], start=(c == 0), stop=(c == C - 1))
                mm.then_inc(mean_ready, 1)
                pe.wait_ge(sq_done, q * C + C)
                for c in range(C):
                    mm = pe.matmul(ps_v[:, 1, :], g.mean_w[:], sq[:, c, :], start=(c == 0), stop=(c == C - 1))
                mm.then_inc(var_ready, 1)

        @block.scalar
        def _(act):
            act.wait_ge(loads, 16)
            with act.Fori(0, NBLK) as q:
                act.wait_ge(var_ready, q + 1)
                for c in range(C):
                    act.wait_ge(vstep, q * per_block + C + c + 2)
                    act.activation(sq[:, c, :], r[:, c, :], ACT.Square).then_inc(sq_done, 1)
                act.wait_ge(var_ready, q + 2)
                act.activation(sd[:], ps_v[:, 1, :], ACT.Sqrt, bias=g.eps[:, 1:2]).then_inc(sd_done, 1)

        @block.vector
        def _(dve):
            dve.sem_inc(o_done, 1)
            dve.sem_inc(vstep, 1)
            dve.sem_inc(xm_done, 2)
            dve.wait_ge(loads, 16)
            with dve.Fori(0, NBLK) as q:
                for e in range(E3):
                    dve.wait_ge(b_ready, q * E3 + e + 1)
                    if e < 2:
                        dve.wait_ge(xm_read, q * E3 + 1)
                    else:
                        dve.wait_ge(xm_read, q * E3 + e)
                    dve.tensor_tensor(xm[e % 2][:], ps_b[e % 2][:].unsqueeze(1).to_broadcast([P, C, BLK]),
                                      g.y[:, :, bass.ds(q * BLK, BLK)], ALU.mult).then_inc(xm_done, 1)
                s = Steps(vstep, q * per_block + 1)
                dve.wait_ge(y_ready, q + 1)
                dve.wait_ge(o_done, q * C + 1)
                for c in range(C):
                    s.did(dve.tensor_tensor(r[:, c, :], ps_y[:, c, :], g.y[:, c, bass.ds(q * BLK, BLK)], ALU.add))
                dve.wait_ge(mean_ready, q + 1)
                for c in range(C):
                    s.did(dve.tensor_tensor(r[:, c, :], r[:, c, :], ps_v[:, 0, :], ALU.subtract))
                dve.wait_ge(sd_done, q + 1)
                s.did(dve.reciprocal(sd[:], sd[:]))
                for c in range(C):
                    s.did(dve.tensor_scalar(r[:, c, :], r[:, c, :], cols[:, c:c + 1], None, ALU.mult))
                s.settle(dve)
                for c in range(C):
                    s.did(dve.tensor_tensor(r[:, c, :], r[:, c, :], sd[:], ALU.mult))
                s.settle(dve)
                assert s.n == per_block
                dve.wait_ge(stored, q * 16 + 1)
                for c in range(C):
                    dve.scalar_tensor_tensor(out=o[:, c, :], in0=r[:, c, :], scalar=cols[:, C + c:C + c + 1],
                                             in1=g.x[:, c, bass.ds(q * BLK, BLK)], op0=ALU.add, op1=ALU.add).then_inc(o_done, 1)


class Held:
    pass


def program(nc, a, out):
    g = Held()
    with ExitStack() as ctx:
        g.x = ctx.enter_context(nc.sbuf_tensor("all_x", [P, C, T], F32))
        g.cond_all = ctx.enter_context(nc.sbuf_tensor("all_cond_all", [P, B * E8], F32))
        g.best = ctx.enter_context(nc.sbuf_tensor("all_best", [1, B * 8], U32))
        g.pair_idx = ctx.enter_context(nc.sbuf_tensor("all_pair_idx", [1, B * 8], U32))
        g.pair_w = ctx.enter_context(nc.sbuf_tensor("all_pair_w", [P, 2 * B], F32))
        g.ident = ctx.enter_context(nc.sbuf_tensor("all_ident", [P, P], F32))
        g.mean_w = ctx.enter_context(nc.sbuf_tensor("all_mean_w", [P, P], F32))
        g.eps = ctx.enter_context(nc.sbuf_tensor("all_eps", [P, 2], F32))
        g.iota_a = ctx.enter_context(nc.sbuf_tensor("all_iota_a", [P, P], F32))
        g.iota_b = ctx.enter_context(nc.sbuf_tensor("all_iota_b", [P, 64], F32))
        setup(nc, a, g)
        with ExitStack() as layer:
            g.key_map = layer.enter_context(nc.sbuf_tensor("layer0_key_map", [P, C, NG * NKEYS], F32))
            keys_fold(nc, a, g)
            swiglu(nc, a, g)
            peer(nc, a, g)
        lora(nc, a, g)
        with ExitStack() as layer:
            g.y = layer.enter_context(nc.sbuf_tensor("layer2_y", [P, C, T], F32))
            g.qw = layer.enter_context(nc.sbuf_tensor("layer2_qw", [P, 3 * NQW], F32))
            skills(nc, a, g)
            weights4(nc, a, g)
            quant_ffn(nc, a, g)
        with ExitStack() as layer:
            g.y = layer.enter_context(nc.sbuf_tensor("layer3_y", [P, C, T], F32))
            g.b_bot = layer.enter_context(nc.sbuf_tensor("layer3_b_bot", [P, C], F32))
            g.logit = layer.enter_context(nc.sbuf_tensor("layer3_logit", [P, NT, E3], F32))
            with ExitStack() as attention:
                g.o = attention.enter_context(nc.sbuf_tensor("layer3_o", [P, C, T], F32))
                attend(nc, a, g)
                norm(nc, a, g)
            g.w12 = layer.enter_context(nc.sbuf_tensor("layer3_w12", [P, E3, C, D], F32))
            g.c12 = layer.enter_context(nc.sbuf_tensor("layer3_c12", [E3, D], F32))
            g.weight8 = layer.enter_context(nc.sbuf_tensor("layer3_weight8", [E3, T], F32))
            experts(nc, a, g)
            gates(nc, a, g)
            moe(nc, a, g, out)


def columns(v):
    return v.reshape(v.shape[:-1] + (-1, P)).swapaxes(-1, -2)


def rows(w):
    return w.reshape(w.shape[:-2] + (-1, P, w.shape[-1])).swapaxes(-3, -2)


def lay_out(np, z):
    def turn(name):
        return z[name].swapaxes(-1, -2)

    def flat(w, keep):
        return w.reshape(w.shape[:keep] + (-1,))

    def by_row_of_experts(w):
        return w.reshape(NKEYS, NKEYS // 2, 2, D).transpose(1, 2, 0, 3).reshape(NEXP, D)

    return {
        "x": rows(z["x"].reshape(T, D).T),
        "cond": z["cond_8"],
        "cond0": np.concatenate(
            [flat(rows(turn("L0_cond_W_" + k)), 2) for k in ("up", "gate", "down")]
            + [columns(z["L0_cond_b_" + k]) for k in ("up", "gate", "down")], axis=-1),
        "norm_w": columns(z["L0_ffn_norm_w"]),
        "wq": rows(z["L0_ffn_w_q"]),
        "keys": z["L0_ffn_keys"].transpose(3, 0, 2, 1).reshape(P, NG, NKEYS),
        "down": rows(by_row_of_experts(z["L0_ffn_expert_down"]).T),
        "up": rows(by_row_of_experts(z["L0_ffn_expert_up"])),
        "l1_a": z["L1_cond_As"].reshape(P, D),
        "l1_b": z["L1_cond_Bs"].transpose(0, 2, 1).reshape(P, D),
        "l1_w": np.repeat(z["cond_8"], R1, axis=1).T,
        "l1_wbase": rows(turn("L1_cond_W_base")),
        "l1_cols": np.concatenate([columns(z["L1_cond_b_base"]), columns(z["L1_ffn_base_b"])], axis=-1),
        "l1_basew": rows(turn("L1_ffn_base_W")),
        "l1_ra": rows(np.concatenate([z["L1_ffn_routed_A"].reshape(E1 * R1, D), z["L1_ffn_shared_A"]]).T),
        "l1_rb": np.concatenate([z["L1_ffn_routed_B"].transpose(0, 2, 1).reshape(E1 * R1, D), turn("L1_ffn_shared_B")]),
        "l1_rw": rows(turn("L1_ffn_router_W")),
        "l1_rbias": z["L1_ffn_router_b"],
        "skills": np.concatenate([flat(rows(z["L2_cond_skill_" + k]), 2) for k in ("gate", "up", "down")], axis=-1),
        "skill_shared": np.concatenate([flat(rows(z["L2_cond_shared_" + k]), 1) for k in ("gate", "up", "down")], axis=-1),
        "q_w": np.concatenate([flat(rows(z["L2_ffn_" + k]), 1) for k in ("w_up", "w_gate", "w_down")], axis=-1),
        "l3_w": rows(turn("L3_cond_weight")).swapaxes(0, 1).reshape(P, E3, C * D),
        "l3_mask": flat(rows(turn("L3_cond_mask")), 1),
        "l3_win": rows(turn("L3_ffn_in_proj_w")),
        "l3_bin": columns(z["L3_ffn_in_proj_b"]),
        "l3_bbot": columns(z["L3_cond_bias"]),
        "l3_wout": rows(turn("L3_ffn_out_proj_w")),
        "l3_wg": rows(z["L3_ffn_wg"]),
        "l3_cols": np.concatenate([columns(z["L3_ffn_" + k]) for k in ("out_proj_b", "ln1_g", "ln1_b")], axis=-1),
        "l3_cols2": np.concatenate([columns(z["L3_ffn_" + k]) for k in ("ln2_g", "ln2_b")], axis=-1),
        "l3_w1": rows(turn("L3_ffn_w1")),
        "l3_w2": rows(z["L3_ffn_w2"]),
        "l3_b1": flat(rows(z["L3_ffn_b1"].T), 1),
        "l3_b2": rows(z["L3_ffn_b2"].T),
    }


def kernel(**inputs):
    import numpy as np
    import concourse.bacc as bacc
    from concourse.bass_utils import run_bass_kernel_spmd

    laid = lay_out(np, {name: np.asarray(v) for name, v in inputs.items()})
    arrays = {f"in_{name}": np.ascontiguousarray(v) for name, v in laid.items()}
    nc = bacc.Bacc("TRN2", target_bir_lowering=False, num_devices=1)
    a = {name: nc.dram_tensor(f"in_{name}", v.shape, F32, kind="ExternalInput").ap() for name, v in laid.items()}
    out = nc.dram_tensor("out", (P, C, T), F32, kind="ExternalOutput").ap()
    program(nc, a, out)
    result = run_bass_kernel_spmd(nc, [arrays], core_ids=[0])
    return result.results[0]["out"].transpose(2, 1, 0).reshape(B, S, D)
```

```python
from contextlib import ExitStack

import concourse.bass as bass
from concourse import mybir

F32 = mybir.dt.float32
U32 = mybir.dt.uint32
ALU = mybir.AluOpType
ACT = mybir.ActivationFunctionType
AX_X = mybir.AxisListType.X

P = 128
B, S, D = 2, 1024, 256
T = B * S
C = D // P
BLK = 512
NBLK = T // BLK
BPB = S // BLK
E8 = 8

H0 = 512
M0 = H0 // P
HEADS, DK, TOPK, NKEYS = 8, 128, 8, 64
NEXP = NKEYS * NKEYS
NG = 2 * HEADS
SLOTS = HEADS * TOPK
TPB = BLK // P
NJ = NEXP // P
COND0 = 2 * C * H0 + M0 * D
COND0_BIAS = 2 * M0 + C

R1 = 16
E1 = 6
R1ALL = (E1 + 1) * R1
I2 = 1024
M2 = I2 // P
SKILL = 2 * C * I2 + M2 * D
Q2 = 768
MQ = Q2 // P
QB = 32
ROUND = 12582912.0
HD = 64
E3 = 8
FF = 1024
CAP = T // E3


class Steps:

    def __init__(self, sem, base=0):
        self.sem, self.base, self.n = sem, base, 0

    def did(self, instruction):
        instruction.then_inc(self.sem, 1)
        self.n += 1

    def settle(self, engine):
        engine.wait_ge(self.sem, self.base + self.n)


class Stage:

    def __init__(self, nc, name):
        self.nc, self.name, self.ctx = nc, name, ExitStack()

    def __enter__(self):
        self.ctx.__enter__()
        return self

    def __exit__(self, *e):
        return self.ctx.__exit__(*e)

    def sb(self, name, shape, dt=F32):
        return self.ctx.enter_context(self.nc.sbuf_tensor(f"{self.name}_{name}", shape, dt))

    def ps(self, name, shape):
        return self.ctx.enter_context(self.nc.psum_tensor(f"{self.name}_{name}", shape, F32))

    def sem(self, name):
        return self.ctx.enter_context(self.nc.semaphore(f"{self.name}_{name}"))

    def block(self):
        return self.ctx.enter_context(self.nc.Block())


def setup(nc, a, g):
    with Stage(nc, "setup") as st:
        sb, sem = st.sb, st.sem
        cond_row = sb("cond_row", [1, B * E8])
        top = sb("top", [1, B * 8])
        neg_max = sb("neg_max", [1, B])
        shifted = sb("shifted", [1, B * E8])
        ex = sb("ex", [1, B * E8])
        total = sb("total", [1, B])
        prob = sb("prob", [1, B * E8])
        ptop = sb("ptop", [1, B * 8])
        two = sb("two", [1, B])
        wpair = sb("wpair", [1, 2 * B])
        wlarge = sb("wlarge", [1, 2 * B])
        ones_row = sb("ones_row", [1, P])
        ps_pair = st.ps("ps_pair", [P, 2 * B])
        loads = sem("loads")
        ident_step = sem("ident_step")
        consts = sem("consts")
        d = sem("dve_step")
        exp_done = sem("exp_done")
        pair_ready = sem("pair_ready")
        pair_spread = sem("pair_spread")
        block = st.block()

        @block.sync
        def _(sp):
            sp.dma_start(cond_row[:], a["cond"].rearrange("b e -> (b e)").rearrange("(o n) -> o n", o=1)).then_inc(loads, 16)
            sp.dma_start(g.cond_all[:], a["cond"].rearrange("b e -> (b e)").partition_broadcast(P)).then_inc(loads, 16)

        @block.gpsimd
        def _(pool):
            pool.memset(g.ident[:], 0.0).then_inc(ident_step, 1)
            pool.wait_ge(ident_step, 1)
            pool.affine_select(out=g.ident[:], in_=g.ident[:], compare_op=ALU.not_equal, fill=1.0, base=0,
                               pattern=[[-1, P]], channel_multiplier=1).then_inc(ident_step, 1)
            for t, v in ((g.mean_w[:], 1.0 / D), (g.eps[:, 0:1], 1e-6), (g.eps[:, 1:2], 1e-5)):
                pool.memset(t, v).then_inc(consts, 1)
            pool.iota(g.iota_a[:], pattern=[[1, P]], base=0, channel_multiplier=0,
                      allow_small_or_imprecise_dtypes=True).then_inc(consts, 1)
            pool.wait_ge(consts, 4)
            for half in range(2):
                pool.iota(g.iota_b[64 * half:64 * half + 64, :], pattern=[[1, 64]], base=-32 * half,
                          channel_multiplier=0, allow_small_or_imprecise_dtypes=True).then_inc(consts, 1)
                pool.wait_ge(consts, 5 + half)

        @block.vector
        def _(dve):
            s = Steps(d)
            s.did(dve.memset(ones_row[:], 1.0))
            dve.wait_ge(loads, 32)
            for b in range(B):
                e = slice(8 * b, 8 * b + 8)
                s.did(dve.max(top[:, e], cond_row[:, e]))
            s.settle(dve)
            for b in range(B):
                e = slice(8 * b, 8 * b + 8)
                s.did(dve.max_index(g.best[:, e], top[:, e], cond_row[:, e]))
                s.did(dve.tensor_scalar(shifted[:, e], cond_row[:, e], top[:, 8 * b:8 * b + 1], None, ALU.subtract))
            assert s.n == 7
            dve.wait_ge(exp_done, B)
            for b in range(B):
                s.did(dve.reciprocal(two[:, b:b + 1], total[:, b:b + 1]))
            s.settle(dve)
            for b in range(B):
                e = slice(8 * b, 8 * b + 8)
                s.did(dve.tensor_scalar(prob[:, e], ex[:, e], two[:, b:b + 1], None, ALU.mult))
            s.settle(dve)
            for b in range(B):
                e = slice(8 * b, 8 * b + 8)
                s.did(dve.max(ptop[:, e], prob[:, e]))
            s.settle(dve)
            for b in range(B):
                e = slice(8 * b, 8 * b + 8)
                s.did(dve.max_index(g.pair_idx[:, e], ptop[:, e], prob[:, e]))
                s.did(dve.tensor_tensor(total[:, b:b + 1], ptop[:, 8 * b:8 * b + 1], ptop[:, 8 * b + 1:8 * b + 2], ALU.add))
            s.settle(dve)
            for b in range(B):
                s.did(dve.reciprocal(two[:, b:b + 1], total[:, b:b + 1]))
            s.settle(dve)
            for b in range(B):
                s.did(dve.tensor_scalar(wpair[:, 2 * b:2 * b + 2], ptop[:, 8 * b:8 * b + 2], two[:, b:b + 1], None, ALU.mult))
            s.settle(dve)
            s.did(dve.tensor_scalar(wlarge[:], wpair[:], 1.0 - 1.0 / 12, None, ALU.mult))
            s.settle(dve)
            dve.scalar_tensor_tensor(out=wpair[:], in0=wpair[:], scalar=1.0 / 12, in1=wlarge[:],
                                     op0=ALU.mult, op1=ALU.add).then_inc(pair_ready, 1)
            dve.wait_ge(pair_spread, 1)
            dve.tensor_copy(g.pair_w[:], ps_pair[:]).then_inc(pair_ready, 1)
            dve.wait_ge(pair_ready, 2)

        @block.scalar
        def _(act):
            act.wait_ge(d, 7)
            for b in range(B):
                e = slice(8 * b, 8 * b + 8)
                act.activation(ex[:, e], shifted[:, e], ACT.Exp, accum_out=total[:, b:b + 1]).then_inc(exp_done, 1)

        @block.tensor
        def _(pe):
            pe.wait_ge(pair_ready, 1)
            pe.matmul(ps_pair[:], ones_row[:], wpair[:], start=True, stop=True).then_inc(pair_spread, 1)


def keys_fold(nc, a, g):
    with Stage(nc, "fold") as st:
        ps = st.ps("ps", [P, C, NG * NKEYS])
        folded, copied = st.sem("folded"), st.sem("copied")
        block = st.block()

        @block.tensor
        def _(pe):
            for c in range(C):
                for q in range(NG):
                    mm = pe.matmul(ps[:, c, q * NKEYS:(q + 1) * NKEYS], g.wq[:, q, c * P:(c + 1) * P], g.keys[:, q, :],
                                   start=(q % 8 == 0), stop=True, skip_group_check=True)
                mm.then_inc(folded, 1)

        @block.vector
        def _(dve):
            for c in range(C):
                dve.wait_ge(folded, c + 1)
                dve.tensor_copy(g.key_map[:, c, :], ps[:, c, :]).then_inc(copied, 1)
            dve.wait_ge(copied, C)


def swiglu(nc, a, g):
    with Stage(nc, "swiglu") as st:
        sb, ps, sem = st.sb, st.ps, st.sem
        x = sb("x", [P, C, T])
        w = sb("w", [P, COND0 + COND0_BIAS])
        w_up = w[:, 0:C * H0].rearrange("p (c h) -> p c h", c=C)
        w_gate = w[:, C * H0:2 * C * H0].rearrange("p (c h) -> p c h", c=C)
        w_down = w[:, 2 * C * H0:COND0].rearrange("p (k d) -> p k d", k=M0)
        b_up = w[:, COND0:COND0 + M0]
        b_gate = w[:, COND0 + M0:COND0 + 2 * M0]
        b_down = w[:, COND0 + 2 * M0:COND0 + 2 * M0 + C]
        norm_w = sb("norm_w", [P, C])
        su = sb("su", [P, M0, BLK])
        hid = sb("hid", [P, M0, BLK])
        xc = sb("xc", [P, C, BLK])
        sq = sb("sq", [P, C, BLK])
        ms = sb("ms", [P, BLK])
        rms = sb("rms", [P, BLK])
        ps_u = [ps(f"ps_u{i}", [P, BLK]) for i in range(2)]
        ps_g = [ps(f"ps_g{i}", [P, BLK]) for i in range(2)]
        ps_d = ps("ps_d", [P, C, BLK])
        ps_v = ps("ps_v", [P, BLK])
        wload, nload, xload, ahead = sem("wload"), sem("nload"), sem("xload"), sem("ahead")
        up_ready, gate_ready, su_done, hid_done = sem("up_ready"), sem("gate_ready"), sem("su_done"), sem("hid_done")
        down_ready, xc_done, sq_done = sem("down_ready"), sem("xc_done"), sem("sq_done")
        ms_ready, ms_done, rms_done, xn_done = sem("ms_ready"), sem("ms_done"), sem("rms_done"), sem("xn_done")
        block = st.block()

        @block.sync
        def _(sp):
            sp.dma_start(norm_w[:], a["norm_w"]).then_inc(nload, 16)
            sp.dma_start(x[:], a["x"]).then_inc(xload, 16)
            for b in range(B):
                e = sp.value_load(g.best[0:1, b * 8:b * 8 + 1], min_val=0, max_val=E8 - 1)
                if b > 0:
                    sp.wait_ge(xc_done, b * (BPB * C) + 1)
                sp.dma_start(w[:], a["cond0"][bass.ds(e, 1), :, :].rearrange("a p n -> p (a n)")).then_inc(wload, 16)
                if b == 0:
                    for name, buf in (("wq", g.wq), ("keys", g.keys), ("down", g.down), ("up", g.up)):
                        sp.dma_start(buf[:], a[name]).then_inc(ahead, 16)
            sp.wait_ge(ahead, 64)

        @block.tensor
        def _(pe):
            pe.sem_inc(down_ready, 1)
            pe.wait_ge(xload, 16)
            with pe.Fori(0, B) as b:
                pe.wait_ge(wload, b * 16 + 16)
                for k in range(BPB):
                    q = b * BPB + k
                    for m in range(M0):
                        for weight, bank, free, ready in ((w_up, ps_u, su_done, up_ready), (w_gate, ps_g, hid_done, gate_ready)):
                            pe.wait_ge(free, q * M0 + m + 1)
                            for c in range(C):
                                mm = pe.matmul(bank[m % 2][:], weight[:, c, m * P:(m + 1) * P], x[:, c, bass.ds(q * BLK, BLK)],
                                               start=(c == 0), stop=(c == C - 1))
                            mm.then_inc(ready, 1)
                    pe.wait_ge(hid_done, q * M0 + M0 + 2)
                    pe.wait_ge(xc_done, q * C + 1)
                    for c in range(C):
                        for m in range(M0):
                            mm = pe.matmul(ps_d[:, c, :], w_down[:, m, c * P:(c + 1) * P], hid[:, m, :],
                                           start=(m == 0), stop=(m == M0 - 1))
                        mm.then_inc(down_ready, 1)
                    pe.wait_ge(ms_done, q + 1)
                    pe.wait_ge(sq_done, q * C + C)
                    for c in range(C):
                        mm = pe.matmul(ps_v[:], g.mean_w[:], sq[:, c, :], start=(c == 0), stop=(c == C - 1))
                    mm.then_inc(ms_ready, 1)

        @block.scalar
        def _(act):
            act.sem_inc(su_done, 2)
            act.sem_inc(ms_done, 1)
            act.sem_inc(xc_done, 1)
            with act.Fori(0, B) as b:
                act.wait_ge(wload, b * 16 + 16)
                for k in range(BPB):
                    q = b * BPB + k
                    act.wait_ge(hid_done, q * M0 + 2)
                    for m in range(M0):
                        act.wait_ge(up_ready, q * M0 + m + 1)
                        act.activation(su[:, m, :], ps_u[m % 2][:], ACT.Silu, bias=b_up[:, m:m + 1]).then_inc(su_done, 1)
                    act.wait_ge(xn_done, q * C + 1)
                    for c in range(C):
                        act.wait_ge(down_ready, q * C + c + 2)
                        act.activation(xc[:, c, :], ps_d[:, c, :], ACT.Identity, bias=b_down[:, c:c + 1]).then_inc(xc_done, 1)
                        act.wait_ge(xc_done, q * C + c + 2)
                        act.activation(sq[:, c, :], xc[:, c, :], ACT.Square).then_inc(sq_done, 1)
                    act.wait_ge(ms_ready, q + 1)
                    act.activation(ms[:], ps_v[:], ACT.Sqrt, bias=g.eps[:, 0:1]).then_inc(ms_done, 1)

        @block.vector
        def _(dve):
            dve.sem_inc(hid_done, 2)
            dve.sem_inc(xn_done, 1)
            dve.wait_ge(nload, 16)
            with dve.Fori(0, B) as b:
                dve.wait_ge(wload, b * 16 + 16)
                for k in range(BPB):
                    q = b * BPB + k
                    dve.wait_ge(down_ready, q * C + 1)
                    for m in range(M0):
                        dve.wait_ge(su_done, q * M0 + m + 3)
                        dve.wait_ge(gate_ready, q * M0 + m + 1)
                        dve.scalar_tensor_tensor(out=hid[:, m, :], in0=ps_g[m % 2][:], scalar=b_gate[:, m:m + 1], in1=su[:, m, :],
                                                 op0=ALU.add, op1=ALU.mult).then_inc(hid_done, 1)
                    dve.wait_ge(ms_done, q + 2)
                    dve.reciprocal(rms[:], ms[:]).then_inc(rms_done, 1)
                    dve.wait_ge(rms_done, q + 1)
                    for c in range(C):
                        dve.scalar_tensor_tensor(out=g.x[:, c, bass.ds(q * BLK, BLK)], in0=xc[:, c, :], scalar=norm_w[:, c:c + 1],
                                                 in1=rms[:], op0=ALU.mult, op1=ALU.mult).then_inc(xn_done, 1)
            dve.wait_ge(xn_done, NBLK * C + 1)


PB = 256
NPB = T // PB
PT = PB // P
PAIRS = 8
CHUNKS = PB // 2 // PAIRS
CPT = CHUNKS // PT
RING = 4
NGRP = NJ // 2


def peer(nc, a, g):
    with Stage(nc, "peer") as st:
        sb, ps, sem = st.sb, st.ps, st.sem
        down, up = g.down, g.up
        hg = [sb(f"hg{i}", [P, NJ, PB]) for i in range(2)]
        am = [sb(f"am{i}", [P, PAIRS, P]) for i in range(RING)]
        bm = [sb(f"bm{i}", [P, PAIRS, 64]) for i in range(RING)]
        xin = [sb(f"xin{i}", [P, C, PB]) for i in range(2)]
        xt = sb("xt", [P, C, PB])
        slots = [sb(f"slots{i}", [P, 3, PB // 2]) for i in range(2)]
        s8 = sb("s8", [P, NG, 8])
        i8 = sb("i8", [P, NG, 8], U32)
        i8f = sb("i8f", [P, NG, 8])
        sums = sb("sums", [P, HEADS, 8, 8])
        f8 = sb("f8", [P, SLOTS])
        p8 = sb("p8", [P, SLOTS], U32)
        rank = sb("rank", [P, 2, SLOTS], U32)
        rankf = sb("rankf", [P, 2, SLOTS])
        oneh = sb("oneh", [P, SLOTS, 8])
        ij = sb("ij", [P, 2, SLOTS])
        ju = sb("ju", [P, SLOTS], U32)
        jb = sb("jb", [P, 2, SLOTS], U32)
        jf = sb("jf", [P, 2, SLOTS])
        codes = sb("codes", [P, 3, SLOTS])
        ps_h = [ps(f"ps_h{i}", [P, 2, PB]) for i in range(2)]
        ps_w = [ps(f"ps_w{i}", [P, PAIRS, 64]) for i in range(2)]
        ps_o = ps("ps_o", [P, C, PB])
        ps_s = ps("ps_s", [P, 2, BLK])
        ps_t = ps("ps_t", [P, BLK])
        xload = [sem(f"xload{i}") for i in range(2)]
        xt_done, sim_ready, sim_read, vstep, seen = sem("xt_done"), sem("sim_ready"), sem("sim_read"), sem("vstep"), sem("seen")
        codes_done, turned, kept = sem("codes_done"), sem("turned"), sem("kept")
        h_ready, gelu_done = sem("h_ready"), sem("gelu_done")
        a_done, beq_done, b_done = sem("a_done"), sem("beq_done"), sem("b_done")
        w_ready, p_done, o_ready, x_done = sem("w_ready"), sem("p_done"), sem("o_ready"), sem("x_done")
        block = st.block()
        per_tile = NG + 1 + 2 * HEADS + 3 + 1 + 2 * 3 + 1 + 2 + 1 + 2

        @block.sync
        def _(sp):
            def load_x(i, k):
                sp.dma_start(xin[k][:], a["x"][:, :, bass.ds(i * PB, PB)]).then_inc(xload[k], 16)

            for k in range(2):
                load_x(k, k)
            with sp.Fori(1, NPB // 2) as r:
                for k in range(2):
                    sp.wait_ge(x_done, r * 2 + k - 1)
                    load_x(r * 2 + k, k)

        @block.tensor
        def _(pe):
            def scores(i, t):
                n = i * PT + t
                if t == 0:
                    pe.wait_ge(xt_done, i + 1)
                pe.wait_ge(sim_read, n)
                for h in range(2):
                    for c in range(C):
                        mm = pe.matmul(ps_s[:, h, :], xt[:, c, t * P:(t + 1) * P],
                                       g.key_map[:, c, h * BLK:(h + 1) * BLK], start=(c == 0), stop=(c == C - 1))
                mm.then_inc(sim_ready, 1)

            def turn(i, t):
                n = i * PT + t
                pe.wait_ge(codes_done, n + 1)
                pe.wait_ge(kept, n * 6)
                flat = codes[:].rearrange("p a k -> p (a k)")
                pe.transpose(ps_t[:, 0:P], flat[:, 0:P], g.ident[:])
                pe.transpose(ps_t[0:SLOTS, P:2 * P], flat[:, P:P + SLOTS], g.ident[:]).then_inc(turned, 1)

            def act_rows(i, group):
                n = i * NGRP + group
                pe.wait_ge(gelu_done, n)
                for r in range(2):
                    j = 2 * group + r
                    for c in range(C):
                        mm = pe.matmul(ps_h[group % 2][:, r, :], down[:, c, j * P:(j + 1) * P],
                                       g.x[:, c, bass.ds(i * PB, PB)], start=(c == 0), stop=(c == C - 1))
                mm.then_inc(h_ready, 1)

            def weigh(i, c):
                n = i * CHUNKS + c
                pe.wait_ge(a_done, n + 1)
                pe.wait_ge(b_done, n + 1)
                pe.wait_ge(p_done, n)
                for m in range(PAIRS):
                    mm = pe.matmul(ps_w[c % 2][:, m, :], am[c % RING][:, m, :], bm[c % RING][:, m, :], start=True, stop=True)
                mm.then_inc(w_ready, 1)

            def work(i, half, first=False, more=True, route=True):
                for c in range(CHUNKS):
                    weigh(i, c)
                    if more:
                        if first and c % CPT == 0:
                            scores(i + 1, c // CPT)
                        act_rows(i + 1, c)
                        if first and c == CPT + 1:
                            turn(i + 1, 0)
                        if not first and c == 2:
                            turn(i + 1, 1)
                if route:
                    scores(i + 2, 0)
                pe.wait_ge(p_done, i * CHUNKS + CHUNKS + 1)
                pe.wait_ge(x_done, i)
                for c in range(C):
                    for j in range(NJ):
                        mm = pe.matmul(ps_o[:, c, :], up[:, j, c * P:(c + 1) * P], hg[half][:, j, :],
                                       start=(j == 0), stop=(j == NJ - 1))
                        if c == 0 and j == NJ // 2 and first:
                            turn(i + 1, 1)
                        if c == 0 and j == NJ // 2 and route:
                            scores(i + 2, 1)
                        if c == 1 and j == 2 and route:
                            turn(i + 2, 0)
                mm.then_inc(o_ready, 1)

            scores(0, 0)
            for group in range(NGRP):
                act_rows(0, group)
                if group == 3:
                    scores(0, 1)
                if group == 5:
                    turn(0, 0)
            turn(0, 1)
            work(0, 0, first=True)
            with pe.Fori(0, NPB // 2 - 2) as r:
                work(r * 2 + 1, 1)
                work(r * 2 + 2, 0)
            work(NPB - 3, 1)
            work(NPB - 2, 0, route=False)
            work(NPB - 1, 1, more=False, route=False)

        @block.scalar
        def _(act):
            def stage_x(i):
                act.activation(xt[:], g.x[:, :, bass.ds(i * PB, PB)], ACT.Copy).then_inc(xt_done, 1)

            def gelu(i, half, group):
                act.wait_ge(h_ready, i * NGRP + group + 1)
                act.activation(hg[half][:, 2 * group:2 * group + 2, :], ps_h[group % 2][:], ACT.Gelu).then_inc(gelu_done, 1)

            def keep(i, half, t):
                act.wait_ge(turned, i * PT + t + 1)
                for z in range(2):
                    r, f, col = slice(64 * z, 64 * z + 64), 64 * z, slice(64 * t, 64 * t + 64)
                    act.activation(slots[half][r, 0, col], ps_t[0:64, f:f + 64], ACT.Copy).then_inc(kept, 1)
                    act.activation(slots[half][r, 1, col], ps_t[64:128, f:f + 64], ACT.Copy).then_inc(kept, 1)
                    act.activation(slots[half][r, 2, col], ps_t[0:64, P + f:P + f + 64], ACT.Copy).then_inc(kept, 1)

            def slots_free(i):
                act.wait_ge(a_done, (i - 1) * CHUNKS)
                act.wait_ge(b_done, (i - 1) * CHUNKS)

            def ahead(i, half, route=True):
                slots_free(i)
                keep(i, half, 0)
                act.wait_ge(o_ready, i - 1)
                for group in range(NGRP):
                    gelu(i, half, group)
                    if group == 3:
                        keep(i, half, 1)
                    if group == CPT and route:
                        act.wait_ge(sim_ready, (i + 1) * PT)
                        stage_x(i + 1)

            act.sem_inc(gelu_done, 1)
            stage_x(0)
            for group in range(NGRP):
                gelu(0, 0, group)
                if group == 5:
                    keep(0, 0, 0)
            keep(0, 0, 1)
            act.wait_ge(sim_ready, PT)
            stage_x(1)
            for group in range(NGRP):
                gelu(1, 1, group)
                if group == CPT + 1:
                    keep(1, 1, 0)
                if group == CPT + 3:
                    act.wait_ge(sim_ready, 2 * PT)
                    stage_x(2)
            keep(1, 1, 1)
            with act.Fori(0, NPB // 2 - 2) as r:
                ahead(r * 2 + 2, 0)
                ahead(r * 2 + 3, 1)
            ahead(NPB - 2, 0)
            ahead(NPB - 1, 1, route=False)

        @block.gpsimd
        def _(pool):
            def weights(n, c, half):
                pool.wait_ge(beq_done, n + 1)
                pool.tensor_tensor(bm[c % RING][:], bm[c % RING][:],
                                   slots[half][:, 2, c * PAIRS:(c + 1) * PAIRS].unsqueeze(2).to_broadcast([P, PAIRS, 64]),
                                   ALU.mult).then_inc(b_done, 1)

            with pool.Fori(0, NPB // 2) as r:
                for half in range(2):
                    for c in range(CHUNKS):
                        weights((r * 2 + half) * CHUNKS + c, c, half)

        @block.vector
        def _(dve):
            def pick(i, t):
                n = i * PT + t
                s = Steps(vstep, n * per_tile)
                groups = [ps_s[:, j // 8, (j % 8) * NKEYS:(j % 8 + 1) * NKEYS] for j in range(NG)]
                pair = s8[:].rearrange("p (h two) k -> p h two k", two=2)
                cand = sums[:].rearrange("p h a b -> p h (a b)")
                dve.wait_ge(sim_ready, n + 1)
                dve.sem_inc(seen, 1)
                for j in range(NG // 2):
                    s.did(dve.max(s8[:, j, :], groups[j]))
                yield
                for j in range(NG // 2, NG):
                    s.did(dve.max(s8[:, j, :], groups[j]))
                yield
                s.settle(dve)
                dve.sem_inc(seen, 1)
                for j in range(NG // 2):
                    dve.max_index(i8[:, j, :], s8[:, j, :], groups[j])
                yield
                for j in range(NG // 2, NG - 1):
                    dve.max_index(i8[:, j, :], s8[:, j, :], groups[j])
                dve.max_index(i8[:, NG - 1, :], s8[:, NG - 1, :], groups[NG - 1]).then_inc(sim_read, 1)
                s.did(dve.tensor_tensor(sums[:], pair[:, :, 0, :].unsqueeze(3).to_broadcast([P, HEADS, 8, 8]),
                                        pair[:, :, 1, :].unsqueeze(2).to_broadcast([P, HEADS, 8, 8]), ALU.add))
                yield
                s.settle(dve)
                dve.sem_inc(seen, 1)
                for h in range(HEADS):
                    s.did(dve.max(f8[:, h * 8:h * 8 + 8], cand[:, h, :]))
                yield
                s.settle(dve)
                dve.sem_inc(seen, 1)
                for h in range(HEADS):
                    s.did(dve.max_index(p8[:, h * 8:h * 8 + 8], f8[:, h * 8:h * 8 + 8], cand[:, h, :]))
                s.settle(dve)
                s.did(dve.tensor_copy(i8f[:], i8[:]))
                s.did(dve.tensor_scalar(rank[:, 0, :], p8[:], 3, None, ALU.logical_shift_right))
                s.did(dve.tensor_scalar(rank[:, 1, :], p8[:], 7, None, ALU.bitwise_and))
                s.settle(dve)
                s.did(dve.tensor_copy(rankf[:], rank[:]))
                yield
                ids = i8f[:].rearrange("p (h two) k -> p h two k", two=2)
                for z in range(2):
                    s.settle(dve)
                    s.did(dve.tensor_tensor(oneh[:], rankf[:, z, :].unsqueeze(2).to_broadcast([P, SLOTS, 8]),
                                            g.iota_a[:, 0:8].unsqueeze(1).to_broadcast([P, SLOTS, 8]), ALU.is_equal))
                    s.settle(dve)
                    o = oneh[:].rearrange("p (h k) a -> p h k a", h=HEADS)
                    s.did(dve.tensor_tensor(o, o, ids[:, :, z, :].unsqueeze(2).to_broadcast([P, HEADS, 8, 8]), ALU.mult))
                    s.settle(dve)
                    s.did(dve.tensor_reduce(ij[:, z, :], oneh[:], AX_X, ALU.add))
                    if z == 0:
                        yield
                s.settle(dve)
                s.did(dve.tensor_copy(ju[:], ij[:, 1, :]))
                s.settle(dve)
                s.did(dve.tensor_scalar(jb[:, 0, :], ju[:], 1, None, ALU.bitwise_and))
                s.did(dve.tensor_scalar(jb[:, 1, :], ju[:], 1, None, ALU.logical_shift_right))
                s.settle(dve)
                s.did(dve.tensor_copy(jf[:], jb[:]))
                s.settle(dve)
                dve.wait_ge(turned, n)
                s.did(dve.tensor_copy(codes[:, 1, :], jf[:, 1, :]))
                s.did(dve.tensor_scalar(codes[:, 2, :], f8[:], 0.0, None, ALU.max))
                dve.scalar_tensor_tensor(out=codes[:, 0, :], in0=jf[:, 0, :], scalar=64.0, in1=ij[:, 0, :],
                                         op0=ALU.mult, op1=ALU.add).then_inc(codes_done, 1)
                dve.wait_ge(codes_done, n + 1)
                assert s.n == per_tile, s.n
                yield

            def build(i, c, half):
                if c % CPT == 0:
                    dve.wait_ge(kept, (i * PT + c // CPT + 1) * 6)
                col = slice(c * PAIRS, (c + 1) * PAIRS)
                dve.tensor_tensor(bm[c % RING][:], g.iota_b[:].unsqueeze(1).to_broadcast([P, PAIRS, 64]),
                                  slots[half][:, 1, col].unsqueeze(2).to_broadcast([P, PAIRS, 64]), ALU.is_equal).then_inc(beq_done, 1)
                dve.tensor_tensor(am[c % RING][:], g.iota_a[:].unsqueeze(1).to_broadcast([P, PAIRS, P]),
                                  slots[half][:, 0, col].unsqueeze(2).to_broadcast([P, PAIRS, P]), ALU.is_equal).then_inc(a_done, 1)

            def add_out(i, half, n_load):
                dve.wait_ge(xload[half], n_load * 16 + 16)
                dve.wait_ge(o_ready, i + 1)
                dve.tensor_tensor(g.x[:, :, bass.ds(i * PB, PB)], ps_o[:], xin[half][:], ALU.add).then_inc(x_done, 1)

            def work(i, half, r, first=False, last=False, route=True):
                for c in range(CHUNKS):
                    n = i * CHUNKS + c
                    at = c + RING - 1
                    if not (last and at >= CHUNKS):
                        dve.wait_ge(w_ready, n)
                        build(i + at // CHUNKS, at % CHUNKS, (half + at // CHUNKS) % 2)
                    if c == 0 and not first:
                        add_out(i - 1, 1 - half, r)
                    if first:
                        if c % CPT == 0:
                            parts = pick(i + 1, c // CPT)
                        next(parts)
                    if c == 0:
                        dve.wait_ge(gelu_done, i * NGRP + NGRP + 1)
                    dve.wait_ge(w_ready, n + 1)
                    t0 = c // CPT * P + c % CPT * PAIRS
                    h = hg[half][:].rearrange("p j (z m) -> p z j m", z=PT * 2)
                    z0, m0 = 2 * (c // CPT), c % CPT * PAIRS
                    acts = h[:, z0:z0 + 2, :, m0:m0 + PAIRS]
                    dve.tensor_tensor(acts, ps_w[c % 2][:].rearrange("p m (z j) -> p z j m", z=2), acts, ALU.mult).then_inc(p_done, 1)
                if route:
                    for t in range(PT):
                        for _ in pick(i + 2, t):
                            pass

            dve.sem_inc(p_done, 1)
            for t in range(PT):
                for _ in pick(0, t):
                    pass
            for c in range(RING - 1):
                build(0, c, 0)
            work(0, 0, 0, first=True)
            with dve.Fori(0, NPB // 2 - 2) as r:
                work(r * 2 + 1, 1, r)
                work(r * 2 + 2, 0, r)
            work(NPB - 3, 1, NPB // 2 - 2)
            work(NPB - 2, 0, NPB // 2 - 2, route=False)
            work(NPB - 1, 1, NPB // 2 - 1, last=True, route=False)
            add_out(NPB - 1, 1, NPB // 2 - 1)
            dve.wait_ge(x_done, NPB)


def lora(nc, a, g):
    with Stage(nc, "lora") as st:
        sb, ps, sem = st.sb, st.ps, st.sem
        a_rows = sb("a_rows", [P, D])
        b_rows = sb("b_rows", [P, D])
        w_rep = sb("w_rep", [P, B])
        b_scaled = [sb(f"b_scaled{b}", [P, D]) for b in range(B)]
        w_base = sb("w_base", [P, C, D])
        w_eff = [sb(f"w_eff{b}", [P, C, D]) for b in range(B)]
        cols = sb("cols", [P, 2 * C])
        base_w = sb("base_w", [P, C, D])
        ra = sb("ra", [P, C, R1ALL])
        rb = sb("rb", [R1ALL, D])
        rw = sb("rw", [P, C, E1])
        rbias = sb("rbias", [P, E1])
        xl = sb("xl", [P, C, T])
        logit = sb("logit", [P, T // P, E1])
        peak = sb("peak", [P, T // P])
        ex = sb("ex", [P, T // P, E1])
        gate = sb("gate", [P, T // P, 8])
        g8 = sb("g8", [P, T // P, 8])
        gi = sb("gi", [P, T // P, 8], U32)
        gif = sb("gif", [P, T // P, 8])
        hot = sb("hot", [P, 2, T // P, E1])
        sparse = sb("sparse", [P, T // P, E1])
        total = sb("total", [P, T // P])
        inv = sb("inv", [P, T // P])
        wide = sb("wide", [P, T // P, R1ALL])
        hs = sb("hs", [R1ALL, T])
        hw = [sb(f"hw{i}", [R1ALL, BLK]) for i in range(2)]
        ps_a = ps("ps_a", [P, C, BLK])
        ps_l = ps("ps_l", [P, T // P, 8])
        ps_h = ps("ps_h", [P, BLK])
        ps_o = [ps(f"ps_o{i}", [P, C, BLK]) for i in range(2)]
        loads, presets, ahead = sem("loads"), sem("presets"), sem("ahead")
        scaled, fold_ready, w_done = sem("scaled"), sem("fold_ready"), sem("w_done")
        xl_ready, xl_done, l_ready, ex_done = sem("xl_ready"), sem("xl_done"), sem("l_ready"), sem("ex_done")
        h_ready, hs_done, vstep = sem("h_ready"), sem("hs_done"), sem("vstep")
        wide_done, w_ready, hw_done, o_ready, x_done = sem("wide_done"), sem("w_ready"), sem("hw_done"), sem("o_ready"), sem("x_done")
        block = st.block()
        names = ["l1_a", "l1_b", "l1_w", "l1_wbase", "l1_cols", "l1_basew", "l1_ra", "l1_rb", "l1_rw"]
        bufs = [a_rows, b_rows, w_rep, w_base, cols, base_w, ra, rb, rw]
        n_loads = 16 * (len(names) + 1)
        tiles = T // P
        all_e = [P, tiles, E1]
        blocks = [slice(q * BLK, (q + 1) * BLK) for q in range(NBLK)]

        @block.sync
        def _(sp):
            for name, buf in zip(names, bufs):
                sp.dma_start(buf[:], a[name]).then_inc(loads, 16)
            sp.dma_start(rbias[:], a["l1_rbias"].partition_broadcast(P)).then_inc(loads, 16)
            e = sp.value_load(g.pair_idx[0:1, 0:1], min_val=0, max_val=E8 - 1)
            sp.dma_start(g.skill[:], a["skills"][bass.ds(e, 1), :, :].rearrange("a p n -> p (a n)")).then_inc(ahead, 16)
            sp.dma_start(g.q4[:].rearrange("p n q -> p (n q)"), a["q_w"]).then_inc(ahead, 16)
            sp.wait_ge(ahead, 32)

        @block.gpsimd
        def _(pool):
            pool.memset(gate[:], -1.0).then_inc(presets, 1)
            pool.memset(wide[:], 1.0).then_inc(presets, 1)
            pool.wait_ge(presets, 2)

        @block.tensor
        def _(pe):
            def fold(b):
                pe.wait_ge(scaled, b + 1)
                if b > 0:
                    pe.wait_ge(w_done, b)
                for c in range(C):
                    mm = pe.matmul(ps_a[:, c, 0:D], a_rows[:, c * P:(c + 1) * P], b_scaled[b][:], start=True, stop=True)
                mm.then_inc(fold_ready, 1)

            def mapped(q):
                for m in range(C):
                    if q > 0:
                        pe.wait_ge(xl_done, (q - 1) * C + m + 1)
                    for c in range(C):
                        mm = pe.matmul(ps_a[:, m, :], w_eff[q // BPB][:, c, m * P:(m + 1) * P], g.x[:, c, blocks[q]],
                                       start=(c == 0), stop=(c == C - 1))
                    mm.then_inc(xl_ready, 1)

            def logits(q):
                pe.wait_ge(xl_done, q * C + C)
                for t in range(q * TPB, (q + 1) * TPB):
                    for c in range(C):
                        mm = pe.matmul(ps_l[:, t, 0:E1], xl[:, c, t * P:(t + 1) * P], rw[:, c, :],
                                       start=(c == 0), stop=(c == C - 1))
                mm.then_inc(l_ready, 1)

            def lowered(q):
                if q > 0:
                    pe.wait_ge(hs_done, q)
                for c in range(C):
                    mm = pe.matmul(ps_h[0:R1ALL, :], ra[:, c, :], xl[:, c, blocks[q]], start=(c == 0), stop=(c == C - 1))
                mm.then_inc(h_ready, 1)

            def base(q):
                if q >= 2:
                    pe.wait_ge(x_done, (q - 1) * C)
                for m in range(C):
                    for c in range(C):
                        pe.matmul(ps_o[q % 2][:, m, :], base_w[:, c, m * P:(m + 1) * P], xl[:, c, blocks[q]],
                                  start=(c == 0), stop=False)

            def spread(q):
                if q > 0:
                    pe.wait_ge(hw_done, q)
                for t in range(TPB):
                    mm = pe.matmul(ps_h[0:R1ALL, t * P:(t + 1) * P], wide[:, q * TPB + t, :], g.ident[:], start=True, stop=True)
                mm.then_inc(w_ready, 1)

            pe.wait_ge(loads, n_loads)
            for b in range(B):
                fold(b)
            pe.wait_ge(w_done, B)
            mapped(0)
            for q in range(NBLK):
                if q + 1 < NBLK:
                    mapped(q + 1)
                logits(q)
                lowered(q)
            for q in range(2):
                base(q)
            pe.wait_ge(hs_done, NBLK)
            pe.wait_ge(wide_done, 1)
            spread(0)
            for q in range(NBLK):
                pe.wait_ge(hw_done, q + 1)
                if q + 1 < NBLK:
                    spread(q + 1)
                for m in range(C):
                    mm = pe.matmul(ps_o[q % 2][:, m, :], rb[:, m * P:(m + 1) * P], hw[q % 2][:], start=False, stop=True)
                mm.then_inc(o_ready, 1)
                if q + 2 < NBLK:
                    base(q + 2)

        @block.scalar
        def _(act):
            act.wait_ge(loads, n_loads)

            def keep_mapped(q):
                for m in range(C):
                    act.wait_ge(xl_ready, q * C + m + 1)
                    act.activation(xl[:, m, blocks[q]], ps_a[:, m, :], ACT.Identity, bias=cols[:, m:m + 1]).then_inc(xl_done, 1)

            keep_mapped(0)
            for q in range(NBLK):
                if q + 1 < NBLK:
                    keep_mapped(q + 1)
                act.wait_ge(h_ready, q + 1)
                act.activation(hs[:, blocks[q]], ps_h[0:R1ALL, :], ACT.Copy).then_inc(hs_done, 1)
            act.wait_ge(vstep, 3)
            act.activation(ex[:], logit[:], ACT.Exp).then_inc(ex_done, 1)

        @block.vector
        def _(dve):
            s = Steps(vstep)

            def then(*ops):
                for op in ops:
                    s.did(op)
                s.settle(dve)

            dve.wait_ge(presets, 2)
            dve.wait_ge(loads, n_loads)
            for b in range(B):
                dve.tensor_scalar(b_scaled[b][:], b_rows[:], w_rep[:, b:b + 1], 2.0, ALU.mult, ALU.mult).then_inc(scaled, 1)
            for b in range(B):
                dve.wait_ge(fold_ready, b + 1)
                dve.tensor_tensor(w_eff[b][:], ps_a[:, :, 0:D], w_base[:], ALU.add).then_inc(w_done, 1)
            dve.wait_ge(l_ready, NBLK)
            then(dve.tensor_tensor(logit[:], ps_l[:, :, 0:E1], rbias[:].unsqueeze(1).to_broadcast(all_e), ALU.add))
            then(dve.tensor_reduce(peak[:], logit[:], AX_X, ALU.max))
            then(dve.tensor_tensor(logit[:], logit[:], peak[:].unsqueeze(2).to_broadcast(all_e), ALU.subtract))
            dve.wait_ge(ex_done, 1)
            then(dve.tensor_reduce(total[:], ex[:], AX_X, ALU.add))
            then(dve.reciprocal(inv[:], total[:]))
            then(dve.tensor_tensor(gate[:, :, 0:E1], ex[:], inv[:].unsqueeze(2).to_broadcast(all_e), ALU.mult))
            then(*[dve.max(g8[:, t, :], gate[:, t, :]) for t in range(tiles)])
            then(*[dve.max_index(gi[:, t, :], g8[:, t, :], gate[:, t, :]) for t in range(tiles)])
            then(dve.tensor_copy(gif[:], gi[:]))
            then(*[dve.tensor_tensor(hot[:, z, :, :], g.iota_a[:, 0:E1].unsqueeze(1).to_broadcast(all_e),
                                     gif[:, :, z:z + 1].to_broadcast(all_e), ALU.is_equal) for z in range(2)])
            then(dve.tensor_tensor(sparse[:], hot[:, 0, :, :], hot[:, 1, :, :], ALU.add))
            then(dve.tensor_tensor(sparse[:], sparse[:], gate[:, :, 0:E1], ALU.mult))
            then(dve.tensor_reduce(total[:], sparse[:], AX_X, ALU.add))
            then(dve.tensor_scalar(total[:], total[:], 1e-6, None, ALU.add))
            then(dve.reciprocal(inv[:], total[:]))
            then(dve.tensor_tensor(sparse[:], sparse[:], inv[:].unsqueeze(2).to_broadcast(all_e), ALU.mult))
            dve.tensor_copy(wide[:, :, 0:E1 * R1].rearrange("p t (e r) -> p t e r", r=R1),
                            sparse[:].unsqueeze(3).to_broadcast([P, tiles, E1, R1])).then_inc(wide_done, 1)

            def weighted(q):
                dve.wait_ge(w_ready, q + 1)
                dve.wait_ge(hs_done, q + 1)
                if q >= 2:
                    dve.wait_ge(o_ready, q - 1)
                dve.tensor_tensor(hw[q % 2][:], ps_h[0:R1ALL, :], hs[:, blocks[q]], ALU.mult).then_inc(hw_done, 1)

            weighted(0)
            for q in range(NBLK):
                if q + 1 < NBLK:
                    weighted(q + 1)
                dve.wait_ge(o_ready, q + 1)
                for m in range(C):
                    xs = g.x[:, m, blocks[q]]
                    dve.scalar_tensor_tensor(out=xs, in0=ps_o[q % 2][:, m, :], scalar=cols[:, C + m:C + m + 1], in1=xs,
                                             op0=ALU.add, op1=ALU.add).then_inc(x_done, 1)
            dve.wait_ge(x_done, NBLK * C)


NQW = C * Q2
NQB = 3 * NQW // QB


class FourBits:

    def __init__(self, st, w):
        self.w, self.peak, self.scale, self.inv = w, st.sb("peak", [P, NQB]), st.sb("scale", [P, NQB]), st.sb("inv", [P, NQB])
        self.scaled, self.step = st.sem("four_scaled"), st.sem("four_step")

    def scales(self, dve):
        dve.tensor_reduce(self.peak[:], self.w[:], AX_X, ALU.max, apply_absolute_value=True).then_inc(self.scaled, 1)
        dve.wait_ge(self.scaled, 1)
        dve.tensor_scalar(self.scale[:], self.peak[:], 1.0 / 7, 1e-12, ALU.mult, ALU.max).then_inc(self.scaled, 1)
        dve.wait_ge(self.scaled, 2)
        dve.reciprocal(self.inv[:], self.scale[:]).then_inc(self.scaled, 1)

    def rounded(self, pool):
        wide = [P, NQB, QB]
        w = self.w[:]
        pool.wait_ge(self.scaled, 3)
        pool.tensor_tensor(w, w, self.inv[:].unsqueeze(2).to_broadcast(wide), ALU.mult).then_inc(self.step, 1)
        pool.wait_ge(self.step, 1)
        pool.tensor_scalar(w, w, ROUND, ROUND, ALU.add, ALU.subtract).then_inc(self.step, 1)
        pool.wait_ge(self.step, 2)
        pool.tensor_scalar(w, w, -8.0, 7.0, ALU.max, ALU.min).then_inc(self.step, 1)
        pool.wait_ge(self.step, 3)
        pool.tensor_tensor(w, w, self.scale[:].unsqueeze(2).to_broadcast(wide), ALU.mult).then_inc(self.step, 1)
        pool.wait_ge(self.step, 4)


def skills(nc, a, g):
    with Stage(nc, "skills") as st:
        sb, ps, sem = st.sb, st.ps, st.sem
        nw = SKILL
        w = [g.skill] + [sb(f"w{i}", [P, nw]) for i in range(1, 3)]
        w_gate = [x[:, 0:C * I2].rearrange("p (c i) -> p c i", c=C) for x in w]
        w_up = [x[:, C * I2:2 * C * I2].rearrange("p (c i) -> p c i", c=C) for x in w]
        w_down = [x[:, 2 * C * I2:nw].rearrange("p (m d) -> p m d", m=M2) for x in w]
        act_g = [sb(f"act_g{i}", [P, BLK]) for i in range(2)]
        hid = [sb(f"hid{i}", [P, BLK]) for i in range(4)]
        ps_g = [ps(f"ps_g{i}", [P, BLK]) for i in range(2)]
        ps_u = [ps(f"ps_u{i}", [P, BLK]) for i in range(2)]
        acc = [[ps(f"acc{k}{c}", [P, BLK]) for c in range(C)] for k in range(BPB)]
        wload = [sem(f"wload{i}") for i in range(3)]
        g_ready, u_ready, gelu_done, hid_done = sem("g_ready"), sem("u_ready"), sem("gelu_done"), sem("hid_done")
        d_ready, y_done = sem("d_ready"), sem("y_done")
        block = st.block()
        plan = [(s, k, m) for s in range(3) for k in range(BPB) for m in range(M2)]
        n_b = len(plan)
        four = FourBits(st, g.q4)

        @block.sync
        def _(sp):
            sp.sem_inc(wload[0], 16)
            for b in range(B):
                for s in range(2):
                    if (b, s) == (0, 0):
                        continue
                    e = sp.value_load(g.pair_idx[0:1, b * 8 + s:b * 8 + s + 1], min_val=0, max_val=E8 - 1)
                    sp.wait_ge(d_ready, b * n_b + 1)
                    sp.dma_start(w[s][:], a["skills"][bass.ds(e, 1), :, :].rearrange("a p n -> p (a n)")).then_inc(wload[s], 16)
                sp.dma_start(w[2][:], a["skill_shared"]).then_inc(wload[2], 16)

        @block.gpsimd
        def _(pool):
            four.rounded(pool)

        @block.tensor
        def _(pe):
            pe.sem_inc(d_ready, 1)
            def down(b, j):
                s, k, m = plan[j]
                n = b * n_b + j
                pe.wait_ge(hid_done, n + 3)
                if j == 0:
                    pe.wait_ge(y_done, b * (BPB * C) + 1)
                for c in range(C):
                    mm = pe.matmul(acc[k][c][:], w_down[s][:, m, c * P:(c + 1) * P], hid[j % 4][:],
                                   start=(s == 0 and m == 0), stop=(s == 2 and m == M2 - 1))
                mm.then_inc(d_ready, 1)

            with pe.Fori(0, B) as b:
                for j, (s, k, m) in enumerate(plan):
                    n = b * n_b + j
                    if k == 0 and m == 0:
                        pe.wait_ge(wload[s], b * 16 + 16)
                    for weight, bank, free, ready in ((w_gate[s], ps_g[j % 2], gelu_done, g_ready),
                                                      (w_up[s], ps_u[j % 2], hid_done, u_ready)):
                        pe.wait_ge(free, n + 1)
                        for c in range(C):
                            mm = pe.matmul(bank[:], weight[:, c, m * P:(m + 1) * P],
                                           g.x[:, c, bass.ds((b * BPB + k) * BLK, BLK)], start=(c == 0), stop=(c == C - 1))
                        mm.then_inc(ready, 1)
                    if j:
                        down(b, j - 1)
                down(b, n_b - 1)

        @block.scalar
        def _(act):
            act.sem_inc(gelu_done, 2)
            act.sem_inc(y_done, 1)
            with act.Fori(0, B) as b:
                for j in range(n_b):
                    n = b * n_b + j
                    act.wait_ge(g_ready, n + 1)
                    act.wait_ge(hid_done, n + 1)
                    act.activation(act_g[j % 2][:], ps_g[j % 2][:], ACT.Gelu_apprx_tanh).then_inc(gelu_done, 1)
                act.wait_ge(d_ready, b * n_b + n_b + 1)
                for k in range(BPB):
                    for c in range(C):
                        act.activation(g.y[:, c, bass.ds((b * BPB + k) * BLK, BLK)], acc[k][c][:], ACT.Copy).then_inc(y_done, 1)
            act.wait_ge(y_done, NBLK * C + 1)

        @block.vector
        def _(dve):
            dve.sem_inc(hid_done, 2)
            four.scales(dve)
            with dve.Fori(0, B) as b:
                for j, (s, k, m) in enumerate(plan):
                    n = b * n_b + j
                    dve.wait_ge(gelu_done, n + 3)
                    dve.wait_ge(u_ready, n + 1)
                    if j >= 4:
                        dve.wait_ge(d_ready, n - 3 + 1)
                    else:
                        dve.wait_ge(d_ready, b * n_b + 1)
                    scale = g.pair_w[:, bass.ds(b * 2 + s, 1)] if s < 2 else 1.0
                    dve.scalar_tensor_tensor(out=hid[j % 4][:], in0=ps_u[j % 2][:], scalar=scale, in1=act_g[j % 2][:],
                                             op0=ALU.mult, op1=ALU.mult).then_inc(hid_done, 1)


def weights4(nc, a, g):
    with Stage(nc, "weights4") as st:
        ps, sem = st.ps, st.sem
        bank = [ps(f"bank{i}", [P, 4, P]) for i in range(2)]
        turned, kept = sem("turned"), sem("kept")
        block = st.block()
        flat = g.q4[:].rearrange("p n q -> p (n q)")

        turns = [(flat[:, (z * MQ + m) * D + c * P:(z * MQ + m) * D + (c + 1) * P], z, c, m)
                 for z in range(2) for c in range(C) for m in range(MQ)]
        turns += [(flat[:, 2 * NQW + c * Q2 + m * P:2 * NQW + c * Q2 + (m + 1) * P], 2, m, c)
                  for m in range(MQ) for c in range(C)]

        @block.tensor
        def _(pe):
            for n, (src, *_) in enumerate(turns):
                r = n // 4
                if n % 4 == 0 and r >= 2:
                    pe.wait_ge(kept, r - 1)
                mm = pe.transpose(bank[r % 2][:, n % 4, :], src, g.ident[:])
                if n % 4 == 3:
                    mm.then_inc(turned, 1)

        @block.scalar
        def _(act):
            dst = g.qw[:].rearrange("p (r n) -> p r n", n=4 * P)
            for r in range(len(turns) // 4):
                act.wait_ge(turned, r + 1)
                act.activation(dst[:, r, :], bank[r % 2][:].rearrange("p a b -> p (a b)"), ACT.Copy).then_inc(kept, 1)
            act.wait_ge(kept, len(turns) // 4)


def quant_ffn(nc, a, g):
    with Stage(nc, "quant") as st:
        sb, ps, sem = st.sb, st.ps, st.sem
        wt = [g.qw[:, z * NQW:(z + 1) * NQW].rearrange("p (c i) -> p c i", c=C) for z in range(2)]
        wd = g.qw[:, 2 * NQW:3 * NQW].rearrange("p (m d) -> p m d", m=MQ)
        up = sb("up", [P, MQ, T])
        gate = sb("gate", [P, MQ, T])
        sig = [g.o[:, i, :] for i in range(C)]
        magic = sb("magic", [P, 1])
        term = sb("term", [P, C * D])
        peaks = sb("peaks", [P, 16])
        top = sb("top", [P, 8])
        alltop = sb("alltop", [P, 8])
        scale = sb("scale", [P, 8])
        inv = sb("inv", [P, 8])
        ps_m = [ps(f"ps_m{i}", [P, BLK]) for i in range(8)]
        vstep, spread, mm_ready, kept = sem("vstep"), sem("spread"), sem("mm_ready"), sem("kept")
        sig_done, sigq_done, x_done, d_ready = sem("sig_done"), sem("sigq_done"), sem("x_done"), sem("d_ready")
        mixed = sem("mixed")
        ahead, rounded, sig_step = sem("ahead"), sem("rounded"), sem("sig_step")
        block = st.block()
        marks = {}

        def quant(dve, s, t, n, rounds=None):
            if rounds is None:
                s.did(dve.tensor_scalar(t, t, inv[:, n:n + 1], ROUND, ALU.mult, ALU.add))
                s.settle(dve)
            else:
                dve.wait_ge(rounded, rounds)
            s.did(dve.tensor_scalar(t, t, ROUND, 32767.0, ALU.subtract, ALU.min))
            s.settle(dve)
            s.did(dve.tensor_scalar(t, t, -32768.0, scale[:, n:n + 1], ALU.max, ALU.mult))

        def scales(dve, s, n, count):
            s.settle(dve)
            s.did(dve.tensor_reduce(top[:, n:n + 1], peaks[:, 0:count], AX_X, ALU.max))
            marks["top", n] = s.n
            dve.wait_ge(spread, n + 1)
            s.did(dve.tensor_scalar(scale[:, n:n + 1], alltop[:, n:n + 1], 1.0 / 32767, 1e-12, ALU.mult, ALU.max))
            s.settle(dve)
            s.did(dve.reciprocal(inv[:, n:n + 1], scale[:, n:n + 1]))
            s.settle(dve)

        def peak(dve, s, t, n):
            s.did(dve.tensor_reduce(peaks[:, n:n + 1], t, AX_X, ALU.max, apply_absolute_value=True))

        @block.sync
        def _(sp):
            for name, buf in (("l3_w", g.ws), ("l3_mask", g.mask), ("l3_win", g.w_in), ("l3_bin", g.b_in), ("l3_bbot", g.b_bot)):
                sp.dma_start(buf[:], a[name]).then_inc(ahead, 16)
            sp.wait_ge(ahead, 16 * 5)

        @block.vector
        def _(dve):
            s = Steps(vstep)
            s.did(dve.memset(magic[:], ROUND))
            for c in range(C):
                peak(dve, s, g.y[:, c, :], c)
            scales(dve, s, 0, C)
            for c in range(C):
                quant(dve, s, g.y[:, c, :], 0)
            marks["x"] = s.n
            for z, t in enumerate((up, gate)):
                for m in range(MQ):
                    dve.wait_ge(kept, NBLK * (z * MQ + m + 1))
                    peak(dve, s, t[:, m, :], m)
                scales(dve, s, 1 + z, MQ)
                marks["inv", 1 + z] = s.n
                for m in range(MQ):
                    quant(dve, s, t[:, m, :], 1 + z, m + 1 if z == 1 else None)
                    marks[z, m] = s.n
            for m in range(MQ):
                dve.wait_ge(sig_done, m + 1)
                u = sig[m % 2]
                s.did(dve.tensor_scalar(u, u, ROUND, 65535.0, ALU.subtract, ALU.min))
                s.settle(dve)
                s.did(dve.tensor_scalar(u, u, 0.0, 1.0 / 65536, ALU.max, ALU.mult))
                s.settle(dve)
                dve.tensor_tensor(gate[:, m, :], gate[:, m, :], u, ALU.mult).then_inc(sigq_done, 1)
                dve.wait_ge(sigq_done, m + 1)
                peak(dve, s, gate[:, m, :], m)
            scales(dve, s, 3, MQ)
            marks["inv", 3] = s.n
            for m in range(MQ):
                quant(dve, s, gate[:, m, :], 3, MQ + m + 1)
                s.settle(dve)
                s.did(dve.tensor_tensor(gate[:, m, :], gate[:, m, :], up[:, m, :], ALU.mult))
                s.settle(dve)
                peak(dve, s, gate[:, m, :], m)
            scales(dve, s, 4, MQ)
            marks["inv", 4] = s.n
            for m in range(MQ):
                quant(dve, s, gate[:, m, :], 4, 2 * MQ + m + 1)
                marks["o", m] = s.n
            for q in range(NBLK):
                for c in range(C):
                    dve.wait_ge(d_ready, q * C + c + 1)
                    xs = g.x[:, c, q * BLK:(q + 1) * BLK]
                    dve.tensor_tensor(xs, ps_m[(q * C + c) % 8][:], xs, ALU.add).then_inc(x_done, 1)
            dve.wait_ge(x_done, NBLK * C)

        @block.gpsimd
        def _(pool):
            s = Steps(mixed)

            def mix(b):
                wide = [P, C * D]
                for e in range(E3):
                    y = g.cond_all[:, b * E8 + e:b * E8 + e + 1].to_broadcast(wide)
                    s.settle(pool)
                    if e == 0:
                        s.did(pool.tensor_tensor(g.wb[:, b, :], g.ws[:, 0, :], y, ALU.mult))
                    else:
                        s.did(pool.tensor_tensor(term[:], g.ws[:, e, :], y, ALU.mult))
                        s.settle(pool)
                        s.did(pool.tensor_tensor(g.wb[:, b, :], g.wb[:, b, :], term[:], ALU.add))
                s.settle(pool)
                s.did(pool.tensor_tensor(g.wb[:, b, :], g.wb[:, b, :], g.mask[:], ALU.mult))
                s.settle(pool)

            for n in range(5):
                pool.wait_ge(vstep, marks["top", n])
                pool.partition_all_reduce(alltop[:, n:n + 1], top[:, n:n + 1], P, bass.bass_isa.ReduceOp.max).then_inc(spread, 1)
                pool.wait_ge(spread, n + 1)
                if n < B:
                    pool.wait_ge(ahead, 16 * 5)
                    mix(n)
            pool.wait_ge(spread, 5)

        @block.tensor
        def _(pe):
            pe.wait_ge(vstep, marks["x"])
            n = 0
            for z in range(2):
                for m in range(MQ):
                    for q in range(NBLK):
                        if n >= 8:
                            pe.wait_ge(kept, n - 7)
                        for c in range(C):
                            mm = pe.matmul(ps_m[n % 8][:], wt[z][:, c, m * P:(m + 1) * P], g.y[:, c, q * BLK:(q + 1) * BLK],
                                           start=(c == 0), stop=(c == C - 1))
                        mm.then_inc(mm_ready, 1)
                        n += 1
            pe.wait_ge(kept, n)
            for m in range(MQ):
                pe.wait_ge(vstep, marks["o", m])
                for q in range(NBLK):
                    for c in range(C):
                        mm = pe.matmul(ps_m[(q * C + c) % 8][:], wd[:, m, c * P:(c + 1) * P], gate[:, m, q * BLK:(q + 1) * BLK],
                                       start=(m == 0), stop=(m == MQ - 1))
                        if m == MQ - 1:
                            mm.then_inc(d_ready, 1)

        @block.scalar
        def _(act):
            n = 0
            for t in (up, gate):
                for m in range(MQ):
                    for q in range(NBLK):
                        act.wait_ge(mm_ready, n + 1)
                        act.activation(t[:, m, q * BLK:(q + 1) * BLK], ps_m[n % 8][:], ACT.Copy).then_inc(kept, 1)
                        n += 1

            def round_scaled(m, n):
                act.wait_ge(vstep, marks["inv", n])
                act.activation(gate[:, m, :], gate[:, m, :], ACT.Identity, bias=magic[:],
                               scale=inv[:, n:n + 1]).then_inc(rounded, 1)

            round_scaled(0, 2)
            for m in range(MQ):
                if m < 2:
                    for k in ((1,), range(2, MQ))[m]:
                        round_scaled(k, 2)
                act.wait_ge(vstep, marks[1, m])
                if m >= 2:
                    act.wait_ge(sigq_done, m - 1)
                act.activation(sig[m % 2], gate[:, m, :], ACT.Sigmoid).then_inc(sig_step, 1)
                act.wait_ge(sig_step, m + 1)
                act.activation(sig[m % 2], sig[m % 2], ACT.Identity, bias=magic[:], scale=65536.0).then_inc(sig_done, 1)
            for n in (3, 4):
                for m in range(MQ):
                    round_scaled(m, n)


NQKV = 3 * C
WRING = 4
NP3 = S // BLK


def attend(nc, a, g):
    with Stage(nc, "attend") as st:
        sb, ps, sem = st.sb, st.ps, st.sem
        w_in, b_in = g.w_in, g.b_in
        w_bot = g.wb[:].rearrange("p b (c o) -> p b c o", c=C)
        qkv = sb("qkv", [P, NQKV, T])
        heads = sb("heads", [P, P])
        prod = [sb(f"prod{i}", [P, B, B, BLK]) for i in range(2)]
        sc = [sb(f"sc{i}", [P, B, B, BLK]) for i in range(2)]
        peak = sb("peak", [P, B, BLK])
        total = sb("total", [P, B, BLK])
        ps_m = [ps(f"ps_m{i}", [P, BLK]) for i in range(4)]
        ps_s = ps("ps_s", [P, 4, BLK])
        presets = sem("presets")
        x_ready, x_done, q_ready, q_done = sem("x_ready"), sem("x_done"), sem("q_ready"), sem("q_done")
        vstep, s_ready, sc_done, ex_done = sem("vstep"), sem("s_ready"), sem("sc_done"), sem("ex_done")
        block = st.block()
        steps = [(r, c) for r in range(NP3) for c in range(C)]
        marks = {}

        @block.gpsimd
        def _(pool):
            pool.memset(heads[:], 0.0).then_inc(presets, 1)
            pool.wait_ge(presets, 1)
            for r in (slice(0, HD), slice(HD, P)):
                pool.memset(heads[r, r], 1.0).then_inc(presets, 1)
            pool.wait_ge(presets, 3)

        @block.vector
        def _(dve):
            s = Steps(vstep)
            wide = [P, B, B, BLK]

            def rows(n, kind):
                r, c = steps[n]
                return qkv[:, kind * C + c, :].rearrange("p (b t) -> p b t", b=B)[:, :, r * BLK:(r + 1) * BLK]

            def multiply(n):
                if n >= 2:
                    dve.wait_ge(s_ready, n - 1)
                s.did(dve.tensor_tensor(prod[n % 2][:], rows(n, 0).unsqueeze(2).to_broadcast(wide),
                                        rows(n, 1).unsqueeze(1).to_broadcast(wide), ALU.mult))
                marks["prod", n] = s.n

            dve.wait_ge(q_done, NBLK * NQKV + 1)
            multiply(0)
            for n in range(len(steps)):
                r, c = steps[n]
                e = sc[n % 2]
                dve.wait_ge(sc_done, n + 1)
                s.did(dve.tensor_tensor(peak[:], e[:, :, 0, :], e[:, :, 1, :], ALU.max))
                s.settle(dve)
                s.did(dve.tensor_tensor(e[:], e[:], peak[:].unsqueeze(2).to_broadcast(wide), ALU.subtract))
                marks["shifted", n] = s.n
                if n + 1 < len(steps):
                    multiply(n + 1)
                dve.wait_ge(ex_done, n + 1)
                s.did(dve.tensor_tensor(total[:], e[:, :, 0, :], e[:, :, 1, :], ALU.add))
                s.settle(dve)
                s.did(dve.reciprocal(total[:], total[:]))
                s.did(dve.tensor_tensor(e[:], e[:], rows(n, 2).unsqueeze(1).to_broadcast(wide), ALU.mult))
                s.settle(dve)
                s.did(dve.tensor_tensor(peak[:], e[:, :, 0, :], e[:, :, 1, :], ALU.add))
                marks["through", n] = s.n
                s.settle(dve)
                o = g.o[:, c, :].rearrange("p (b t) -> p b t", b=B)[:, :, r * BLK:(r + 1) * BLK]
                s.did(dve.tensor_tensor(o, peak[:], total[:], ALU.mult))
                s.settle(dve)

        @block.tensor
        def _(pe):
            for b in range(B):
                for k in range(BPB):
                    for m in range(C):
                        n = (b * BPB + k) * C + m
                        if n >= 4:
                            pe.wait_ge(x_done, n - 3)
                        for c in range(C):
                            mm = pe.matmul(ps_m[n % 4][:], w_bot[:, b, c, m * P:(m + 1) * P],
                                           g.x[:, c, (b * BPB + k) * BLK:(b * BPB + k + 1) * BLK],
                                           start=(c == 0), stop=(c == C - 1))
                        mm.then_inc(x_ready, 1)
            pe.wait_ge(x_done, NBLK * C)
            with pe.Fori(0, NBLK) as q:
                for m in range(NQKV):
                    n = q * NQKV + m
                    pe.wait_ge(q_done, n - min(m, 3) + 1)
                    for c in range(C):
                        mm = pe.matmul(ps_m[m % 4][:], w_in[:, c, m * P:(m + 1) * P], g.y[:, c, bass.ds(q * BLK, BLK)],
                                       start=(c == 0), stop=(c == C - 1))
                    mm.then_inc(q_ready, 1)
            pe.wait_ge(presets, 3)
            for n in range(len(steps)):
                pe.wait_ge(vstep, marks["prod", n])
                if n > 0:
                    pe.wait_ge(sc_done, n)
                for z in range(4):
                    mm = pe.matmul(ps_s[:, z, :], heads[:], prod[n % 2][:, z // B, z % B, :], start=True, stop=True)
                mm.then_inc(s_ready, 1)

        @block.scalar
        def _(act):
            act.sem_inc(q_done, 1)
            for n in range(NBLK * C):
                q, m = n // C, n % C
                act.wait_ge(x_ready, n + 1)
                act.activation(g.y[:, m, q * BLK:(q + 1) * BLK], ps_m[n % 4][:], ACT.Identity,
                               bias=g.b_bot[:, m:m + 1]).then_inc(x_done, 1)
            with act.Fori(0, NBLK) as q:
                for m in range(NQKV):
                    act.wait_ge(q_ready, q * NQKV + m + 1)
                    act.activation(qkv[:, m, bass.ds(q * BLK, BLK)], ps_m[m % 4][:], ACT.Identity,
                                   bias=b_in[:, m:m + 1]).then_inc(q_done, 1)

            def keep_scores(n):
                act.wait_ge(s_ready, n + 1)
                if n >= 2:
                    act.wait_ge(vstep, marks["through", n - 2])
                act.activation(sc[n % 2][:].rearrange("p l m t -> p (l m) t"), ps_s[:], ACT.Copy,
                               scale=1.0 / 8).then_inc(sc_done, 1)

            keep_scores(0)
            for n in range(len(steps)):
                act.wait_ge(vstep, marks["shifted", n])
                act.activation(sc[n % 2][:], sc[n % 2][:], ACT.Exp).then_inc(ex_done, 1)
                if n + 1 < len(steps):
                    keep_scores(n + 1)


def norm(nc, a, g):
    with Stage(nc, "norm") as st:
        sb, ps, sem = st.sb, st.ps, st.sem
        w_out = sb("w_out", [P, C, D])
        wg = sb("wg", [P, C, E3])
        cols = sb("cols", [P, 3 * C])
        r = [sb(f"r{i}", [P, C, BLK]) for i in range(2)]
        sq = [sb(f"sq{i}", [P, C, BLK]) for i in range(2)]
        sd = [sb(f"sd{i}", [P, BLK]) for i in range(2)]
        y = [sb(f"y{i}", [P, C, BLK]) for i in range(2)]
        ps_m = [ps(f"ps_m{i}", [P, C, BLK]) for i in range(2)]
        ps_v = [ps(f"ps_v{i}", [P, BLK]) for i in range(2)]
        ps_l = ps("ps_l", [P, TPB, E3])
        loads, m_ready, mean_ready, var_ready = sem("loads"), sem("m_ready"), sem("mean_ready"), sem("var_ready")
        sq_done, sd_done, vstep, y_done, l_ready, l_done, y_kept = (
            sem("sq_done"), sem("sd_done"), sem("vstep"), sem("y_done"), sem("l_ready"), sem("l_done"), sem("y_kept"))
        ahead = sem("ahead")
        block = st.block()
        names, bufs = ["l3_wout", "l3_wg", "l3_cols"], [w_out, wg, cols]
        marks = {}

        @block.sync
        def _(sp):
            for name, buf in zip(names, bufs):
                sp.dma_start(buf[:], a[name]).then_inc(loads, 16)
            sp.dma_start(g.b1[:], a["l3_b1"]).then_inc(ahead, 16)
            sp.dma_start(g.b2[:], a["l3_b2"]).then_inc(ahead, 16)
            for e in range(WRING):
                sp.dma_start(g.w1[e][:], a["l3_w1"][e]).then_inc(ahead, 16)
                sp.dma_start(g.w2[e][:], a["l3_w2"][e]).then_inc(ahead, 16)
            sp.wait_ge(ahead, 16 * (2 * WRING + 2))

        @block.vector
        def _(dve):
            s = Steps(vstep)

            def add(q):
                for c in range(C):
                    dve.wait_ge(m_ready, q * C + c + 1)
                    if q >= 2:
                        dve.wait_ge(y_done, (q - 1) * C)
                    s.did(dve.scalar_tensor_tensor(out=r[q % 2][:, c, :], in0=ps_m[q % 2][:, c, :], scalar=cols[:, c:c + 1],
                                                   in1=g.y[:, c, q * BLK:(q + 1) * BLK], op0=ALU.add, op1=ALU.add))
                marks["added", q] = s.n

            def center(q):
                dve.wait_ge(mean_ready, q + 1)
                dve.wait_ge(vstep, marks["added", q])
                for c in range(C):
                    s.did(dve.tensor_tensor(r[q % 2][:, c, :], r[q % 2][:, c, :], ps_v[q % 2][:], ALU.subtract))
                    marks["centered", q, c] = s.n

            def invert(q):
                dve.wait_ge(sd_done, q + 1)
                s.did(dve.reciprocal(sd[q % 2][:], sd[q % 2][:]))

            def scale(q):
                for c in range(C):
                    s.did(dve.tensor_scalar(r[q % 2][:, c, :], r[q % 2][:, c, :], cols[:, C + c:C + c + 1], None, ALU.mult))
                s.settle(dve)
                for c in range(C):
                    s.did(dve.tensor_tensor(r[q % 2][:, c, :], r[q % 2][:, c, :], sd[q % 2][:], ALU.mult))
                    marks["scaled", q, c] = s.n

            dve.wait_ge(loads, 16 * len(names))
            for q in range(NBLK + 1):
                if q < NBLK:
                    add(q)
                if q > 0:
                    invert(q - 1)
                if q < NBLK:
                    center(q)
                if q > 0:
                    scale(q - 1)

        @block.tensor
        def _(pe):
            pe.wait_ge(loads, 16 * len(names))

            def products(q):
                if q >= 2:
                    pe.wait_ge(vstep, marks["added", q - 2])
                for m in range(C):
                    for c in range(C):
                        mm = pe.matmul(ps_m[q % 2][:, m, :], w_out[:, c, m * P:(m + 1) * P], g.o[:, c, q * BLK:(q + 1) * BLK],
                                       start=(c == 0), stop=(c == C - 1))
                    mm.then_inc(m_ready, 1)

            def mean(q):
                pe.wait_ge(vstep, marks["added", q])
                if q >= 2:
                    pe.wait_ge(sd_done, q - 1)
                for c in range(C):
                    mm = pe.matmul(ps_v[q % 2][:], g.mean_w[:], r[q % 2][:, c, :], start=(c == 0), stop=(c == C - 1))
                mm.then_inc(mean_ready, 1)

            def variance(q):
                pe.wait_ge(sq_done, q * C + C)
                for c in range(C):
                    mm = pe.matmul(ps_v[q % 2][:], g.mean_w[:], sq[q % 2][:, c, :], start=(c == 0), stop=(c == C - 1))
                mm.then_inc(var_ready, 1)

            def logits(q):
                pe.wait_ge(y_done, q * C + C)
                if q > 0:
                    pe.wait_ge(l_done, q)
                for t in range(TPB):
                    for c in range(C):
                        mm = pe.matmul(ps_l[:, t, :], y[q % 2][:, c, t * P:(t + 1) * P], wg[:, c, :], start=(c == 0), stop=(c == C - 1))
                mm.then_inc(l_ready, 1)

            products(0)
            for q in range(NBLK):
                mean(q)
                if q + 1 < NBLK:
                    products(q + 1)
                variance(q)
                if q > 0:
                    logits(q - 1)
            logits(NBLK - 1)

        @block.scalar
        def _(act):
            def squares(q):
                for c in range(C):
                    act.wait_ge(vstep, marks["centered", q, c])
                    if q >= 2:
                        act.wait_ge(var_ready, q - 1)
                    act.activation(sq[q % 2][:, c, :], r[q % 2][:, c, :], ACT.Square).then_inc(sq_done, 1)

            def deviation(q):
                act.wait_ge(var_ready, q + 1)
                act.activation(sd[q % 2][:], ps_v[q % 2][:], ACT.Sqrt, bias=g.eps[:, 1:2]).then_inc(sd_done, 1)

            def shift(q):
                if q >= 2:
                    act.wait_ge(l_ready, q - 1)
                    act.wait_ge(y_kept, q - 1)
                for c in range(C):
                    act.wait_ge(vstep, marks["scaled", q, c])
                    act.activation(y[q % 2][:, c, :], r[q % 2][:, c, :], ACT.Identity,
                                   bias=cols[:, 2 * C + c:2 * C + c + 1]).then_inc(y_done, 1)

            def keep_logits(q):
                act.wait_ge(l_ready, q + 1)
                act.activation(g.logit[:, q * TPB:(q + 1) * TPB, :], ps_l[:], ACT.Copy).then_inc(l_done, 1)

            act.wait_ge(loads, 16 * len(names))
            for q in range(NBLK):
                squares(q)
                deviation(q)
                if q > 0:
                    shift(q - 1)
                    keep_logits(q - 1)
            shift(NBLK - 1)
            keep_logits(NBLK - 1)
            act.wait_ge(l_done, NBLK)

        @block.gpsimd
        def _(pool):
            for q in range(NBLK):
                pool.wait_ge(y_done, q * C + C)
                pool.tensor_copy(g.y[:, :, q * BLK:(q + 1) * BLK], y[q % 2][:]).then_inc(y_kept, 1)
            pool.wait_ge(y_kept, NBLK)


NT = T // P


def experts(nc, a, g):
    with Stage(nc, "experts") as st:
        sb, ps, sem = st.sb, st.ps, st.sem
        n_f = FF // P
        w1, w2, b1, b2 = g.w1, g.w2, g.b1, g.b2
        b1_of = sb("b1_of", [P, E3, n_f, E3])
        ps_w = [ps(f"ps_w{i}", [P, C, D]) for i in range(2)]
        ps_c = ps("ps_c", [P, D])
        loads = [sem(f"loads{i}") for i in range(WRING)]
        folded, kept, b_step = sem("folded"), sem("kept"), sem("b_step")
        block = st.block()

        @block.sync
        def _(sp):
            for e in range(WRING, E3):
                sp.wait_ge(folded, e - WRING + 1)
                sp.dma_start(w1[e % WRING][:], a["l3_w1"][e]).then_inc(loads[e % WRING], 16)
                sp.dma_start(w2[e % WRING][:], a["l3_w2"][e]).then_inc(loads[e % WRING], 16)

        @block.tensor
        def _(pe):
            pe.wait_ge(b_step, E3 + 1)
            for e in range(E3):
                if e >= WRING:
                    pe.wait_ge(loads[e % WRING], 32 * (e // WRING))
                if e >= 2:
                    pe.wait_ge(kept, e - 1)
                for c in range(C):
                    for f in range(n_f):
                        pe.matmul(ps_w[e % 2][:, c, :], w1[e % WRING][:, f, c * P:(c + 1) * P], w2[e % WRING][:, f, :],
                                  start=(f == 0), stop=(f == n_f - 1))
                for f in range(n_f):
                    mm = pe.matmul(ps_c[0:E3, :], b1_of[:, e, f, :], w2[e % WRING][:, f, :],
                                   start=(e == 0 and f == 0), stop=(e == E3 - 1 and f == n_f - 1))
                mm.then_inc(folded, 1)

        @block.vector
        def _(dve):
            dve.memset(b1_of[:], 0.0).then_inc(b_step, 1)
            dve.wait_ge(b_step, 1)
            for e in range(E3):
                dve.tensor_copy(b1_of[:, e, :, e:e + 1], b1[:].rearrange("p (f e) -> p f e", e=E3)[:, :, e:e + 1]).then_inc(b_step, 1)
            for e in range(E3):
                dve.wait_ge(folded, e + 1)
                dve.tensor_copy(g.w12[:, e, :, :], ps_w[e % 2][:]).then_inc(kept, 1)
            dve.tensor_tensor(g.c12[:], ps_c[0:E3, :], b2[:], ALU.add).then_inc(kept, 1)
            dve.wait_ge(kept, E3 + 1)


def gates(nc, a, g):
    with Stage(nc, "gates") as st:
        sb, ps, sem = st.sb, st.ps, st.sem
        peak = sb("peak", [P, NT])
        total = sb("total", [P, NT])
        ex = sb("ex", [P, NT, E3])
        g8 = sb("g8", [P, NT, 8])
        gi = sb("gi", [P, NT, 8], U32)
        gif = sb("gif", [P, NT, 8])
        hot = sb("hot", [P, NT, E3])
        before = sb("before", [P, NT, E3])
        keep = sb("keep", [P, NT, E3])
        upto = sb("upto", [P, P])
        ones = sb("ones", [P, P])
        ps_c = ps("ps_c", [P, NT, E3])
        ps_n = ps("ps_n", [P, NT, E3])
        ps_t = ps("ps_t", [P, NT * P])
        presets, vstep, ex_done, counted, turned, kept = (
            sem("presets"), sem("vstep"), sem("ex_done"), sem("counted"), sem("turned"), sem("kept"))
        block = st.block()
        marks = {}
        wide = [P, NT, E3]

        @block.gpsimd
        def _(pool):
            pool.memset(ones[:], 1.0).then_inc(presets, 1)
            pool.memset(upto[:], 1.0).then_inc(presets, 1)
            pool.wait_ge(presets, 2)
            pool.affine_select(out=upto[:], in_=upto[:], compare_op=ALU.is_ge, fill=0.0, base=0,
                               pattern=[[1, P]], channel_multiplier=-1).then_inc(presets, 1)
            pool.wait_ge(presets, 3)

        @block.vector
        def _(dve):
            s = Steps(vstep)

            def then(*ops):
                for op in ops:
                    s.did(op)
                s.settle(dve)

            then(dve.tensor_reduce(peak[:], g.logit[:], AX_X, ALU.max))
            then(dve.tensor_tensor(g.logit[:], g.logit[:], peak[:].unsqueeze(2).to_broadcast(wide), ALU.subtract))
            marks["shifted"] = s.n
            dve.wait_ge(ex_done, 1)
            then(dve.tensor_reduce(total[:], ex[:], AX_X, ALU.add))
            then(dve.reciprocal(total[:], total[:]))
            then(dve.tensor_tensor(ex[:], ex[:], total[:].unsqueeze(2).to_broadcast(wide), ALU.mult))
            then(*[dve.max(g8[:, t, :], ex[:, t, :]) for t in range(NT)])
            then(*[dve.max_index(gi[:, t, :], g8[:, t, :], ex[:, t, :]) for t in range(NT)])
            then(dve.tensor_copy(gif[:], gi[:]))
            then(dve.tensor_tensor(hot[:], g.iota_a[:, 0:E3].unsqueeze(1).to_broadcast(wide),
                                   gif[:, :, 0:1].to_broadcast(wide), ALU.is_equal))
            marks["hot"] = s.n
            then(dve.memset(before[:, 0, :], 0.0))
            dve.wait_ge(counted, 2)
            for t in range(1, NT):
                then(dve.tensor_tensor(before[:, t, :], ps_n[:, t - 1, :], before[:, t - 1, :], ALU.add))
            then(dve.tensor_tensor(keep[:], ps_c[:], before[:], ALU.add))
            then(dve.scalar_tensor_tensor(out=hot[:], in0=keep[:], scalar=float(CAP), in1=hot[:],
                                          op0=ALU.is_le, op1=ALU.mult))
            then(dve.tensor_tensor(hot[:], hot[:], g8[:, :, 0:1].to_broadcast(wide), ALU.mult))
            marks["weight"] = s.n
            for b in range(4):
                dve.wait_ge(turned, b + 1)
                dve.tensor_copy(g.weight8[:, b * BLK:(b + 1) * BLK], ps_t[0:E3, b * BLK:(b + 1) * BLK]).then_inc(kept, 1)
            dve.wait_ge(kept, 4)

        @block.scalar
        def _(act):
            act.wait_ge(vstep, marks["shifted"])
            act.activation(ex[:], g.logit[:], ACT.Exp).then_inc(ex_done, 1)

        @block.tensor
        def _(pe):
            pe.wait_ge(presets, 3)
            pe.wait_ge(vstep, marks["hot"])
            flat = hot[:].rearrange("p t e -> p (t e)")
            pe.matmul(ps_c[:].rearrange("p t e -> p (t e)"), upto[:], flat, start=True, stop=True).then_inc(counted, 1)
            pe.matmul(ps_n[:].rearrange("p t e -> p (t e)"), ones[:], flat, start=True, stop=True).then_inc(counted, 1)
            pe.wait_ge(vstep, marks["weight"])
            for t in range(NT):
                mm = pe.transpose(ps_t[0:E3, t * P:(t + 1) * P], hot[:, t, :], g.ident[:])
                if t % 4 == 3:
                    mm.then_inc(turned, 1)


def moe(nc, a, g, out):
    with Stage(nc, "moe") as st:
        sb, ps, sem = st.sb, st.ps, st.sem
        sel = sb("sel", [E3, E3, P])
        cols = sb("cols", [P, 2 * C])
        xm = [sb(f"xm{i}", [P, C, BLK]) for i in range(2)]
        r = sb("r", [P, C, BLK])
        sq = sb("sq", [P, C, BLK])
        sd = sb("sd", [P, BLK])
        o = sb("o", [P, C, BLK])
        ps_b = [ps(f"ps_b{i}", [P, BLK]) for i in range(2)]
        ps_y = [ps(f"ps_y{i}", [P, C, BLK]) for i in range(2)]
        ps_v = ps("ps_v", [P, 2, BLK])
        loads, presets, b_ready, xm_done = sem("loads"), sem("presets"), sem("b_ready"), sem("xm_done")
        xm_read, y_ready, mean_ready, var_ready = sem("xm_read"), sem("y_ready"), sem("mean_ready"), sem("var_ready")
        sq_done, sd_done, vstep, o_done, stored = sem("sq_done"), sem("sd_done"), sem("vstep"), sem("o_done"), sem("stored")
        block = st.block()
        per_block = 4 * C + 1

        @block.sync
        def _(sp):
            sp.dma_start(cols[:], a["l3_cols2"]).then_inc(loads, 16)
            for q in range(NBLK):
                sp.wait_ge(o_done, (q + 1) * C)
                sp.dma_start(out[:, :, q * BLK:(q + 1) * BLK], o[:]).then_inc(stored, 16)
            sp.wait_ge(stored, 16 * NBLK)

        @block.gpsimd
        def _(pool):
            pool.memset(sel[:], 0.0).then_inc(presets, 1)
            pool.wait_ge(presets, 1)
            pool.affine_select(out=sel[:], in_=sel[:], compare_op=ALU.not_equal, fill=1.0, base=0,
                               pattern=[[-1, E3], [0, P]], channel_multiplier=1).then_inc(presets, 1)
            pool.wait_ge(presets, 2)

        @block.tensor
        def _(pe):
            def spread(n):
                if n >= 2:
                    pe.wait_ge(xm_done, n - 1)
                q, e = divmod(n, E3)
                pe.matmul(ps_b[n % 2][:], sel[:, e, :], g.weight8[:, q * BLK:(q + 1) * BLK],
                          start=True, stop=True).then_inc(b_ready, 1)

            def mean(q):
                pe.wait_ge(vstep, q * per_block + C)
                for c in range(C):
                    mm = pe.matmul(ps_v[:, 0, :], g.mean_w[:], r[:, c, :], start=(c == 0), stop=(c == C - 1))
                mm.then_inc(mean_ready, 1)

            def variance(q):
                pe.wait_ge(sq_done, q * C + C)
                for c in range(C):
                    mm = pe.matmul(ps_v[:, 1, :], g.mean_w[:], sq[:, c, :], start=(c == 0), stop=(c == C - 1))
                mm.then_inc(var_ready, 1)

            pe.wait_ge(presets, 2)
            spread(0)
            for q in range(NBLK):
                for e in range(E3):
                    n = q * E3 + e
                    if n + 1 < NBLK * E3:
                        spread(n + 1)
                    if e == 0 and q >= 2:
                        pe.wait_ge(vstep, (q - 2) * per_block + C)
                    pe.wait_ge(xm_done, n + 1)
                    for m in range(C):
                        for c in range(C):
                            mm = pe.matmul(ps_y[q % 2][:, m, :], g.w12[:, e, c, m * P:(m + 1) * P], xm[e % 2][:, c, :],
                                           start=(e == 0 and c == 0), stop=False)
                    mm.then_inc(xm_read, 1)
                    if e == 1 and q > 0:
                        mean(q - 1)
                    if e == 3 and q > 0:
                        variance(q - 1)
                for m in range(C):
                    mm = pe.matmul(ps_y[q % 2][:, m, :], g.c12[:, m * P:(m + 1) * P], g.weight8[:, q * BLK:(q + 1) * BLK],
                                   start=False, stop=True)
                mm.then_inc(y_ready, 1)
            mean(NBLK - 1)
            variance(NBLK - 1)

        @block.scalar
        def _(act):
            for q in range(NBLK):
                if q > 0:
                    act.wait_ge(var_ready, q)
                for c in range(C):
                    act.wait_ge(vstep, q * per_block + C + c + 1)
                    act.activation(sq[:, c, :], r[:, c, :], ACT.Square).then_inc(sq_done, 1)
                act.wait_ge(var_ready, q + 1)
                act.activation(sd[:], ps_v[:, 1, :], ACT.Sqrt, bias=g.eps[:, 1:2]).then_inc(sd_done, 1)

        @block.vector
        def _(dve):
            def weighted(n):
                q, e = divmod(n, E3)
                dve.wait_ge(b_ready, n + 1)
                if n >= 2:
                    dve.wait_ge(xm_read, n - 1)
                dve.tensor_tensor(xm[e % 2][:], ps_b[n % 2][:].unsqueeze(1).to_broadcast([P, C, BLK]),
                                  g.y[:, :, q * BLK:(q + 1) * BLK], ALU.mult).then_inc(xm_done, 1)

            def layer_norm(q):
                s = Steps(vstep, q * per_block)
                if q > 0:
                    dve.wait_ge(o_done, q * C)
                dve.wait_ge(y_ready, q + 1)
                for c in range(C):
                    s.did(dve.tensor_tensor(r[:, c, :], ps_y[q % 2][:, c, :], g.y[:, c, q * BLK:(q + 1) * BLK], ALU.add))
                yield
                dve.wait_ge(mean_ready, q + 1)
                for c in range(C):
                    s.did(dve.tensor_tensor(r[:, c, :], r[:, c, :], ps_v[:, 0, :], ALU.subtract))
                yield
                dve.wait_ge(sd_done, q + 1)
                s.did(dve.reciprocal(sd[:], sd[:]))
                yield
                for c in range(C):
                    s.did(dve.tensor_scalar(r[:, c, :], r[:, c, :], cols[:, c:c + 1], None, ALU.mult))
                s.settle(dve)
                for c in range(C):
                    s.did(dve.tensor_tensor(r[:, c, :], r[:, c, :], sd[:], ALU.mult))
                s.settle(dve)
                assert s.n == per_block
                yield
                if q > 0:
                    dve.wait_ge(stored, q * 16)
                for c in range(C):
                    dve.scalar_tensor_tensor(out=o[:, c, :], in0=r[:, c, :], scalar=cols[:, C + c:C + c + 1],
                                             in1=g.x[:, c, q * BLK:(q + 1) * BLK], op0=ALU.add, op1=ALU.add).then_inc(o_done, 1)
                yield

            dve.wait_ge(loads, 16)
            for q in range(NBLK):
                for e in range(E3):
                    weighted(q * E3 + e)
                    if q > 0 and e == 1:
                        parts = layer_norm(q - 1)
                    if q > 0 and e in (1, 2, 5, 6, 7):
                        next(parts)
            for _ in layer_norm(NBLK - 1):
                pass


class Held:
    pass


def program(nc, a, out):
    g = Held()
    with ExitStack() as ctx:
        g.x = ctx.enter_context(nc.sbuf_tensor("all_x", [P, C, T], F32))
        g.cond_all = ctx.enter_context(nc.sbuf_tensor("all_cond_all", [P, B * E8], F32))
        g.best = ctx.enter_context(nc.sbuf_tensor("all_best", [1, B * 8], U32))
        g.pair_idx = ctx.enter_context(nc.sbuf_tensor("all_pair_idx", [1, B * 8], U32))
        g.pair_w = ctx.enter_context(nc.sbuf_tensor("all_pair_w", [P, 2 * B], F32))
        g.ident = ctx.enter_context(nc.sbuf_tensor("all_ident", [P, P], F32))
        g.mean_w = ctx.enter_context(nc.sbuf_tensor("all_mean_w", [P, P], F32))
        g.eps = ctx.enter_context(nc.sbuf_tensor("all_eps", [P, 2], F32))
        g.iota_a = ctx.enter_context(nc.sbuf_tensor("all_iota_a", [P, P], F32))
        g.iota_b = ctx.enter_context(nc.sbuf_tensor("all_iota_b", [P, 64], F32))
        setup(nc, a, g)
        with ExitStack() as layer:
            g.key_map = layer.enter_context(nc.sbuf_tensor("layer0_key_map", [P, C, NG * NKEYS], F32))
            g.down = layer.enter_context(nc.sbuf_tensor("layer0_down", [P, C, NEXP], F32))
            g.up = layer.enter_context(nc.sbuf_tensor("layer0_up", [P, NJ, D], F32))
            with ExitStack() as routing:
                g.wq = routing.enter_context(nc.sbuf_tensor("layer0_wq", [P, NG, D], F32))
                g.keys = routing.enter_context(nc.sbuf_tensor("layer0_keys", [P, NG, NKEYS], F32))
                swiglu(nc, a, g)
                keys_fold(nc, a, g)
            peer(nc, a, g)
        g.y = ctx.enter_context(nc.sbuf_tensor("layers_y", [P, C, T], F32))
        g.b_bot = ctx.enter_context(nc.sbuf_tensor("layer3_b_bot", [P, C], F32))
        g.logit = ctx.enter_context(nc.sbuf_tensor("layer3_logit", [P, NT, E3], F32))
        g.o = ctx.enter_context(nc.sbuf_tensor("layer3_o", [P, C, T], F32))
        with ExitStack() as mixed:
            g.ws = mixed.enter_context(nc.sbuf_tensor("layer3_ws", [P, E3, C * D], F32))
            g.wb = mixed.enter_context(nc.sbuf_tensor("layer3_wb", [P, B, C * D], F32))
            g.mask = mixed.enter_context(nc.sbuf_tensor("layer3_mask", [P, C * D], F32))
            g.w_in = mixed.enter_context(nc.sbuf_tensor("layer3_w_in", [P, C, 3 * D], F32))
            g.b_in = mixed.enter_context(nc.sbuf_tensor("layer3_b_in", [P, NQKV], F32))
            with ExitStack() as layer:
                g.qw = layer.enter_context(nc.sbuf_tensor("layer2_qw", [P, 3 * NQW], F32))
                with ExitStack() as four:
                    g.q4 = four.enter_context(nc.sbuf_tensor("layer2_q4", [P, NQB, QB], F32))
                    g.skill = four.enter_context(nc.sbuf_tensor("layer2_skill", [P, SKILL], F32))
                    lora(nc, a, g)
                    skills(nc, a, g)
                    weights4(nc, a, g)
                quant_ffn(nc, a, g)
            attend(nc, a, g)
        g.w12 = ctx.enter_context(nc.sbuf_tensor("layer3_w12", [P, E3, C, D], F32))
        g.c12 = ctx.enter_context(nc.sbuf_tensor("layer3_c12", [E3, D], F32))
        g.weight8 = ctx.enter_context(nc.sbuf_tensor("layer3_weight8", [E3, T], F32))
        with ExitStack() as folds:
            g.b1 = folds.enter_context(nc.sbuf_tensor("layer3_b1", [P, FF // P * E3], F32))
            g.b2 = folds.enter_context(nc.sbuf_tensor("layer3_b2", [E3, D], F32))
            g.w1 = [folds.enter_context(nc.sbuf_tensor(f"layer3_w1_{i}", [P, FF // P, D], F32)) for i in range(WRING)]
            g.w2 = [folds.enter_context(nc.sbuf_tensor(f"layer3_w2_{i}", [P, FF // P, D], F32)) for i in range(WRING)]
            norm(nc, a, g)
            experts(nc, a, g)
        gates(nc, a, g)
        moe(nc, a, g, out)


def columns(v):
    return v.reshape(v.shape[:-1] + (-1, P)).swapaxes(-1, -2)


def rows(w):
    return w.reshape(w.shape[:-2] + (-1, P, w.shape[-1])).swapaxes(-3, -2)


def lay_out(np, z):
    def turn(name):
        return z[name].swapaxes(-1, -2)

    def flat(w, keep):
        return w.reshape(w.shape[:keep] + (-1,))

    def by_row_of_experts(w):
        return w.reshape(NKEYS, NKEYS // 2, 2, D).transpose(1, 2, 0, 3).reshape(NEXP, D)

    return {
        "x": rows(z["x"].reshape(T, D).T),
        "cond": z["cond_8"],
        "cond0": np.concatenate(
            [flat(rows(turn("L0_cond_W_" + k)), 2) for k in ("up", "gate", "down")]
            + [columns(z["L0_cond_b_" + k]) for k in ("up", "gate", "down")], axis=-1),
        "norm_w": columns(z["L0_ffn_norm_w"]),
        "wq": rows(z["L0_ffn_w_q"]),
        "keys": z["L0_ffn_keys"].transpose(3, 0, 2, 1).reshape(P, NG, NKEYS),
        "down": rows(by_row_of_experts(z["L0_ffn_expert_down"]).T),
        "up": rows(by_row_of_experts(z["L0_ffn_expert_up"])),
        "l1_a": z["L1_cond_As"].reshape(P, D),
        "l1_b": z["L1_cond_Bs"].transpose(0, 2, 1).reshape(P, D),
        "l1_w": np.repeat(z["cond_8"], R1, axis=1).T,
        "l1_wbase": rows(turn("L1_cond_W_base")),
        "l1_cols": np.concatenate([columns(z["L1_cond_b_base"]), columns(z["L1_ffn_base_b"])], axis=-1),
        "l1_basew": rows(turn("L1_ffn_base_W")),
        "l1_ra": rows(np.concatenate([z["L1_ffn_routed_A"].reshape(E1 * R1, D), z["L1_ffn_shared_A"]]).T),
        "l1_rb": np.concatenate([z["L1_ffn_routed_B"].transpose(0, 2, 1).reshape(E1 * R1, D), turn("L1_ffn_shared_B")]),
        "l1_rw": rows(turn("L1_ffn_router_W")),
        "l1_rbias": z["L1_ffn_router_b"],
        "skills": np.concatenate([flat(rows(z["L2_cond_skill_" + k]), 2) for k in ("gate", "up", "down")], axis=-1),
        "skill_shared": np.concatenate([flat(rows(z["L2_cond_shared_" + k]), 1) for k in ("gate", "up", "down")], axis=-1),
        "q_w": np.concatenate([flat(rows(z["L2_ffn_" + k]), 1) for k in ("w_up", "w_gate", "w_down")], axis=-1),
        "l3_w": rows(turn("L3_cond_weight")).swapaxes(0, 1).reshape(P, E3, C * D),
        "l3_mask": flat(rows(turn("L3_cond_mask")), 1),
        "l3_win": rows(turn("L3_ffn_in_proj_w")),
        "l3_bin": columns(z["L3_ffn_in_proj_b"]),
        "l3_bbot": columns(z["L3_cond_bias"]),
        "l3_wout": rows(turn("L3_ffn_out_proj_w")),
        "l3_wg": rows(z["L3_ffn_wg"]),
        "l3_cols": np.concatenate([columns(z["L3_ffn_" + k]) for k in ("out_proj_b", "ln1_g", "ln1_b")], axis=-1),
        "l3_cols2": np.concatenate([columns(z["L3_ffn_" + k]) for k in ("ln2_g", "ln2_b")], axis=-1),
        "l3_w1": rows(turn("L3_ffn_w1")),
        "l3_w2": rows(z["L3_ffn_w2"]),
        "l3_b1": flat(rows(z["L3_ffn_b1"].T), 1),
        "l3_b2": z["L3_ffn_b2"],
    }


def kernel(**inputs):
    import numpy as np
    import concourse.bacc as bacc
    from concourse.bass_utils import run_bass_kernel_spmd

    laid = lay_out(np, {name: np.asarray(v) for name, v in inputs.items()})
    arrays = {f"in_{name}": np.ascontiguousarray(v) for name, v in laid.items()}
    nc = bacc.Bacc("TRN2", target_bir_lowering=False, num_devices=1)
    a = {name: nc.dram_tensor(f"in_{name}", v.shape, F32, kind="ExternalInput").ap() for name, v in laid.items()}
    out = nc.dram_tensor("out", (P, C, T), F32, kind="ExternalOutput").ap()
    program(nc, a, out)
    result = run_bass_kernel_spmd(nc, [arrays], core_ids=[0])
    return result.results[0]["out"].transpose(2, 1, 0).reshape(B, S, D)
```
